# Optimizing a Trainium2 kernel written in Bass

```python
import numpy as np
import jax
import jax.numpy as jnp

def _softmax(x, axis=-1):
    return jax.nn.softmax(x, axis=axis)

def _gelu(x):
    return jax.nn.gelu(x, approximate=True)

def _silu(x):
    return jax.nn.silu(x)

def _sigmoid(x):
    return jax.nn.sigmoid(x)

def _layernorm(x, axis=-1, eps=1e-05):
    m = jnp.mean(x, axis=axis, keepdims=True)
    v = jnp.var(x, axis=axis, keepdims=True)
    return (x - m) / jnp.sqrt(v + eps)

def _scatter_add(tgt, idx, src, axis=0):
    return tgt.at[idx].add(src)

def _segment_sum(src, seg, n):
    return jax.ops.segment_sum(src, seg, n)
kernel_name = 'mk_gnn_preln_d2_gnn_r64_9ebdd1'

def setup_inputs(seed: int=0):
    np.random.seed(seed)
    _w = jnp.asarray

    def _rec_inputs():
        import jax
        import jax.numpy as jnp
        _gk = jax.random.key(seed)
        x = -0.0005121 + 1.001 * jax.random.normal(jax.random.fold_in(_gk, 1), (100000, 64), jnp.float32)
        src = jax.random.randint(jax.random.fold_in(_gk, 2), (25000,), 0, 100000, jnp.int32)
        dst = jax.random.randint(jax.random.fold_in(_gk, 3), (25000,), 0, 100000, jnp.int32)
        _o = jnp.argsort(dst, stable=True)
        src = src[_o]
        dst = dst[_o]
        edge_attr_64 = 0.000189758 + 1.00013 * jax.random.normal(jax.random.fold_in(_gk, 11), (25000, 64), jnp.float32)
        return (x, src, dst, edge_attr_64)
    x, src, dst, edge_attr_64 = _rec_inputs()

    def _L0_gnn_setup():
        import jax, jax.numpy as jnp
        import numpy as np
        N_NODES = 50000
        N_EDGES = 12500
        D = 64
        H = 2 * D
        EPS_MSG = 1e-07
        EPS_SOFTMAX = 1e-16
        BN_EPS = 1e-05
        key = jax.random.key(seed)
        ks = jax.random.split(key, 8)
        x = jax.random.normal(ks[0], (N_NODES, D), dtype=jnp.float32)
        edge_index = jax.random.randint(ks[1], (2, N_EDGES), 0, N_NODES, dtype=jnp.int64)
        edge_attr = jax.random.normal(ks[2], (N_EDGES, D), dtype=jnp.float32)
        s = 1.0 / np.sqrt(D)
        W_edge = jax.random.uniform(ks[3], (D, D), jnp.float32, -s, s)
        W1 = jax.random.uniform(ks[4], (D, H), jnp.float32, -s, s)
        gamma = jnp.ones((H,), jnp.float32)
        beta = jnp.zeros((H,), jnp.float32)
        sh = 1.0 / np.sqrt(H)
        W2 = jax.random.uniform(ks[5], (H, D), jnp.float32, -sh, sh)
        return {'x': x, 'edge_index': edge_index, 'edge_attr': edge_attr, 'W_edge': W_edge, 'W1': W1, 'gamma': gamma, 'beta': beta, 'W2': W2}
    _L0_gnn_all = _L0_gnn_setup()
    _L0_gnn_in = {k: v for k, v in _L0_gnn_all.items() if k in ('W_edge', 'W1', 'gamma', 'beta', 'W2')}
    del _L0_gnn_all

    def _L1_gnn_setup():
        import jax, jax.numpy as jnp
        import numpy as np
        N_NODES = 100000
        key = jax.random.key(seed)
        k1, k2, k3 = jax.random.split(key, 3)
        x = jax.random.normal(k1, (N_NODES, 64), dtype=jnp.float32)
        edge_index = jax.random.randint(k2, (2, 1250000), 0, N_NODES, dtype=jnp.int64)
        W = jax.random.normal(k3, (128, 64), dtype=jnp.float32) * (1.0 / np.sqrt(128.0))
        b = jnp.zeros((64,), dtype=jnp.float32)
        return {'x': x, 'edge_index': edge_index, 'W': W, 'b': b}
    _L1_gnn_all = _L1_gnn_setup()
    _L1_gnn_in = {k: v for k, v in _L1_gnn_all.items() if k in ('W', 'b')}
    del _L1_gnn_all
    return {'x': x, 'src': src, 'dst': dst, 'edge_attr_64': edge_attr_64, 'L0_gnn_W_edge': _L0_gnn_in['W_edge'], 'L0_gnn_W1': _L0_gnn_in['W1'], 'L0_gnn_gamma': _L0_gnn_in['gamma'], 'L0_gnn_beta': _L0_gnn_in['beta'], 'L0_gnn_W2': _L0_gnn_in['W2'], 'L1_gnn_W': _L1_gnn_in['W'], 'L1_gnn_b': _L1_gnn_in['b']}

def reference(x, src, dst, edge_attr_64, L0_gnn_W_edge, L0_gnn_W1, L0_gnn_gamma, L0_gnn_beta, L0_gnn_W2, L1_gnn_W, L1_gnn_b):
    import jax
    import jax.numpy as jnp

    def _L0_gnn_ref(x, edge_index, edge_attr, W_edge, W1, gamma, beta, W2):
        import jax, jax.numpy as jnp
        import numpy as np
        N_NODES = 50000
        N_EDGES = 12500
        D = 64
        H = 2 * D
        EPS_MSG = 1e-07
        EPS_SOFTMAX = 1e-16
        BN_EPS = 1e-05
        N = x.shape[0]
        src, dst = (edge_index[0], edge_index[1])
        x_j = x[src]
        msg = jax.nn.relu(x_j + edge_attr @ W_edge) + EPS_MSG
        max_per = jax.ops.segment_max(msg, dst, num_segments=N)
        exp_s = jnp.exp(msg - max_per[dst])
        sum_per = jax.ops.segment_sum(exp_s, dst, num_segments=N)
        alpha = exp_s / (sum_per[dst] + EPS_SOFTMAX)
        agg = jax.ops.segment_sum(msg * alpha, dst, num_segments=N)
        out = agg + x
        h = out @ W1
        mu = jnp.mean(h, axis=0)
        var = jnp.mean((h - mu) ** 2, axis=0)
        h = (h - mu) * jax.lax.rsqrt(var + BN_EPS) * gamma + beta
        return jax.nn.relu(h) @ W2

    def _L1_gnn_ref(x, edge_index, W, b):
        import jax, jax.numpy as jnp
        import numpy as np
        N_NODES = 100000
        n = x.shape[0]
        row, col = (edge_index[0], edge_index[1])
        neigh = jax.ops.segment_sum(x[row], col, num_segments=n)
        count = jax.ops.segment_sum(jnp.ones_like(col, dtype=x.dtype), col, num_segments=n)
        count = jnp.where(count == 0, jnp.asarray(1.0, x.dtype), count)
        neigh = neigh / count[:, None]
        x_aggr = jnp.concatenate([x, neigh], axis=-1)
        out = x_aggr @ W + b
        return jax.nn.relu(out)
    edge_index = jnp.stack([src, dst])
    h = jnp.maximum(_layernorm(x, axis=-1), 0.0)
    x = x + _L0_gnn_ref(h, edge_index, edge_attr_64, L0_gnn_W_edge, L0_gnn_W1, L0_gnn_gamma, L0_gnn_beta, L0_gnn_W2)
    h = jnp.maximum(_layernorm(x, axis=-1), 0.0)
    x = x + _L1_gnn_ref(h, edge_index, L1_gnn_W, L1_gnn_b)
    return x

_drawn_inputs = setup_inputs


def setup_inputs(seed=0):
    import zlib

    import numpy as np

    out = dict(_drawn_inputs(seed))
    spreads = {'L0_gnn_gamma': (1.0, 0.2), 'L0_gnn_beta': (0.0, 0.1), 'L1_gnn_b': (0.0, 0.1)}
    factors = {}
    for name, (base, spread) in spreads.items():
        noise = np.random.default_rng([zlib.crc32(name.encode()), seed]).standard_normal(out[name].shape)
        drawn = base * np.exp(spread * noise) if base else spread * noise
        out[name] = jnp.asarray(drawn.astype(out[name].dtype))
    for name, factor in factors.items():
        out[name] = (out[name] * factor).astype(out[name].dtype)
    return out
```

```python
from contextlib import ExitStack

import numpy as np

import concourse.bass as bass
from concourse import mybir

F32 = mybir.dt.float32
BF16 = mybir.dt.bfloat16
I32 = mybir.dt.int32
U8 = mybir.dt.uint8
ALU = mybir.AluOpType
ACT = mybir.ActivationFunctionType
AX = mybir.AxisListType

P = 128
LN_EPS = 1e-5
BN_EPS = 1e-5
MSG_EPS = 1e-7
SOFTMAX_EPS = 1e-16


def ds(start, size):
    return bass.ds(start, size)


class Part:

    def __init__(self, n, g0, k0, tiles):
        self.n, self.g0, self.k0, self.tiles = n, g0, k0, tiles

    def after(self, n, tiles):
        return Part(n, self.g0 + self.n, (self.k0[0] + (self.n + 1) // 2, self.k0[1] + self.n // 2), tiles)

    def chunk(self, i, u):
        return Chunk(self, i, u)


class Chunk:

    def __init__(self, part, i, u):
        self.part, self.tiles, self.pairs = part, part.tiles, part.tiles // 2
        self.c = i * 2 + u
        self.g = self.c + part.g0
        self.s = u % 2
        self.w = i + u // 2
        self.k = self.w + part.k0[self.s]


def walk(e, part, first, step, last):
    first(part.chunk(0, 0))
    rounds = (part.n - 1) // 2
    with e.Fori(0, rounds) as i:
        step(part.chunk(i, 0), part.chunk(i, 1))
        step(part.chunk(i, 1), part.chunk(i, 2))
    if part.n % 2 == 0:
        step(part.chunk(rounds, 0), part.chunk(rounds, 1))
        last(part.chunk(rounds, 1))
    else:
        last(part.chunk(rounds, 0))


def each(e, part, step):
    with e.Fori(0, part.n // 2) as i:
        step(part.chunk(i, 0))
        step(part.chunk(i, 1))


def build(nc, x, src, dst, edge_attr, w_edge, w1, gamma, beta, w2, w_out, b_out, out):
    N, D = x.shape
    E = src.shape[0]
    H = w1.shape[1]
    assert D == 64 and H == P

    BT = 16
    BROWS = BT * P
    BC = -(-N // BROWS)
    LAST0 = N - BROWS
    OVER = BC * BROWS - N
    assert OVER % BT == 0 and BC % 2 == 1
    OVERP = OVER // BT

    EJ = 7
    HT = -(-E // (2 * P * EJ)) * EJ
    HALF = HT * P
    ET = 2 * EJ
    EC = HT // EJ
    assert EC % 2 == 0
    W = EJ * P
    PADS = 2 * HALF - E
    assert 0 < PADS < P - 1
    TAIL = P - PADS

    NODES = Part(BC, 0, (0, 0), BT)
    SOURCES = NODES.after(EC, ET)
    DESTS = SOURCES.after(EC, ET)
    EDGES = Part(EC, 0, (0, 0), ET)

    agg_tab = nc.dram_tensor("agg_tab", [N, D], F32, kind="Internal").ap()
    h_node = nc.dram_tensor("h_node", [N, D], F32, kind="Internal").ap()
    x_src, x_dst, h_src, h_dst, agg_src, agg_dst = (
        nc.dram_tensor(n, [EC * P, ET * D], F32, kind="Internal").ap()
        for n in ("x_src", "x_dst", "h_src", "h_dst", "agg_src", "agg_dst"))

    with ExitStack() as ctx:
        def sb(name, shape, dt=F32):
            return ctx.enter_context(nc.sbuf_tensor(name, shape, dt))

        def sem(name):
            return ctx.enter_context(nc.semaphore(name))

        def sem2(name):
            return [sem(name + "_0"), sem(name + "_1")]

        ident = sb("ident", [P, P])
        swap = sb("swap", [P, P])
        down = sb("down", [P, P])
        blocks = sb("blocks", [P, P])
        ones_col = sb("ones_col", [P, 1])
        own_rows = sb("own_rows", [P, 1])
        ones_row = sb("ones_row", [P, W], BF16)
        ones3 = sb("ones3", [96, P], BF16)
        bias3 = sb("bias3", [96, 8 * D], BF16)
        we_blk = sb("we_blk", [P, P])
        wa_blk = sb("wa_blk", [P, P])
        wb_blk = sb("wb_blk", [P, P])
        w1_dup = sb("w1_dup", [P, H])
        w2_sb = sb("w2_sb", [H, D])
        vecs = sb("vecs", [P, 16])
        (gamma_c, beta_c, mean_c, ex2_c, m2_c, var_c, std_c, rs_c, scale_c, mscale_c, shift_c, sum_c,
         norm_eps, soft_eps) = (vecs[:, n:n + 1] for n in range(14))
        gram_sb = sb("gram_sb", [P, P])
        gram_w = sb("gram_w", [P, H])
        links = sb("links", [P, 16])
        run_max, tot_max, other_dst = (links[:, n:n + 1] for n in range(3))
        soft_ends, soft_carry, mean_ends, mean_carry = (links[:, n:n + 2] for n in (4, 6, 8, 10))

        src_idx = sb("src_idx", [P, HT * 2], I32)
        dst_idx = sb("dst_idx", [P, HT * 2], I32)
        put_idx = sb("put_idx", [P, HT * 2], I32)
        seg_end = sb("seg_end", [P, HT * 2])
        other_raw = sb("other_raw", [P, 1], I32)
        stage_idx = [sb(f"stage_idx{s}", [P, ET], I32) for s in range(2)]

        reg_m = sb("reg_m", [P, HALF])
        reg_a = sb("reg_a", [P, HALF])
        same = sb("same", [P, HALF + 4], U8)
        linked = sb("linked", [P, HALF], U8)

        xb = [sb(f"xb{s}", [P, BT * D]) for s in range(2)]
        xc = [sb(f"xc{s}", [P, BT * D]) for s in range(2)]
        sq = sb("sq", [P, BT * D])
        hb = [sb(f"hb{s}", [P, BT // 2, P + 1]) for s in range(2)]
        hin = [sb(f"hin{s}", [P, BT * D]) for s in range(2)]
        x1b = [sb(f"x1b{s}", [P, BT * D]) for s in range(2)]
        ht = [sb(f"ht{u}", [P, 4 * P]) for u in range(2)]
        yb = [sb(f"yb{u}", [P, 2 * 4 * P]) for u in range(2)]
        h1t = [sb(f"h1t{u}", [P, 4 * P]) for u in range(2)]
        gb = [sb(f"gb{s}", [P, ET * D]) for s in range(2)]
        st = [sb(f"st{s}", [P, 4, BT]) for s in range(2)]

        bias_part = sb("bias_part", [96, 8 * D], BF16)

        ea = hin
        ea_t = yb
        dcol = [x1b[s][:, 0:W + 1].bitcast(I32) for s in range(2)]
        vb = [x1b[s][:, 0:EJ * (P + 1)].rearrange("p (j q) -> p j q", q=P + 1) for s in range(2)]
        agg_t = yb
        mean_t = gb
        raw = [reg_m[:, n * 2 * P:(n + 1) * 2 * P].bitcast(I32) for n in range(3)]
        flt = [reg_m[:, (n + 3) * 2 * P:(n + 4) * 2 * P] for n in range(6)]
        bias_f = [reg_m[0:96, (n + 9) * 2 * P:(n + 9) * 2 * P + 8 * D] for n in (0, 2, 4)]
        zeros = reg_a[:, 0:BT * D]

        psum = ctx.enter_context(nc.psum_tensor("psum", [P, 8, 512], F32))
        ps_t = [psum[:, 0, :], psum[:, 1, :]]
        ps_z = psum[:, 2:4, :]
        ps_z_flat = psum[:, 2:4, :].rearrange("p a b -> p (a b)")
        ps_w = psum[:, 4, :]
        ps_o = psum[:, 5, :]
        ps_t1 = [psum[:, 6, :], psum[:, 7, :]]
        ps_t1_flat = psum[:, 6:8, :].rearrange("p a b -> p (a b)")
        ps_g = psum[:, 7, :]

        const_made, raw_filled, raw_in, idx_float, idx_step, idx_turned, idx_made = \
            (sem(n) for n in ("const_made", "raw_filled", "raw_in", "idx_float", "idx_step", "idx_turned",
                              "idx_made"))
        weights_in, bias_made, zeroed, staged = \
            (sem(n) for n in ("weights_in", "bias_made", "zeroed", "staged"))
        gathered, kept = sem2("gathered"), sem2("kept")
        pool_steps, sync_steps = sem("pool_steps"), sem("sync_steps")
        x_in, ln_centred, h_used, h_out = (sem2(n) for n in ("x_in", "ln_centred", "h_used", "h_out"))
        ln_sum, ln_squared, ln_ssq, ln_std, ln_rstd, ln_h = \
            (sem(n) for n in ("ln_sum", "ln_squared", "ln_ssq", "ln_std", "ln_rstd", "ln_h"))
        ea_in, dcol_in, d_in, v_used = (sem2(n) for n in ("ea_in", "dcol_in", "d_in", "v_used"))
        ea_turned, ea_copied, same_made, linked_made, msg_made, run_made, edges_set, v_made = \
            (sem(n) for n in ("ea_turned", "ea_copied", "same_made", "linked_made", "msg_made", "run_made",
                              "edges_set", "v_made"))
        max_made, link_col, link_ps, link_made, max_linked, arg_made, exp_made, weighted, e_summed, a_summed = \
            (sem(n) for n in ("max_made", "link_col", "link_ps", "link_made", "max_linked", "arg_made",
                              "exp_made", "weighted", "e_summed", "a_summed"))
        s_linked, a_linked, inv_guess, newton_a, newton_b, agg_made, agg_turned, agg_rows = \
            (sem(n) for n in ("s_linked", "a_linked", "inv_guess", "newton_a", "newton_b", "agg_made",
                              "agg_turned", "agg_rows"))
        agg_stored, agg_put = sem2("agg_stored"), sem2("agg_put")
        stat, stat_mid, stat_ps, stat_std, bn_ready = \
            (sem(n) for n in ("stat", "stat_mid", "stat_ps", "stat_std", "bn_ready"))
        two_in, agg_in = sem2("two_in"), sem2("agg_in")
        h_summed, t_done, t_copied, z_done, y_done, w_done, x1_done = \
            (sem(n) for n in ("h_summed", "t_done", "t_copied", "z_done", "y_done", "w_done", "x1_done"))
        l_sum, l_centred, l_squared, l_ssq, l_std, l_rstd, l_h = \
            (sem(n) for n in ("l_sum", "l_centred", "l_squared", "l_ssq", "l_std", "l_rstd", "l_h"))
        t1_done, t1_copied, o_done, fin_done, hs_turned = \
            (sem(n) for n in ("t1_done", "t1_copied", "o_done", "fin_done", "hs_turned"))
        n_summed, c_summed, n_linked, c_linked, mean_made = \
            (sem(n) for n in ("n_summed", "c_summed", "n_linked", "c_linked", "mean_made"))
        out_stored, patched = sem2("out_stored"), sem2("patched")

        block = ctx.enter_context(nc.Block())

        CONSTS = 24
        WEIGHTS = 12
        STAGED = (0, EC, 3 * EC)

        def inv_place(ch, before):
            return (gb if before else xc)[ch.s][:, 0:W]

        def cols(ch):
            return ds(ch.c * W, W)

        def node_view(t, rows):
            return t[rows, :].rearrange("(p t) d -> p (t d)", p=P)

        def node_rows(ch):
            return ds(ch.c * BROWS, BROWS)

        def edge_rows(t, ch):
            return t[ds(ch.c * P, P), :]

        def tile_rows(buf, ch):
            return buf[:, 0:ch.tiles * D].rearrange("p (t d) -> p t d", d=D)

        def pair_rows(buf, ch):
            return buf[:, 0:ch.tiles * D].rearrange("p (j q) -> p j q", q=2 * D)

        def spread(ch, row):
            return st[ch.s][:, row, 0:ch.tiles].unsqueeze(2).to_broadcast([P, ch.tiles, D])

        def quads(ch):
            return ((0, 4), (4, ch.pairs - 4))

        @block.gpsimd
        def _(e):
            made = 0

            def note(ins):
                nonlocal made
                ins.then_inc(const_made, 1)
                made += 1

            def diagonal(ap, base):
                e.wait_ge(const_made, made)
                note(e.affine_select(out=ap, in_=ap, compare_op=ALU.not_equal, fill=1.0, base=base,
                                     pattern=[[-1, P]], channel_multiplier=1))

            for m in (ident, swap, down, blocks, bias3, we_blk, wa_blk, wb_blk):
                note(e.memset(m[:, :], 0.0))
            for m in (ones_col, own_rows, ones_row, ones3):
                note(e.memset(m[:, :], 1.0))
            for m in hb:
                note(e.memset(m[:, :, P:P + 1], 1.0))
            note(e.memset(norm_eps, LN_EPS))
            note(e.memset(soft_eps, SOFTMAX_EPS))
            note(e.memset(zeros, 0.0))
            diagonal(ident[:, :], 0)
            diagonal(swap[:, :], D)
            diagonal(swap[:, :], -D)
            diagonal(down[:, :], D)
            for half in (slice(0, D), slice(D, P)):
                e.wait_ge(const_made, made)
                note(e.memset(blocks[half, half], 1.0))
            e.wait_ge(const_made, made)
            note(e.affine_select(out=own_rows[:, :], in_=own_rows[:, :], compare_op=ALU.is_ge, fill=0.0,
                                 base=-OVERP, pattern=[[0, 1]], channel_multiplier=1))
            assert made == CONSTS

            def stage(idx, ch, before):
                e.tensor_copy(stage_idx[ch.s][:, :], idx[:, ds(ch.c * ET, ET)]).then_inc(staged, 1)
                e.wait_ge(staged, ch.c + (before + 1))
                e.sem_inc(pool_steps, 1)

            def gather(table, idx, rows, turn):
                part = Part(EC, 0, (turn * EC // 2, turn * EC // 2), ET)

                def get(ch):
                    e.wait_ge(kept[ch.s], ch.k * 16)
                    stage(idx, ch, STAGED[turn])
                    for t in range(ET):
                        e.indirect_dma_start(
                            gb[ch.s][:, t * D:(t + 1) * D], None, table,
                            bass.IndirectOffsetOnAxis(ap=stage_idx[ch.s][:, t:t + 1], axis=0),
                        ).then_inc(gathered[ch.s], 16)

                def keep(ch):
                    e.wait_ge(gathered[ch.s], (ch.k + 1) * (16 * ET))
                    e.dma_start(edge_rows(rows, ch), gb[ch.s][:, :]).then_inc(kept[ch.s], 16)

                def get_and_keep(before, ch):
                    get(ch)
                    keep(before)

                walk(e, part, get, get_and_keep, keep)

            def put(ch, table, buf, before, done):
                stage(put_idx, ch, before)
                for t in range(ET):
                    e.indirect_dma_start(
                        table, bass.IndirectOffsetOnAxis(ap=stage_idx[ch.s][:, t:t + 1], axis=0),
                        buf[:, t * D:(t + 1) * D], None, bounds_check=N - 1, oob_is_err=False,
                    ).then_inc(done[ch.s], 16)

            e.wait_ge(idx_made, 4)
            gather(x, src_idx, x_src, 0)
            gather(x, dst_idx, x_dst, 1)

            e.wait_ge(zeroed, 16 * BC)

            def put_agg(ch):
                e.wait_ge(agg_rows, ch.c + 1)
                e.wait_ge(agg_put[ch.s], ch.w * (16 * ET))
                put(ch, agg_tab, gb[ch.s], 2 * EC, agg_put)

            each(e, EDGES, put_agg)
            for s in range(2):
                e.wait_ge(agg_put[s], 16 * ET * (EC // 2))
                e.wait_ge(agg_stored[s], 16 * (EC // 2))
            gather(agg_tab, src_idx, agg_src, 2)

            e.wait_ge(out_stored[0], 16 * ((BC + 1) // 2))
            e.wait_ge(out_stored[1], 16 * (BC // 2))

            def put_out(ch):
                e.wait_ge(fin_done, ch.c * 2 + 2 * (BC + 1))
                e.wait_ge(patched[ch.s], ch.w * (16 * ET))
                put(ch, out, x1b[ch.s], 4 * EC, patched)

            each(e, EDGES, put_out)
            for s in range(2):
                e.wait_ge(patched[s], 16 * ET * (EC // 2))

        @block.sync
        def _(e):
            e.wait_ge(raw_filled, 3)
            for buf, ap, ahead in ((raw[0], src, 0), (raw[1], dst, 0), (raw[2], dst, 1)):
                e.dma_start(buf[0:HT, 0:P], ap[ahead:ahead + HALF].rearrange("(t p) -> t p", p=P))\
                    .then_inc(raw_in, 16)
                full = HALF + (HT - 1) * P
                e.dma_start(buf[0:HT - 1, P:2 * P],
                            ap[HALF + ahead:full + ahead].rearrange("(t p) -> t p", p=P)).then_inc(raw_in, 16)
                e.dma_start(buf[HT - 1:HT, P:P + TAIL - ahead],
                            ap[full + ahead:E].rearrange("(t p) -> t p", t=1)).then_inc(raw_in, 16)

            def border(at):
                return dst[at:at + 1].rearrange("(o p) -> o p", o=1).to_broadcast([D, 1])

            e.dma_start(other_raw[0:D, :], border(HALF)).then_inc(raw_in, 16)
            e.dma_start(other_raw[D:P, :], border(HALF - 1)).then_inc(raw_in, 16)
            e.wait_ge(const_made, CONSTS)
            for m, w in ((we_blk, w_edge), (wa_blk, w_out[0:D, :]), (wb_blk, w_out[D:2 * D, :])):
                e.dma_start(m[0:D, 0:D], w).then_inc(weights_in, 16)
                e.dma_start(m[D:P, D:P], w).then_inc(weights_in, 16)
            e.dma_start(w1_dup[0:D, :], w1).then_inc(weights_in, 16)
            e.dma_start(w1_dup[D:P, :], w1).then_inc(weights_in, 16)
            e.dma_start(w2_sb[:, :], w2).then_inc(weights_in, 16)
            e.dma_start(gamma_c, gamma.rearrange("(p o) -> p o", o=1)).then_inc(weights_in, 16)
            e.dma_start(beta_c, beta.rearrange("(p o) -> p o", o=1)).then_inc(weights_in, 16)
            e.dma_start(bias_f[0].rearrange("p (t d) -> p t d", d=D),
                        b_out.rearrange("(a t d) -> a t d", a=1, t=1).to_broadcast([96, 8, D]))\
                .then_inc(weights_in, 16)

            def load_node(ch, rows):
                e.wait_ge(ln_centred[ch.s], ch.k)
                e.dma_start(xb[ch.s][:, :], node_view(x, rows)).then_inc(x_in[ch.s], 16)

            def store_node(ch):
                e.wait_ge(ln_h, ch.g + 1)
                e.dma_start(node_view(h_node, node_rows(ch)).rearrange("p (j q) -> p j q", q=P),
                            hb[ch.s][:, :, 0:P]).then_inc(h_out[ch.s], 16)
                e.dma_start(node_view(agg_tab, node_rows(ch)), zeros).then_inc(zeroed, 16)

            rest = slice(LAST0 + OVER, N)

            def rest_view(t):
                return t[rest, :].rearrange("(p t) d -> p (t d)", t=BT)

            def nodes(load, store, store_last):
                ahead = (BC - 3) // 2
                load(NODES.chunk(0, 0), node_rows(NODES.chunk(0, 0)))
                load(NODES.chunk(0, 1), node_rows(NODES.chunk(0, 1)))
                with e.Fori(0, ahead) as i:
                    for u in range(2):
                        load(NODES.chunk(i, u + 2), node_rows(NODES.chunk(i, u + 2)))
                        store(NODES.chunk(i, u))
                load(NODES.chunk(ahead, 2), slice(LAST0, N))
                store(NODES.chunk(ahead, 0))
                store(NODES.chunk(ahead, 1))
                store_last(NODES.chunk(ahead, 2))

            def store_last_node(ch):
                e.wait_ge(ln_h, ch.g + 1)
                e.dma_start(rest_view(h_node).rearrange("p (j q) -> p j q", q=P),
                            hb[ch.s][OVERP:P, :, 0:P]).then_inc(h_out[ch.s], 16)
                e.dma_start(rest_view(agg_tab), zeros[OVERP:P, :]).then_inc(zeroed, 16)

            e.wait_ge(const_made, CONSTS)
            nodes(load_node, store_node, store_last_node)

            def edge_cols(ap, at, n):
                return ap[ds(at, n)].rearrange("(o n) -> o n", o=1).to_broadcast([D, n])

            def load_source(ch, where):
                e.wait_ge(kept[ch.s], (ch.w + 1) * 16)
                e.sem_inc(sync_steps, 1)
                e.wait_ge(ln_centred[ch.s], ch.k)
                e.dma_start(xb[ch.s][:, 0:ET * D], edge_rows(x_src, ch)).then_inc(x_in[ch.s], 16)
                if where != "first":
                    e.wait_ge(ea_turned, ch.c - 1)
                    e.wait_ge(linked_made, ch.c - 1)
                v = ea[ch.s][:, 0:ET * D].rearrange("p (j a d) -> p j a d", a=2, d=D)

                def attr(at, n):
                    return edge_attr[ds(at, n), :].rearrange("(j p) d -> p j d", p=P)

                e.dma_start(v[:, :, 0, :], attr(ch.c * W, W)).then_inc(ea_in[ch.s], 16)
                if where == "last":
                    full, at = (EJ - 1) * P, HALF + (EC - 1) * W
                    e.dma_start(v[:, 0:EJ - 1, 1, :], attr(at, full)).then_inc(ea_in[ch.s], 16)
                    e.dma_start(v[0:TAIL, EJ - 1, 1, :], edge_attr[at + full:E, :]).then_inc(ea_in[ch.s], 16)
                else:
                    e.dma_start(v[:, :, 1, :], attr(ch.c * W + HALF, W)).then_inc(ea_in[ch.s], 16)
                lo = 1 if where == "first" else 0
                hi = W + 1 - PADS if where == "last" else W + 1
                if where == "first":
                    at = 0
                else:
                    at = ch.c * W - 1
                e.dma_start(dcol[ch.s][0:D, lo:W + 1], edge_cols(dst, at, W + 1 - lo)).then_inc(dcol_in[ch.s], 16)
                e.dma_start(dcol[ch.s][D:P, lo:hi], edge_cols(dst, at + HALF, hi - lo)).then_inc(dcol_in[ch.s], 16)

            def store_source(ch):
                e.wait_ge(ln_h, ch.g + 1)
                e.dma_start(edge_rows(h_src, ch).rearrange("p (j q) -> p j q", q=P),
                            hb[ch.s][:, 0:EJ, 0:P]).then_inc(h_out[ch.s], 16)

            rounds = (EC - 4) // 2
            load_source(SOURCES.chunk(0, 0), "first")
            load_source(SOURCES.chunk(0, 1), "second")
            with e.Fori(0, rounds) as i:
                for u in range(2):
                    load_source(SOURCES.chunk(i, u + 2), "inner")
                    store_source(SOURCES.chunk(i, u))
            load_source(SOURCES.chunk(rounds, 2), "inner")
            store_source(SOURCES.chunk(rounds, 0))
            load_source(SOURCES.chunk(rounds, 3), "last")
            for u in range(1, 4):
                store_source(SOURCES.chunk(rounds, u))

            def store_agg(ch):
                e.wait_ge(agg_rows, ch.c + 1)
                e.dma_start(edge_rows(agg_dst, ch), gb[ch.s][:, :]).then_inc(agg_stored[ch.s], 16)

            each(e, EDGES, store_agg)

            def load_dest(ch):
                e.wait_ge(kept[ch.s], (ch.w + (EC // 2 + 1)) * 16)
                e.sem_inc(sync_steps, 1)
                e.wait_ge(ln_centred[ch.s], ch.k)
                e.dma_start(xb[ch.s][:, 0:ET * D], edge_rows(x_dst, ch)).then_inc(x_in[ch.s], 16)
                e.wait_ge(agg_stored[ch.s], (ch.w + 1) * 16)
                e.sem_inc(sync_steps, 1)
                e.wait_ge(v_used[ch.s], ch.w)
                e.dma_start(hin[ch.s][:, 0:ET * D], edge_rows(agg_dst, ch)).then_inc(d_in[ch.s], 16)

            def store_dest(ch):
                e.wait_ge(ln_h, ch.g + 1)
                e.dma_start(edge_rows(h_dst, ch).rearrange("p (j q) -> p j q", q=P),
                            hb[ch.s][:, 0:EJ, 0:P]).then_inc(h_out[ch.s], 16)

            def edges(part, load, store):
                for u in range(2):
                    load(part.chunk(0, u))
                with e.Fori(0, EC // 2 - 1) as i:
                    for u in range(2):
                        load(part.chunk(i, u + 2))
                        store(part.chunk(i, u))
                for u in range(2):
                    store(part.chunk(EC // 2 - 1, u))

            edges(DESTS, load_dest, store_dest)

            for s in range(2):
                e.wait_ge(h_out[s], 16 * (DESTS.k0[s] + EC // 2))
                e.wait_ge(v_used[s], EC // 2)

            def load2_node(ch, rows, first=False):
                if not first:
                    e.wait_ge(x1_done, ch.g * 2 - 2)
                e.dma_start(hin[ch.s][:, :], node_view(h_node, rows)).then_inc(two_in[ch.s], 16)
                e.dma_start(xb[ch.s][:, :], node_view(x, rows)).then_inc(two_in[ch.s], 16)

            def store2_node(ch):
                e.wait_ge(fin_done, ch.c * 2 + 2)
                e.dma_start(node_view(out, node_rows(ch)), x1b[ch.s][:, :]).then_inc(out_stored[ch.s], 16)

            def store2_last(ch):
                e.wait_ge(fin_done, ch.c * 2 + 2)
                e.dma_start(rest_view(out), x1b[ch.s][OVERP:P, :]).then_inc(out_stored[ch.s], 16)

            ahead = (BC - 3) // 2
            for u in range(2):
                load2_node(NODES.chunk(0, u), node_rows(NODES.chunk(0, u)), first=True)
            with e.Fori(0, ahead) as i:
                for u in range(2):
                    load2_node(NODES.chunk(i, u + 2), node_rows(NODES.chunk(i, u + 2)))
                    store2_node(NODES.chunk(i, u))
            load2_node(NODES.chunk(ahead, 2), slice(LAST0, N))
            store2_node(NODES.chunk(ahead, 0))
            store2_node(NODES.chunk(ahead, 1))
            store2_last(NODES.chunk(ahead, 2))

            def load2_edges(ch, h, xs, agg):
                e.wait_ge(x1_done, ch.g * 2 - 2)
                e.dma_start(hin[ch.s][:, 0:ET * D], edge_rows(h, ch)).then_inc(two_in[ch.s], 16)
                e.dma_start(xb[ch.s][:, 0:ET * D], edge_rows(xs, ch)).then_inc(two_in[ch.s], 16)
                e.wait_ge(l_h, ch.g - 1)
                e.dma_start(xc[ch.s][:, 0:ET * D], edge_rows(agg, ch)).then_inc(agg_in[ch.s], 16)

            def load2_source(ch):
                e.wait_ge(kept[ch.s], (ch.w + (EC + 1)) * 16)
                load2_edges(ch, h_src, x_src, agg_src)

            def load2_dest(ch):
                load2_edges(ch, h_dst, x_dst, agg_dst)

            e.wait_ge(x1_done, 2 * BC)
            e.wait_ge(l_h, BC)
            each(e, SOURCES, load2_source)
            each(e, DESTS, load2_dest)

        @block.tensor
        def _(e):
            e.wait_ge(const_made, CONSTS)
            e.wait_ge(idx_float, 1)
            for n, f in enumerate((flt[0], flt[3], flt[5], flt[4])):
                for a in range(2):
                    mm = e.transpose(psum[:, n, a * HT:(a + 1) * HT], f[0:HT, a * P:(a + 1) * P],
                                     ident[0:HT, 0:HT])
            mm.then_inc(idx_turned, 1)
            e.wait_ge(idx_made, 4)
            e.wait_ge(weights_in, 16 * WEIGHTS)

            def gram(ch, first):
                e.wait_ge(ln_h, ch.g + 1)
                for j in range(ch.pairs):
                    mm = e.matmul(ps_g[:, 0:P + 1], hb[ch.s][:, j, 0:P], hb[ch.s][:, j, :],
                                  start=(first and j == 0), stop=False, skip_group_check=True)
                mm.then_inc(h_used[ch.s], 1)

            gram(NODES.chunk(0, 0), True)
            gram(NODES.chunk(0, 1), False)
            with e.Fori(1, BC // 2) as i:
                gram(NODES.chunk(i, 0), False)
                gram(NODES.chunk(i, 1), False)
            gram(NODES.chunk(BC // 2, 0), False)

            def attrs(ch, parts_in):
                e.wait_ge(ea_in[ch.s], (ch.w + 1) * 32 if parts_in is None else parts_in)
                e.wait_ge(msg_made, ch.c)
                for u, (j0, n) in enumerate(quads(ch)):
                    for j in range(j0, j0 + n):
                        mm = e.transpose(ps_t[u][:, (j - j0) * P:(j - j0 + 1) * P],
                                         ea[ch.s][:, j * P:(j + 1) * P], ident[:, :])
                mm.then_inc(ea_turned, 1)
                for u, (j0, n) in enumerate(quads(ch)):
                    e.wait_ge(ea_copied, ch.c * 2 + (u + 1))
                    e.matmul(ps_z[:, u, 0:n * P], we_blk[:, :], ea_t[ch.s][:, j0 * P:(j0 + n) * P],
                             start=True, stop=False, skip_group_check=True)
                e.wait_ge(ln_h, ch.g + 1)
                for u, (j0, n) in enumerate(quads(ch)):
                    for j in range(j0, j0 + n):
                        mm = e.matmul(ps_z[:, u, (j - j0) * P:(j - j0 + 1) * P], hb[ch.s][:, j, 0:P],
                                      ident[:, :], start=False, stop=(j == j0 + n - 1), skip_group_check=True)
                mm.then_inc(h_used[ch.s], 1)

            with e.Fori(0, EC // 2 - 1) as i:
                attrs(SOURCES.chunk(i, 0), None)
                attrs(SOURCES.chunk(i, 1), None)
            attrs(SOURCES.chunk(EC // 2 - 1, 0), None)
            attrs(SOURCES.chunk(EC // 2 - 1, 1), (EC // 2) * 32 + 16)

            def bring(n, col, how, at):
                e.wait_ge(link_col, n)
                e.matmul(ps_o[:, at:at + col.shape[1]], how[:, :], col, start=True, stop=True).then_inc(link_ps, 1)

            bring(2, run_max, swap, 0)
            bring(4, soft_ends, down, 0)

            def turn_agg(ch):
                e.wait_ge(agg_made, ch.c + 1)
                e.wait_ge(agg_rows, ch.c)
                for j in range(EJ):
                    mm = e.transpose(ps_z_flat[:, j * P:(j + 1) * P], agg_t[ch.s][:, j * P:(j + 1) * P],
                                     ident[:, :])
                mm.then_inc(agg_turned, 1)

            each(e, EDGES, turn_agg)

            def gram_dest(ch):
                e.wait_ge(v_made, ch.c + 1)
                for j in range(EJ):
                    mm = e.matmul(ps_g[:, 0:P + 1], hin[ch.s][:, j * P:(j + 1) * P], vb[ch.s][:, j, :],
                                  start=False, stop=False, skip_group_check=True)
                mm.then_inc(v_used[ch.s], 1)

            each(e, EDGES, gram_dest)

            e.wait_ge(stat, 2)
            e.matmul(ps_w[:, 0:H], gram_sb[:, :], w1_dup[:, :], start=True, stop=True).then_inc(stat_ps, 1)
            e.wait_ge(stat, 3)
            e.matmul(ps_o[:, 0:1], gram_w[:, :], ones_col[:, :], start=True, stop=True).then_inc(stat_ps, 1)
            e.matmul(ps_t[0][:, 0:1], w1_dup[:, :], sum_c, start=True, stop=True).then_inc(stat_ps, 1)
            e.wait_ge(bn_ready, 1)

            def front(ch):
                if ch.part is NODES:
                    e.wait_ge(two_in[ch.s], (ch.k + 1) * 32)
                else:
                    e.wait_ge(h_summed, ch.g - BC + 1)
                for u, (j0, n) in enumerate(quads(ch)):
                    for j in range(j0, j0 + n):
                        mm = e.transpose(ps_t[u][:, (j - j0) * P:(j - j0 + 1) * P],
                                         hin[ch.s][:, j * P:(j + 1) * P], ident[:, :])
                    mm.then_inc(t_done, 1)
                for u, (j0, n) in enumerate(quads(ch)):
                    e.wait_ge(t_copied, ch.g * 2 + (u + 1))
                    if u == 1:
                        e.wait_ge(y_done, ch.g * 2 + 1)
                    for a in range(2):
                        mm = e.matmul(ps_z[:, a, 0:n * P], w1_dup[a * D:(a + 1) * D, :],
                                      ht[u][a * D:(a + 1) * D, 0:n * P], start=True, stop=True)
                    mm.then_inc(z_done, 1)
                for u, (j0, n) in enumerate(quads(ch)):
                    e.wait_ge(y_done, ch.g * 2 + (u + 1))
                    e.wait_ge(x1_done, ch.g * 2 + u)
                    for j in range(n):
                        for a in range(2):
                            mm = e.matmul(ps_w[:, (2 * j + a) * D:(2 * j + a + 1) * D],
                                          yb[u][:, (a * 4 + j) * P:(a * 4 + j + 1) * P], w2_sb[:, :],
                                          start=True, stop=True)
                    mm.then_inc(w_done, 1)

            def back(ch):
                f = ch.c if ch.part is NODES else ch.c + BC
                e.wait_ge(l_h, ch.g + 1)
                for u, (j0, n) in enumerate(quads(ch)):
                    for j in range(j0, j0 + n):
                        mm = e.transpose(ps_t1[u][:, (j - j0) * P:(j - j0 + 1) * P], hb[ch.s][:, j, 0:P],
                                         ident[:, :])
                    mm.then_inc(t1_done, 1)
                if ch.part is DESTS:
                    e.wait_ge(mean_made, ch.c + 1)
                for u, (j0, n) in enumerate(quads(ch)):
                    e.wait_ge(t1_copied, f * 2 + (u + 1))
                    e.wait_ge(fin_done, f * 2 + u)
                    e.matmul(ps_o[:, 0:n * P], ones3[:, :], bias3[:, 0:n * P], start=True, stop=False,
                             skip_group_check=True)
                    for j in range(n):
                        o = ps_o[:, j * P:(j + 1) * P]
                        if ch.part is DESTS:
                            e.matmul(o, mean_t[ch.s][:, (j0 + j) * P:(j0 + j + 1) * P], wb_blk[:, :],
                                     start=False, stop=False, skip_group_check=True)
                        mm = e.matmul(o, h1t[u][:, j * P:(j + 1) * P], wa_blk[:, :],
                                      start=False, stop=(j == n - 1), skip_group_check=True)
                    mm.then_inc(o_done, 1)

            def turn_source(ch):
                e.wait_ge(l_h, ch.g + 1)
                e.wait_ge(n_summed, ch.c)
                for j in range(EJ):
                    mm = e.transpose(ps_t1_flat[:, j * P:(j + 1) * P], hb[ch.s][:, j, 0:P], ident[:, :])
                mm.then_inc(hs_turned, 1)

            def front_and(rear):
                def step(before, ch):
                    front(ch)
                    rear(before)
                return step

            walk(e, NODES, front, front_and(back), back)
            walk(e, SOURCES, front, front_and(turn_source), turn_source)
            bring(6, mean_ends, down, 0)
            walk(e, DESTS, front, front_and(back), back)

        @block.scalar
        def _(e):
            e.wait_ge(const_made, CONSTS)

            def square(ch):
                e.wait_ge(ln_centred[ch.s], ch.k + 1)
                e.wait_ge(ln_ssq, ch.g)
                n = ch.tiles * D
                e.activation(sq[:, 0:n], xc[ch.s][:, 0:n], ACT.Square).then_inc(ln_squared, 1)

            def root(ch):
                e.wait_ge(ln_ssq, ch.g + 1)
                e.activation(st[ch.s][:, 2, 0:ch.tiles], st[ch.s][:, 1, 0:ch.tiles], ACT.Sqrt,
                             bias=norm_eps, scale=1.0 / D).then_inc(ln_std, 1)

            def root_and_square(before, ch):
                root(before)
                square(ch)

            walk(e, NODES, square, root_and_square, root)

            def copy_attrs(ch):
                e.wait_ge(ea_turned, ch.c + 1)
                for u, (j0, n) in enumerate(quads(ch)):
                    e.activation(ea_t[ch.s][:, j0 * P:(j0 + n) * P], ps_t[u][:, 0:n * P], ACT.Copy)\
                        .then_inc(ea_copied, 1)

            def source(ch):
                square(ch)
                root(ch)
                copy_attrs(ch)

            each(e, SOURCES, source)

            def exponent(ch):
                e.wait_ge(arg_made, ch.c + 1)
                e.activation(reg_m[:, cols(ch)], reg_m[:, cols(ch)], ACT.Exp).then_inc(exp_made, 1)

            each(e, EDGES, exponent)

            def inverse(ch, ready, region, before, bias):
                e.wait_ge(ready, ch.c + 1)
                e.wait_ge(newton_b, ch.c + before)
                g = inv_place(ch, before)
                e.activation(g, region[:, cols(ch)], ACT.Ln, bias=bias).then_inc(inv_guess, 1)
                e.wait_ge(inv_guess, (ch.c + before) * 2 + 1)
                e.activation(g, g, ACT.Exp, scale=-1.0).then_inc(inv_guess, 1)

            each(e, EDGES, lambda ch: inverse(ch, s_linked, reg_m, 0, soft_eps))

            walk(e, DESTS, square, root_and_square, root)

            e.wait_ge(stat, 6)
            e.activation(std_c, var_c, ACT.Sqrt, bias=norm_eps).then_inc(stat_std, 1)
            e.wait_ge(bn_ready, 1)

            def copy_h(ch):
                for u, (j0, n) in enumerate(quads(ch)):
                    e.wait_ge(t_done, ch.g * 2 + (u + 1))
                    e.activation(ht[u][:, 0:n * P], ps_t[u][:, 0:n * P], ACT.Copy).then_inc(t_copied, 1)

            def hidden(ch):
                for u, (j0, n) in enumerate(quads(ch)):
                    e.wait_ge(z_done, ch.g * 2 + (u + 1))
                    e.activation(yb[u][:, :].rearrange("p (a q) -> p a q", a=2)[:, :, 0:n * P],
                                 ps_z[:, :, 0:n * P], ACT.Relu, bias=shift_c, scale=scale_c).then_inc(y_done, 1)

            def copy_h1(ch):
                f = ch.c if ch.part is NODES else ch.c + BC
                for u, (j0, n) in enumerate(quads(ch)):
                    e.wait_ge(t1_done, f * 2 + (u + 1))
                    e.activation(h1t[u][:, 0:n * P], ps_t1[u][:, 0:n * P], ACT.Copy).then_inc(t1_copied, 1)

            def norm2(ch):
                n = ch.tiles * D
                e.wait_ge(l_centred, ch.g + 1)
                e.activation(sq[:, 0:n], xc[ch.s][:, 0:n], ACT.Square).then_inc(l_squared, 1)
                e.wait_ge(l_ssq, ch.g + 1)
                e.activation(st[ch.s][:, 2, 0:ch.tiles], st[ch.s][:, 1, 0:ch.tiles], ACT.Sqrt,
                             bias=norm_eps, scale=1.0 / D).then_inc(l_std, 1)

            def second(ch):
                copy_h(ch)
                hidden(ch)
                norm2(ch)

            def second_step(before, ch):
                copy_h(ch)
                hidden(ch)
                copy_h1(before)
                norm2(ch)

            walk(e, NODES, second, second_step, copy_h1)
            each(e, SOURCES, second)
            each(e, EDGES, lambda ch: inverse(ch, c_linked, reg_a, EC, 0.0))
            walk(e, DESTS, second, second_step, copy_h1)

        @block.vector
        def _(e):
            for n, pad in enumerate((0, N, N)):
                e.memset(raw[n], pad).then_inc(raw_filled, 1)
            e.wait_ge(raw_in, 16 * 11)
            for n in range(3):
                e.tensor_copy(flt[n][0:HT, :], raw[n][0:HT, :]).then_inc(idx_step, 1)
            e.tensor_copy(other_dst, other_raw[:, :]).then_inc(idx_step, 1)
            e.wait_ge(idx_step, 4)
            e.tensor_scalar(flt[3][0:HT, :], flt[1][0:HT, :], float(N - 1), None, ALU.min).then_inc(idx_step, 1)
            e.tensor_tensor(flt[4][0:HT, :], flt[1][0:HT, :], flt[2][0:HT, :], ALU.not_equal)\
                .then_inc(idx_step, 1)
            e.wait_ge(idx_step, 6)
            e.scalar_tensor_tensor(out=flt[5][0:HT, :], in0=flt[1][0:HT, :], scalar=-float(N),
                                   in1=flt[4][0:HT, :], op0=ALU.add, op1=ALU.mult).then_inc(idx_step, 1)
            e.wait_ge(idx_step, 7)
            e.tensor_scalar(flt[5][0:HT, :], flt[5][0:HT, :], float(N), None, ALU.add).then_inc(idx_float, 1)
            e.wait_ge(idx_turned, 1)
            for n, to in enumerate((src_idx, dst_idx, put_idx, seg_end)):
                e.tensor_copy(to[:, :].rearrange("p (j a) -> p a j", a=2),
                              psum[:, n, 0:2 * HT].rearrange("p (a j) -> p a j", a=2)).then_inc(idx_made, 1)

            e.wait_ge(weights_in, 16 * WEIGHTS)
            e.wait_ge(const_made, CONSTS)
            low = 0
            for n, row in enumerate((0, 32, 64)):
                part = bias_part
                e.tensor_copy(part[:, :], bias_f[n % 2]).then_inc(bias_made, 1)
                low += 1
                e.wait_ge(bias_made, low)
                e.tensor_copy(bias3[row:row + 1, :], part[row:row + 1, :]).then_inc(bias_made, 1)
                e.tensor_tensor(bias_f[1 - n % 2], bias_f[n % 2], part[:, :], ALU.subtract).then_inc(bias_made, 1)
                low += 2
                e.wait_ge(bias_made, low)

            def row_sum(ch):
                e.wait_ge(x_in[ch.s], (ch.k + 1) * 16)
                e.tensor_reduce(st[ch.s][:, 0, 0:ch.tiles], tile_rows(xb[ch.s], ch), AX.X, ALU.add)\
                    .then_inc(ln_sum, 1)

            def centre(ch):
                e.wait_ge(ln_sum, ch.g + 1)
                e.scalar_tensor_tensor(out=tile_rows(xc[ch.s], ch), in0=spread(ch, 0), scalar=-1.0 / D,
                                       in1=tile_rows(xb[ch.s], ch), op0=ALU.mult, op1=ALU.add)\
                    .then_inc(ln_centred[ch.s], 1)

            def square_sum(ch):
                e.wait_ge(ln_squared, ch.g + 1)
                e.tensor_reduce(st[ch.s][:, 1, 0:ch.tiles], tile_rows(sq, ch), AX.X, ALU.add).then_inc(ln_ssq, 1)

            def invert(ch):
                e.wait_ge(ln_std, ch.g + 1)
                e.reciprocal(st[ch.s][:, 3, 0:ch.tiles], st[ch.s][:, 2, 0:ch.tiles]).then_inc(ln_rstd, 1)

            def norm(ch):
                e.wait_ge(ln_rstd, ch.g + 1)
                e.wait_ge(h_used[ch.s], ch.k if ch.part is not DESTS else DESTS.k0[ch.s])
                e.wait_ge(h_out[ch.s], ch.k * 16)
                e.scalar_tensor_tensor(out=hb[ch.s][:, 0:ch.pairs, 0:P], in0=pair_rows(xc[ch.s], ch), scalar=0.0,
                                       in1=spread(ch, 3), op0=ALU.max, op1=ALU.mult).then_inc(ln_h, 1)

            def start(ch):
                row_sum(ch)
                centre(ch)

            def norm_step(before, ch):
                square_sum(before)
                row_sum(ch)
                invert(before)
                centre(ch)
                norm(before)

            def finish_nodes(ch):
                square_sum(ch)
                e.wait_ge(ln_std, ch.g + 1)
                e.reciprocal(st[ch.s][:, 3, :], st[ch.s][:, 2, :]).then_inc(edges_set, 1)
                e.wait_ge(edges_set, 1)
                e.tensor_scalar(st[ch.s][:, 3, :], st[ch.s][:, 3, :], own_rows[:, :], None, ALU.mult)\
                    .then_inc(ln_rstd, 1)
                norm(ch)

            walk(e, NODES, start, norm_step, finish_nodes)

            e.wait_ge(zeroed, 16 * BC)
            e.memset(same[:, HALF:HALF + 1], 0).then_inc(edges_set, 1)

            def before_col(region, ch):
                return region[:, ds(ch.c * W - 1, 1)]

            def masks(ch, where):
                d = dcol[ch.s]
                e.wait_ge(dcol_in[ch.s], (ch.w + 1) * 32)
                if where == "first":
                    e.memset(d[:, 0:1], -1).then_inc(edges_set, 1)
                    e.wait_ge(edges_set, 3)
                if where == "last":
                    e.memset(d[D:P, W + 1 - PADS:W + 1], N).then_inc(edges_set, 1)
                    e.wait_ge(edges_set, 4)
                e.tensor_tensor(same[:, cols(ch)], d[:, 1:W + 1], d[:, 0:W], ALU.is_equal).then_inc(same_made, 1)
                e.tensor_scalar(linked[:, cols(ch)], d[:, 1:W + 1], other_dst, None, ALU.is_equal)\
                    .then_inc(linked_made, 1)

            def messages(ch, where):
                e.wait_ge(h_used[ch.s], ch.k + 1)
                e.tensor_scalar(reg_a[:, cols(ch)], ps_z_flat[:, 0:W], 0.0, MSG_EPS, ALU.max, ALU.add)\
                    .then_inc(msg_made, 1)
                e.wait_ge(msg_made, ch.c + 1)
                e.wait_ge(same_made, ch.c + 1)
                if where == "first":
                    initial = 0.0
                else:
                    e.wait_ge(run_made, ch.c)
                    initial = before_col(reg_m, ch)
                e.tensor_tensor_scan(reg_m[:, cols(ch)], same[:, cols(ch)], reg_a[:, cols(ch)], initial,
                                     ALU.mult, ALU.max).then_inc(run_made, 1)

            def source(ch, where):
                row_sum(ch)
                centre(ch)
                masks(ch, where)
                square_sum(ch)
                invert(ch)
                norm(ch)
                messages(ch, where)

            source(SOURCES.chunk(0, 0), "first")
            source(SOURCES.chunk(0, 1), "inner")
            with e.Fori(1, EC // 2 - 1) as i:
                source(SOURCES.chunk(i, 0), "inner")
                source(SOURCES.chunk(i, 1), "inner")
            source(SOURCES.chunk(EC // 2 - 1, 0), "inner")
            source(SOURCES.chunk(EC // 2 - 1, 1), "last")

            e.wait_ge(run_made, EC)
            e.tensor_tensor_scan(reg_m[:, ::-1], same[:, 1:HALF + 1][:, ::-1], reg_m[:, ::-1], 0.0,
                                 ALU.mult, ALU.max).then_inc(max_made, 1)

            e.wait_ge(max_made, 1)
            e.tensor_copy(run_max[0:D, :], reg_m[0:D, HALF - 1:HALF]).then_inc(link_col, 1)
            e.tensor_copy(run_max[D:P, :], reg_m[D:P, 0:1]).then_inc(link_col, 1)
            e.wait_ge(link_ps, 1)
            e.wait_ge(link_col, 2)
            e.tensor_tensor(tot_max, ps_o[:, 0:1], run_max, ALU.max).then_inc(link_made, 1)
            e.wait_ge(link_made, 1)

            def argument(ch):
                m, a = reg_m[:, cols(ch)], reg_a[:, cols(ch)]
                e.scalar_tensor_tensor(out=m, in0=linked[:, cols(ch)], scalar=tot_max, in1=m,
                                       op0=ALU.mult, op1=ALU.max).then_inc(max_linked, 1)
                e.wait_ge(max_linked, ch.c + 1)
                e.tensor_tensor(m, a, m, ALU.subtract).then_inc(arg_made, 1)

            def sums(ch, first=False):
                m, a, keep = reg_m[:, cols(ch)], reg_a[:, cols(ch)], same[:, cols(ch)]
                e.wait_ge(exp_made, ch.c + 1)
                e.tensor_tensor(a, a, m, ALU.mult).then_inc(weighted, 1)
                if not first:
                    e.wait_ge(e_summed, ch.c)
                e.tensor_tensor_scan(m, keep, m, 0.0 if first else before_col(reg_m, ch), ALU.mult, ALU.add)\
                    .then_inc(e_summed, 1)
                e.wait_ge(weighted, ch.c + 1)
                if not first:
                    e.wait_ge(a_summed, ch.c)
                e.tensor_tensor_scan(a, keep, a, 0.0 if first else before_col(reg_a, ch), ALU.mult, ALU.add)\
                    .then_inc(a_summed, 1)

            argument(EDGES.chunk(0, 0))
            argument(EDGES.chunk(0, 1))
            sums(EDGES.chunk(0, 0), first=True)
            with e.Fori(0, EC // 2 - 1) as i:
                argument(EDGES.chunk(i, 2))
                sums(EDGES.chunk(i, 1))
                argument(EDGES.chunk(i, 3))
                sums(EDGES.chunk(i, 2))
            sums(EDGES.chunk(EC // 2 - 1, 1))

            def border_sums(ends, carry, n, a_ready, b_ready):
                e.wait_ge(a_ready, EC)
                e.wait_ge(b_ready, EC)
                e.tensor_copy(ends[:, 0:1], reg_m[:, HALF - 1:HALF]).then_inc(link_col, 1)
                e.tensor_copy(ends[:, 1:2], reg_a[:, HALF - 1:HALF]).then_inc(link_col, 1)
                e.wait_ge(link_ps, n)
                e.tensor_copy(carry, ps_o[:, 0:2]).then_inc(link_made, 1)
                e.wait_ge(link_made, n)

            border_sums(soft_ends, soft_carry, 2, e_summed, a_summed)

            def link(ch, region, carry, done):
                r = region[:, cols(ch)]
                e.scalar_tensor_tensor(out=r, in0=linked[:, cols(ch)], scalar=carry, in1=r,
                                       op0=ALU.mult, op1=ALU.add).then_inc(done, 1)

            def newton(ch, region, bias, before):
                g, r = inv_place(ch, before), region[:, cols(ch)]
                e.wait_ge(inv_guess, (ch.c + before) * 2 + 2)
                e.scalar_tensor_tensor(out=r, in0=r, scalar=bias, in1=g, op0=ALU.add, op1=ALU.mult)\
                    .then_inc(newton_a, 1)
                e.wait_ge(newton_a, ch.c + (before + 1))
                e.scalar_tensor_tensor(out=r, in0=r, scalar=-2.0, in1=g, op0=ALU.add, op1=ALU.mult)\
                    .then_inc(newton_b, 1)
                e.wait_ge(newton_b, ch.c + (before + 1))

            for s in range(2):
                e.wait_ge(kept[s], 16 * EC)

            def aggregate(ch):
                link(ch, reg_m, soft_carry[:, 0:1], s_linked)
                link(ch, reg_a, soft_carry[:, 1:2], a_linked)
                newton(ch, reg_m, SOFTMAX_EPS, 0)
                e.wait_ge(a_linked, ch.c + 1)
                e.scalar_tensor_tensor(out=agg_t[ch.s][:, 0:W], in0=reg_m[:, cols(ch)], scalar=-1.0,
                                       in1=reg_a[:, cols(ch)], op0=ALU.mult, op1=ALU.mult).then_inc(agg_made, 1)
                e.wait_ge(agg_turned, ch.c + 1)
                e.wait_ge(agg_stored[ch.s], ch.w * 16)
                e.wait_ge(agg_put[ch.s], ch.w * (16 * ET))
                end = seg_end[:, ds(ch.c * ET, ET)].unsqueeze(2).to_broadcast([P, ET, D])
                e.tensor_tensor(tile_rows(gb[ch.s], ch), ps_z_flat[:, 0:W].rearrange("p (t d) -> p t d", d=D),
                                end, ALU.mult).then_inc(agg_rows, 1)

            each(e, EDGES, aggregate)

            for s in range(2):
                e.memset(vb[s][:, :, P:P + 1], 1.0).then_inc(edges_set, 1)

            def gram_input(ch):
                e.wait_ge(ln_h, ch.g + 1)
                e.wait_ge(d_in[ch.s], (ch.w + 1) * 16)
                e.wait_ge(v_used[ch.s], ch.w)
                e.wait_ge(edges_set, 6)
                e.scalar_tensor_tensor(out=vb[ch.s][:, :, 0:P], in0=hb[ch.s][:, 0:EJ, 0:P], scalar=2.0,
                                       in1=pair_rows(hin[ch.s], ch), op0=ALU.mult, op1=ALU.add).then_inc(v_made, 1)

            def dest_step(before, ch):
                norm_step(before, ch)
                gram_input(before)

            def dest_last(ch):
                square_sum(ch)
                invert(ch)
                norm(ch)
                gram_input(ch)

            walk(e, DESTS, start, dest_step, dest_last)

            for s in range(2):
                e.wait_ge(v_used[s], EC // 2)
            e.tensor_tensor(gram_sb[:, :], ps_g[:, 0:P], blocks[:, :], ALU.mult).then_inc(stat, 1)
            e.tensor_copy(sum_c, ps_g[:, P:P + 1]).then_inc(stat, 1)
            e.wait_ge(stat_ps, 1)
            e.tensor_tensor(gram_w[:, :], ps_w[:, 0:H], w1_dup[:, :], ALU.mult).then_inc(stat, 1)
            e.wait_ge(stat_ps, 3)
            e.tensor_scalar(ex2_c, ps_o[:, 0:1], 1.0 / N, None, ALU.mult).then_inc(stat, 1)
            e.tensor_scalar(mean_c, ps_t[0][:, 0:1], 1.0 / N, None, ALU.mult).then_inc(stat, 1)
            e.wait_ge(stat, 5)
            e.tensor_tensor(m2_c, mean_c, mean_c, ALU.mult).then_inc(stat_mid, 1)
            e.wait_ge(stat_mid, 1)
            e.tensor_tensor(m2_c, ex2_c, m2_c, ALU.subtract).then_inc(stat_mid, 1)
            e.wait_ge(stat_mid, 2)
            e.tensor_scalar(var_c, m2_c, 0.0, None, ALU.max).then_inc(stat, 1)
            e.wait_ge(stat_std, 1)
            e.reciprocal(rs_c, std_c).then_inc(stat_mid, 1)
            e.wait_ge(stat_mid, 3)
            e.tensor_tensor(scale_c, gamma_c, rs_c, ALU.mult).then_inc(stat_mid, 1)
            e.wait_ge(stat_mid, 4)
            e.tensor_tensor(mscale_c, mean_c, scale_c, ALU.mult).then_inc(stat_mid, 1)
            e.wait_ge(stat_mid, 5)
            e.tensor_tensor(shift_c, beta_c, mscale_c, ALU.subtract).then_inc(bn_ready, 1)

            def add_agg(ch):
                n = ET * D
                e.wait_ge(two_in[ch.s], (ch.k + 1) * 32)
                e.wait_ge(agg_in[ch.s], (ch.k - SOURCES.k0[ch.s] + 1) * 16)
                e.tensor_tensor(hin[ch.s][:, 0:n], hin[ch.s][:, 0:n], xc[ch.s][:, 0:n], ALU.add)\
                    .then_inc(h_summed, 1)

            def residual(ch):
                if ch.part is NODES:
                    e.wait_ge(two_in[ch.s], (ch.k + 1) * 32)
                    e.wait_ge(out_stored[ch.s], ch.k * 16)
                if ch.part is DESTS:
                    e.wait_ge(patched[ch.s], ch.w * (16 * ET))
                for u, (j0, n) in enumerate(quads(ch)):
                    part = slice(j0 * P, (j0 + n) * P)
                    e.wait_ge(w_done, ch.g * 2 + (u + 1))
                    e.tensor_tensor(x1b[ch.s][:, part], ps_w[:, 0:n * P], xb[ch.s][:, part], ALU.add)\
                        .then_inc(x1_done, 1)
                e.wait_ge(x1_done, ch.g * 2 + 2)
                e.tensor_reduce(st[ch.s][:, 0, 0:ch.tiles], tile_rows(x1b[ch.s], ch), AX.X, ALU.add)\
                    .then_inc(l_sum, 1)
                e.wait_ge(l_sum, ch.g + 1)
                e.scalar_tensor_tensor(out=tile_rows(xc[ch.s], ch), in0=spread(ch, 0), scalar=-1.0 / D,
                                       in1=tile_rows(x1b[ch.s], ch), op0=ALU.mult, op1=ALU.add)\
                    .then_inc(l_centred, 1)

            def norm2(ch):
                e.wait_ge(l_squared, ch.g + 1)
                e.tensor_reduce(st[ch.s][:, 1, 0:ch.tiles], tile_rows(sq, ch), AX.X, ALU.add).then_inc(l_ssq, 1)
                e.wait_ge(l_std, ch.g + 1)
                e.reciprocal(st[ch.s][:, 3, 0:ch.tiles], st[ch.s][:, 2, 0:ch.tiles]).then_inc(l_rstd, 1)
                e.wait_ge(l_rstd, ch.g + 1)
                e.scalar_tensor_tensor(out=hb[ch.s][:, 0:ch.pairs, 0:P], in0=pair_rows(xc[ch.s], ch), scalar=0.0,
                                       in1=spread(ch, 3), op0=ALU.max, op1=ALU.mult).then_inc(l_h, 1)

            def final(ch):
                f = ch.c if ch.part is NODES else ch.c + BC
                for u, (j0, n) in enumerate(quads(ch)):
                    part = slice(j0 * P, (j0 + n) * P)
                    e.wait_ge(o_done, f * 2 + (u + 1))
                    e.scalar_tensor_tensor(out=x1b[ch.s][:, part], in0=ps_o[:, 0:n * P], scalar=0.0,
                                           in1=x1b[ch.s][:, part], op0=ALU.max, op1=ALU.add).then_inc(fin_done, 1)

            def node_first(ch):
                residual(ch)
                norm2(ch)

            def node_step(before, ch):
                residual(ch)
                final(before)
                norm2(ch)

            walk(e, NODES, node_first, node_step, final)

            def neighbours(ch, first=False):
                e.wait_ge(hs_turned, ch.c + 1)
                if not first:
                    e.wait_ge(n_summed, ch.c)
                    e.wait_ge(c_summed, ch.c)
                e.tensor_tensor_scan(reg_m[:, cols(ch)], same[:, cols(ch)], ps_t1_flat[:, 0:W],
                                     0.0 if first else before_col(reg_m, ch), ALU.mult, ALU.add).then_inc(n_summed, 1)
                e.tensor_tensor_scan(reg_a[:, cols(ch)], same[:, cols(ch)], ones_row[:, :],
                                     0.0 if first else before_col(reg_a, ch), ALU.mult, ALU.add).then_inc(c_summed, 1)

            def edge_front(ch):
                residual(ch)
                norm2(ch)

            e.wait_ge(out_stored[0], 16 * ((BC + 1) // 2))
            e.wait_ge(out_stored[1], 16 * (BC // 2))
            add_agg(SOURCES.chunk(0, 0))
            edge_front(SOURCES.chunk(0, 0))
            add_agg(SOURCES.chunk(0, 1))
            edge_front(SOURCES.chunk(0, 1))
            neighbours(SOURCES.chunk(0, 0), first=True)
            with e.Fori(0, EC // 2 - 1) as i:
                add_agg(SOURCES.chunk(i, 2))
                edge_front(SOURCES.chunk(i, 2))
                neighbours(SOURCES.chunk(i, 1))
                add_agg(SOURCES.chunk(i, 3))
                edge_front(SOURCES.chunk(i, 3))
                neighbours(SOURCES.chunk(i, 2))
            neighbours(SOURCES.chunk(EC // 2 - 1, 1))

            border_sums(mean_ends, mean_carry, 3, n_summed, c_summed)

            def count_inverse(ch):
                link(ch, reg_a, mean_carry[:, 1:2], c_linked)
                link(ch, reg_m, mean_carry[:, 0:1], n_linked)
                newton(ch, reg_a, 0.0, EC)

            each(e, EDGES, count_inverse)
            e.wait_ge(n_linked, EC)

            def mean(ch):
                e.scalar_tensor_tensor(out=mean_t[ch.s][:, 0:W], in0=reg_a[:, cols(ch)], scalar=-1.0,
                                       in1=reg_m[:, cols(ch)], op0=ALU.mult, op1=ALU.mult).then_inc(mean_made, 1)

            def dest_first(ch):
                add_agg(ch)
                residual(ch)
                norm2(ch)
                mean(ch)

            def dest2_step(before, ch):
                add_agg(ch)
                residual(ch)
                final(before)
                norm2(ch)
                mean(ch)

            walk(e, DESTS, dest_first, dest2_step, final)


_INS = ["x", "src", "dst", "edge_attr_64", "L0_gnn_W_edge", "L0_gnn_W1", "L0_gnn_gamma", "L0_gnn_beta",
        "L0_gnn_W2", "L1_gnn_W", "L1_gnn_b"]


def kernel(**inputs):
    import concourse.bacc as _bacc
    from concourse.bass_utils import run_bass_kernel_spmd as _run

    nc = _bacc.Bacc("TRN2", target_bir_lowering=False, num_devices=1)
    arrays, args = {}, []
    for name in _INS:
        a = np.ascontiguousarray(inputs[name])
        arrays[f"in_{name}_dram"] = a
        args.append(nc.dram_tensor(f"in_{name}_dram", a.shape, mybir.dt.from_np(a.dtype), kind="ExternalInput").ap())
    args.append(nc.dram_tensor("out_0_dram", inputs["x"].shape, F32, kind="ExternalOutput").ap())
    build(nc, *args)
    r = _run(nc, [arrays], core_ids=[0])
    return r.results[0]["out_0_dram"]
```

```python
from contextlib import ExitStack

import numpy as np

import concourse.bass as bass
from concourse import mybir

F32 = mybir.dt.float32
BF16 = mybir.dt.bfloat16
I32 = mybir.dt.int32
U8 = mybir.dt.uint8
ALU = mybir.AluOpType
ACT = mybir.ActivationFunctionType
AX = mybir.AxisListType

P = 128
LN_EPS = 1e-5
BN_EPS = 1e-5
MSG_EPS = 1e-7
SOFTMAX_EPS = 1e-16


def ds(start, size):
    return bass.ds(start, size)


class Part:

    def __init__(self, n, g0, k0, tiles):
        self.n, self.g0, self.k0, self.tiles = n, g0, k0, tiles

    def after(self, n, tiles):
        return Part(n, self.g0 + self.n, (self.k0[0] + (self.n + 1) // 2, self.k0[1] + self.n // 2), tiles)


class Chunk:

    def __init__(self, part, unroll, i, u):
        self.part, self.tiles, self.pairs = part, part.tiles, part.tiles // 2
        self.c = i * unroll + u
        self.g = self.c + part.g0
        self.s = u % 2
        self.w = i * (unroll // 2) + u // 2
        self.k = self.w + part.k0[self.s]
        self.q = u % 4
        self.v = i * (unroll // 4) + u // 4


def run(e, part, step, lag=0, lead=0, unroll=2):
    first = 4 if unroll == 4 else 2 + (lag + 1) // 2 * 2
    rounds = max(0, (part.n - lead - first) // unroll)

    def alone(c):
        def at(d):
            if not 0 <= c + d < part.n:
                return None
            return Chunk(part, 4 if unroll == 4 else 2, 0, c + d)
        step(at)

    for c in range(first):
        alone(c)
    with e.Fori(0, rounds) as i:
        for u in range(unroll):
            step(lambda d, u=u: Chunk(part, unroll, i, first + u + d))
    for c in range(first + rounds * unroll, part.n + lag):
        alone(c)


def build(nc, x, src, dst, edge_attr, w_edge, w1, gamma, beta, w2, w_out, b_out, out):
    N, D = x.shape
    E = src.shape[0]
    H = w1.shape[1]
    assert D == 64 and H == P

    BT = 16
    BROWS = BT * P
    BC = -(-N // BROWS)
    LAST0 = N - BROWS
    OVER = BC * BROWS - N
    assert OVER % BT == 0 and BC % 2 == 1
    OVERP = OVER // BT

    EJ = 7
    HT = -(-E // (2 * P * EJ)) * EJ
    HALF = HT * P
    ET = 2 * EJ
    EC = HT // EJ
    assert EC % 2 == 0
    W = EJ * P
    PADS = 2 * HALF - E
    assert 0 < PADS < P - 1
    TAIL = P - PADS

    NODES = Part(BC, 0, (0, 0), BT)
    SOURCES = NODES.after(EC, ET)
    DESTS = SOURCES.after(EC, ET)
    EDGES = Part(EC, 0, (0, 0), ET)

    agg_tab = nc.dram_tensor("agg_tab", [N, D], F32, kind="Internal").ap()
    ht_node = nc.dram_tensor("ht_node", [BC * P, BT * D], F32, kind="Internal").ap()
    x_src, x_dst, h_src, h_dst, agg_src, agg_dst = (
        nc.dram_tensor(n, [EC * P, ET * D], F32, kind="Internal").ap()
        for n in ("x_src", "x_dst", "h_src", "h_dst", "agg_src", "agg_dst"))

    with ExitStack() as ctx:
        def sb(name, shape, dt=F32):
            return ctx.enter_context(nc.sbuf_tensor(name, shape, dt))

        def sem(name):
            return ctx.enter_context(nc.semaphore(name))

        def sem2(name):
            return [sem(f"{name}_{s}") for s in range(2)]

        def sem4(name):
            return [sem(f"{name}_{q}") for q in range(4)]

        ident = sb("ident", [P, P])
        swap = sb("swap", [P, P])
        down = sb("down", [P, P])
        blocks = sb("blocks", [P, P])
        ones_col = sb("ones_col", [P, 1])
        own_rows = sb("own_rows", [P, 1])
        ones_row = sb("ones_row", [P, W], BF16)
        ones3 = sb("ones3", [96, P], BF16)
        bias3 = sb("bias3", [96, 8 * D], BF16)
        we_blk = sb("we_blk", [P, P])
        wa_blk = sb("wa_blk", [P, P])
        wb_blk = sb("wb_blk", [P, P])
        w1_dup = sb("w1_dup", [P, H])
        w2_sb = sb("w2_sb", [H, D])
        vecs = sb("vecs", [P, 16])
        (gamma_c, beta_c, mean_c, ex2_c, m2_c, var_c, std_c, rs_c, scale_c, mscale_c, shift_c, sum_c,
         norm_eps, soft_eps) = (vecs[:, n:n + 1] for n in range(14))
        gram_sb = sb("gram_sb", [P, P])
        gram_w = sb("gram_w", [P, H])
        links = sb("links", [P, 16])
        run_max, tot_max, other_dst = (links[:, n:n + 1] for n in range(3))
        soft_ends, soft_carry, mean_ends, mean_carry = (links[:, n:n + 2] for n in (4, 6, 8, 10))

        src_idx = sb("src_idx", [P, HT * 2], I32)
        dst_idx = sb("dst_idx", [P, HT * 2], I32)
        put_idx = sb("put_idx", [P, HT * 2], I32)
        seg_end = sb("seg_end", [P, HT * 2])
        other_raw = sb("other_raw", [P, 1], I32)
        stage_idx = [sb(f"stage_idx{s}", [P, ET], I32) for s in range(2)]

        reg_m = sb("reg_m", [P, HALF])
        reg_a = sb("reg_a", [P, HALF])
        same = sb("same", [P, HALF + 4], U8)
        linked = sb("linked", [P, HALF], U8)

        xb = [sb(f"xb{s}", [P, BT * D]) for s in range(2)]
        xc = [sb(f"xc{s}", [P, BT * D]) for s in range(2)]
        sq = sb("sq", [P, BT * D])
        hb = [sb(f"hb{s}", [P, BT // 2, P + 1]) for s in range(2)]
        hin = [sb(f"hin{s}", [P, BT * D]) for s in range(2)]
        x1b = [sb(f"x1b{s}", [P, BT * D]) for s in range(2)]
        ht = [sb(f"ht{u}", [P, 4 * P]) for u in range(2)]
        yb = [sb(f"yb{u}", [P, 2 * 4 * P]) for u in range(2)]
        h1t = [sb(f"h1t{u}", [P, 4 * P]) for u in range(2)]
        gb = [sb(f"gb{s}", [P, ET * D]) for s in range(2)]
        st = [sb(f"st{s}", [P, 4, BT]) for s in range(2)]

        bias_part = sb("bias_part", [96, 8 * D], BF16)

        ea = hin
        ea_t = yb
        dcol = [x1b[s][:, 0:W + 1].bitcast(I32) for s in range(2)]
        vb = [x1b[s][:, 0:EJ * (P + 1)].rearrange("p (j q) -> p j q", q=P + 1) for s in range(2)]
        agg_t = yb
        mean_t = gb
        raw = [reg_m[:, n * 2 * P:(n + 1) * 2 * P].bitcast(I32) for n in range(3)]
        flt = [reg_m[:, (n + 3) * 2 * P:(n + 4) * 2 * P] for n in range(6)]
        bias_f = [reg_m[0:96, (n + 9) * 2 * P:(n + 9) * 2 * P + 8 * D] for n in (0, 2, 4)]
        zeros = reg_a[:, 0:BT * D]
        node_h, node_x, node_x1 = ([reg_a[:, n * BT * D:(n + 1) * BT * D] for n in range(m, m + 4)]
                                   for m in (0, 4, 8))
        agg_s = [gb[s][:, :] for s in range(2)]
        spare = [same[:, n * 4 * W:(n + 1) * 4 * W].bitcast(F32) for n in range(3)]
        source_x1 = [x1b[s][:, 0:W] for s in (0, 1, 0, 1)]
        dest_x1 = [x1b[0][:, 0:W], x1b[1][:, 0:W], spare[0], spare[1]]
        count_guess = spare[2]

        psum = ctx.enter_context(nc.psum_tensor("psum", [P, 8, 512], F32))
        ps_t = [psum[:, 0, :], psum[:, 1, :]]
        ps_t_flat = psum[:, 0:2, :].rearrange("p a b -> p (a b)")
        ps_z = psum[:, 2:4, :]
        ps_z_flat = psum[:, 2:4, :].rearrange("p a b -> p (a b)")
        ps_w = psum[:, 4, :]
        ps_o = psum[:, 5, :]
        ps_t1 = [psum[:, 6, :], psum[:, 7, :]]
        ps_t1_flat = psum[:, 6:8, :].rearrange("p a b -> p (a b)")
        ps_agg = [ps_z_flat, ps_t_flat]
        ps_g = psum[:, 7, :]

        const_made, raw_filled, raw_in, idx_float, idx_step, idx_turned, idx_made = \
            (sem(n) for n in ("const_made", "raw_filled", "raw_in", "idx_float", "idx_step", "idx_turned",
                              "idx_made"))
        weights_in, bias_made, zeroed, staged = \
            (sem(n) for n in ("weights_in", "bias_made", "zeroed", "staged"))
        gathered, kept = sem2("gathered"), sem2("kept")
        pool_steps, sync_steps = sem("pool_steps"), sem("sync_steps")
        x_in, ln_centred, h_used, h_out, ht_out = \
            (sem2(n) for n in ("x_in", "ln_centred", "h_used", "h_out", "ht_out"))
        ln_sum, ln_squared, ln_ssq, ln_std, ln_rstd, ln_h, ht_turned, ht_copied = \
            (sem(n) for n in ("ln_sum", "ln_squared", "ln_ssq", "ln_std", "ln_rstd", "ln_h", "ht_turned",
                              "ht_copied"))
        ea_in, dcol_in, d_in, v_used = (sem2(n) for n in ("ea_in", "dcol_in", "d_in", "v_used"))
        ea_turned, ea_copied, same_made, linked_made, msg_made, run_made, edges_set, v_made = \
            (sem(n) for n in ("ea_turned", "ea_copied", "same_made", "linked_made", "msg_made", "run_made",
                              "edges_set", "v_made"))
        max_made, link_col, link_ps, link_made, max_linked, arg_made, exp_made, weighted, e_summed, a_summed = \
            (sem(n) for n in ("max_made", "link_col", "link_ps", "link_made", "max_linked", "arg_made",
                              "exp_made", "weighted", "e_summed", "a_summed"))
        s_linked, a_linked, inv_guess, newton_a, newton_b, agg_made, agg_turned, agg_rows, agg_moved = \
            (sem(n) for n in ("s_linked", "a_linked", "inv_guess", "newton_a", "newton_b", "agg_made",
                              "agg_turned", "agg_rows", "agg_moved"))
        agg_stored, agg_put = sem2("agg_stored"), sem2("agg_put")
        stat, stat_mid, stat_ps, stat_std, bn_ready = \
            (sem(n) for n in ("stat", "stat_mid", "stat_ps", "stat_std", "bn_ready"))
        dest_summed, agg2_in = sem("dest_summed"), sem2("agg2_in")
        node_in, out_stored, patched = sem4("node_in"), sem4("out_stored"), sem4("patched")
        h2_in, x2_in = sem2("h2_in"), sem2("x2_in")
        h_summed, t_done, t_copied, z_done, y_done, w_done, x1_done = \
            (sem(n) for n in ("h_summed", "t_done", "t_copied", "z_done", "y_done", "w_done", "x1_done"))
        l_sum, l_centred, l_squared, l_ssq, l_std, l_rstd, l_h = \
            (sem(n) for n in ("l_sum", "l_centred", "l_squared", "l_ssq", "l_std", "l_rstd", "l_h"))
        t1_done, t1_copied, o_done, fin_done, hs_turned = \
            (sem(n) for n in ("t1_done", "t1_copied", "o_done", "fin_done", "hs_turned"))
        n_summed, c_summed, n_linked, c_linked, mean_made = \
            (sem(n) for n in ("n_summed", "c_summed", "n_linked", "c_linked", "mean_made"))

        block = ctx.enter_context(nc.Block())

        CONSTS = 24
        WEIGHTS = 12
        STAGED = (0, EC, 3 * EC)

        def used(chunks, slots, s):
            return (chunks - s + slots - 1) // slots

        def wait_past(e, which, value):
            if not (isinstance(value, int) and value <= 0):
                e.wait_ge(which, value)

        def inv_place(ch, before):
            return count_guess if before else xc[ch.s][:, 0:W]

        def cols(ch):
            return ds(ch.c * W, W)

        def node_view(t, rows):
            return t[rows, :].rearrange("(p t) d -> p (t d)", p=P)

        def node_rows(ch):
            return ds(ch.c * BROWS, BROWS)

        def edge_rows(t, ch):
            return t[ds(ch.c * P, P), :]

        def tile_rows(buf, ch):
            return buf[:, 0:ch.tiles * D].rearrange("p (t d) -> p t d", d=D)

        def pair_rows(buf, ch):
            return buf[:, 0:ch.tiles * D].rearrange("p (j q) -> p j q", q=2 * D)

        def spread(ch, row):
            return st[ch.s][:, row, 0:ch.tiles].unsqueeze(2).to_broadcast([P, ch.tiles, D])

        def quads(ch):
            return ((0, 4), (4, ch.pairs - 4))

        def outs(ch):
            return ch.c if ch.part is NODES else ch.c + BC

        def w_bank(ch, u):
            if u == 1 and ch.part is not DESTS:
                return ps_t[0] if ch.part is NODES else ps_o
            return ps_w

        def o_bank(ch, u):
            return ps_t[1] if ch.part is NODES and u == 1 else ps_o

        @block.gpsimd
        def _(e):
            made = 0

            def note(ins):
                nonlocal made
                ins.then_inc(const_made, 1)
                made += 1

            def diagonal(ap, base):
                e.wait_ge(const_made, made)
                note(e.affine_select(out=ap, in_=ap, compare_op=ALU.not_equal, fill=1.0, base=base,
                                     pattern=[[-1, P]], channel_multiplier=1))

            for m in (ident, swap, down, blocks, bias3, we_blk, wa_blk, wb_blk):
                note(e.memset(m[:, :], 0.0))
            for m in (ones_col, own_rows, ones_row, ones3):
                note(e.memset(m[:, :], 1.0))
            for m in hb:
                note(e.memset(m[:, :, P:P + 1], 1.0))
            note(e.memset(norm_eps, LN_EPS))
            note(e.memset(soft_eps, SOFTMAX_EPS))
            note(e.memset(zeros, 0.0))
            diagonal(ident[:, :], 0)
            diagonal(swap[:, :], D)
            diagonal(swap[:, :], -D)
            diagonal(down[:, :], D)
            for half in (slice(0, D), slice(D, P)):
                e.wait_ge(const_made, made)
                note(e.memset(blocks[half, half], 1.0))
            e.wait_ge(const_made, made)
            note(e.affine_select(out=own_rows[:, :], in_=own_rows[:, :], compare_op=ALU.is_ge, fill=0.0,
                                 base=-OVERP, pattern=[[0, 1]], channel_multiplier=1))
            assert made == CONSTS

            def stage(idx, ch, before):
                e.tensor_copy(stage_idx[ch.s][:, :], idx[:, ds(ch.c * ET, ET)]).then_inc(staged, 1)
                e.wait_ge(staged, ch.c + (before + 1))
                e.sem_inc(pool_steps, 1)

            def gather(table, idx, rows, turn):
                part = Part(EC, 0, (turn * EC // 2, turn * EC // 2), ET)

                def get(ch):
                    wait_past(e, kept[ch.s], ch.k * 16)
                    stage(idx, ch, STAGED[turn])
                    for t in range(ET):
                        e.indirect_dma_start(
                            gb[ch.s][:, t * D:(t + 1) * D], None, table,
                            bass.IndirectOffsetOnAxis(ap=stage_idx[ch.s][:, t:t + 1], axis=0),
                        ).then_inc(gathered[ch.s], 16)

                def keep(ch):
                    e.wait_ge(gathered[ch.s], (ch.k + 1) * (16 * ET))
                    e.dma_start(edge_rows(rows, ch), gb[ch.s][:, :]).then_inc(kept[ch.s], 16)

                def get_and_keep(at):
                    if at(0):
                        get(at(0))
                    if at(-1):
                        keep(at(-1))

                run(e, part, get_and_keep, lag=1)

            def put(table, buf, ch, done):
                for t in range(ET):
                    e.indirect_dma_start(
                        table, bass.IndirectOffsetOnAxis(ap=stage_idx[ch.s][:, t:t + 1], axis=0),
                        buf[:, t * D:(t + 1) * D], None, bounds_check=N - 1, oob_is_err=False,
                    ).then_inc(done, 16)

            e.wait_ge(idx_made, 4)
            gather(x, src_idx, x_src, 0)
            gather(x, dst_idx, x_dst, 1)

            for s in range(2):
                e.wait_ge(kept[s], 16 * EC)
            e.wait_ge(zeroed, 16 * BC)

            def put_agg(at):
                ch = at(0)
                e.wait_ge(agg_rows, ch.c + 1)
                wait_past(e, agg_put[ch.s], ch.w * (16 * ET))
                e.tensor_copy(gb[ch.s][:, :], reg_m[:, cols(ch)]).then_inc(agg_moved, 1)
                stage(put_idx, ch, 2 * EC)
                e.wait_ge(agg_moved, ch.c + 1)
                e.sem_inc(pool_steps, 1)
                put(agg_tab, gb[ch.s], ch, agg_put[ch.s])

            run(e, EDGES, put_agg)
            for s in range(2):
                e.wait_ge(agg_put[s], 16 * ET * (EC // 2))
            gather(agg_tab, src_idx, agg_src, 2)

            for q in range(4):
                e.wait_ge(out_stored[q], 16 * used(BC, 4, q))

            def put_out(at):
                ch = at(0)
                e.wait_ge(fin_done, ch.c * 2 + 2 * (BC + 1))
                if at(-2):
                    e.wait_ge(patched[at(-2).q], (at(-2).v + 1) * (16 * ET))
                stage(put_idx, ch, 4 * EC)
                put(out, dest_x1[ch.q], ch, patched[ch.q])

            run(e, EDGES, put_out, unroll=4)
            for q in range(4):
                e.wait_ge(patched[q], 16 * ET * used(EC, 4, q))

        @block.sync
        def _(e):
            rest = slice(LAST0 + OVER, N)

            def rest_view(t):
                return t[rest, :].rearrange("(p t) d -> p (t d)", t=BT)

            def rows_of(at):
                return slice(LAST0, N) if at(1) is None else node_rows(at(0))

            e.wait_ge(raw_filled, 3)
            for buf, ap, ahead in ((raw[0], src, 0), (raw[1], dst, 0), (raw[2], dst, 1)):
                e.dma_start(buf[0:HT, 0:P], ap[ahead:ahead + HALF].rearrange("(t p) -> t p", p=P))\
                    .then_inc(raw_in, 16)
                full = HALF + (HT - 1) * P
                e.dma_start(buf[0:HT - 1, P:2 * P],
                            ap[HALF + ahead:full + ahead].rearrange("(t p) -> t p", p=P)).then_inc(raw_in, 16)
                e.dma_start(buf[HT - 1:HT, P:P + TAIL - ahead],
                            ap[full + ahead:E].rearrange("(t p) -> t p", t=1)).then_inc(raw_in, 16)

            def border(at):
                return dst[at:at + 1].rearrange("(o p) -> o p", o=1).to_broadcast([D, 1])

            e.dma_start(other_raw[0:D, :], border(HALF)).then_inc(raw_in, 16)
            e.dma_start(other_raw[D:P, :], border(HALF - 1)).then_inc(raw_in, 16)

            def load_node(at):
                ch = at(0)
                wait_past(e, ln_centred[ch.s], ch.k)
                e.dma_start(xb[ch.s][:, :], node_view(x, rows_of(at))).then_inc(x_in[ch.s], 16)

            def store_node(ch, last):
                e.wait_ge(ht_copied, ch.c * 2 + 2)
                e.dma_start(edge_rows(ht_node, ch), hin[ch.s][:, :]).then_inc(ht_out[ch.s], 16)
                if last:
                    e.dma_start(rest_view(agg_tab), zeros[OVERP:P, :]).then_inc(zeroed, 16)
                else:
                    e.dma_start(node_view(agg_tab, node_rows(ch)), zeros).then_inc(zeroed, 16)

            def weights():
                e.wait_ge(const_made, CONSTS)
                for m, w in ((we_blk, w_edge), (wa_blk, w_out[0:D, :]), (wb_blk, w_out[D:2 * D, :])):
                    e.dma_start(m[0:D, 0:D], w).then_inc(weights_in, 16)
                    e.dma_start(m[D:P, D:P], w).then_inc(weights_in, 16)
                e.dma_start(w1_dup[0:D, :], w1).then_inc(weights_in, 16)
                e.dma_start(w1_dup[D:P, :], w1).then_inc(weights_in, 16)
                e.dma_start(w2_sb[:, :], w2).then_inc(weights_in, 16)
                e.dma_start(gamma_c, gamma.rearrange("(p o) -> p o", o=1)).then_inc(weights_in, 16)
                e.dma_start(beta_c, beta.rearrange("(p o) -> p o", o=1)).then_inc(weights_in, 16)
                e.dma_start(bias_f[0].rearrange("p (t d) -> p t d", d=D),
                            b_out.rearrange("(a t d) -> a t d", a=1, t=1).to_broadcast([96, 8, D]))\
                    .then_inc(weights_in, 16)

            def node_io(at):
                if at(0):
                    load_node(at)
                if at(-1) and at(-2) is None:
                    weights()
                if at(-3):
                    store_node(at(-3), last=at(-2) is None)

            run(e, NODES, node_io, lag=3, lead=1)

            def edge_cols(ap, at, n):
                return ap[ds(at, n)].rearrange("(o n) -> o n", o=1).to_broadcast([D, n])

            def attr(at, n):
                return edge_attr[ds(at, n), :].rearrange("(j p) d -> p j d", p=P)

            def load_source(at):
                ch, first, last = at(0), at(-1) is None, at(1) is None
                e.wait_ge(kept[ch.s], (ch.w + 1) * 16)
                e.sem_inc(sync_steps, 1)
                e.wait_ge(ln_centred[ch.s], ch.k)
                e.dma_start(xb[ch.s][:, 0:ET * D], edge_rows(x_src, ch)).then_inc(x_in[ch.s], 16)
                if at(-2):
                    e.wait_ge(ea_turned, ch.c - 1)
                    e.wait_ge(linked_made, ch.c - 1)
                else:
                    e.wait_ge(ht_out[ch.s], 16 * SOURCES.k0[ch.s])
                v = ea[ch.s][:, 0:ET * D].rearrange("p (j a d) -> p j a d", a=2, d=D)
                e.dma_start(v[:, :, 0, :], attr(ch.c * W, W)).then_inc(ea_in[ch.s], 16)
                if last:
                    full, start = (EJ - 1) * P, HALF + (EC - 1) * W
                    e.dma_start(v[:, 0:EJ - 1, 1, :], attr(start, full)).then_inc(ea_in[ch.s], 16)
                    e.dma_start(v[0:TAIL, EJ - 1, 1, :], edge_attr[start + full:E, :]).then_inc(ea_in[ch.s], 16)
                else:
                    e.dma_start(v[:, :, 1, :], attr(ch.c * W + HALF, W)).then_inc(ea_in[ch.s], 16)
                lo = 1 if first else 0
                hi = W + 1 - PADS if last else W + 1
                start = 0 if first else ch.c * W - 1
                e.dma_start(dcol[ch.s][0:D, lo:W + 1], edge_cols(dst, start, W + 1 - lo)).then_inc(dcol_in[ch.s], 16)
                e.dma_start(dcol[ch.s][D:P, lo:hi], edge_cols(dst, start + HALF, hi - lo)).then_inc(dcol_in[ch.s], 16)

            def store_h(ch, rows):
                e.wait_ge(ln_h, ch.g + 1)
                e.dma_start(edge_rows(rows, ch).rearrange("p (j q) -> p j q", q=P),
                            hb[ch.s][:, 0:EJ, 0:P]).then_inc(h_out[ch.s], 16)

            def source_io(at):
                if at(0):
                    load_source(at)
                if at(-2):
                    store_h(at(-2), h_src)

            run(e, SOURCES, source_io, lag=2, lead=1)

            def store_agg(at):
                ch = at(0)
                e.wait_ge(agg_rows, ch.c + 1)
                e.dma_start(edge_rows(agg_dst, ch), reg_m[:, cols(ch)]).then_inc(agg_stored[ch.s], 16)

            run(e, EDGES, store_agg)

            def load_dest(ch):
                e.wait_ge(kept[ch.s], (ch.w + (EC // 2 + 1)) * 16)
                e.sem_inc(sync_steps, 1)
                e.wait_ge(ln_centred[ch.s], ch.k)
                e.dma_start(xb[ch.s][:, 0:ET * D], edge_rows(x_dst, ch)).then_inc(x_in[ch.s], 16)

            def load_dest_agg(ch):
                if isinstance(ch.c, int) and ch.c < 2:
                    e.wait_ge(agg_stored[0], 16 * (EC // 2))
                    e.wait_ge(agg_stored[1], 16 * (EC // 2))
                wait_past(e, v_used[ch.s], ch.w)
                wait_past(e, dest_summed, ch.c - 1)
                e.dma_start(hin[ch.s][:, 0:ET * D], edge_rows(agg_dst, ch)).then_inc(d_in[ch.s], 16)

            def store_dest(ch):
                e.wait_ge(dest_summed, ch.c + 1)
                e.dma_start(edge_rows(h_dst, ch).rearrange("p (j q) -> p j q", q=P),
                            hb[ch.s][:, 0:EJ, 0:P]).then_inc(h_out[ch.s], 16)

            def dest_io(at):
                if at(0):
                    load_dest(at(0))
                if at(-2):
                    store_dest(at(-2))
                if at(0):
                    load_dest_agg(at(0))

            run(e, DESTS, dest_io, lag=2)

            for s in range(2):
                e.wait_ge(ht_out[s], 16 * SOURCES.k0[s])
                e.wait_ge(h_out[s], 16 * EC)
                e.wait_ge(v_used[s], EC // 2)

            def load2_node(at):
                ch = at(0)
                wait_past(e, x1_done, ch.g * 2 - 6)
                e.dma_start(node_h[ch.q], edge_rows(ht_node, ch)).then_inc(node_in[ch.q], 16)
                e.dma_start(node_x[ch.q], node_view(x, rows_of(at))).then_inc(node_in[ch.q], 16)

            def store2_node(ch, last):
                e.wait_ge(fin_done, ch.c * 2 + 2)
                if last:
                    e.dma_start(rest_view(out), node_x1[ch.q][OVERP:P, :]).then_inc(out_stored[ch.q], 16)
                else:
                    e.dma_start(node_view(out, node_rows(ch)), node_x1[ch.q]).then_inc(out_stored[ch.q], 16)

            def node2_io(at):
                if at(0):
                    load2_node(at)
                if at(-4):
                    store2_node(at(-4), last=at(-3) is None)

            run(e, NODES, node2_io, lag=4, lead=1, unroll=4)

            def load2(ch, h, xs):
                early = ch.part is SOURCES and isinstance(ch.c, int) and ch.c < 2
                if early:
                    e.wait_ge(ln_centred[ch.s], DESTS.k0[ch.s] + EC // 2)
                else:
                    e.wait_ge(t_done, (ch.g - BC) * 2 - 2)
                e.dma_start(hin[ch.s][:, 0:W], edge_rows(h, ch)).then_inc(h2_in[ch.s], 16)
                if ch.part is SOURCES:
                    wait_past(e, h_summed, ch.c - 1)
                    e.dma_start(agg_s[ch.s], edge_rows(agg_src, ch)).then_inc(agg2_in[ch.s], 16)
                if not early:
                    e.wait_ge(x1_done, ch.g * 2 - 2)
                e.dma_start(xb[ch.s][:, 0:W], edge_rows(xs, ch)).then_inc(x2_in[ch.s], 16)

            for s in range(2):
                e.wait_ge(kept[s], 16 * 3 * (EC // 2))
            run(e, SOURCES, lambda at: load2(at(0), h_src, x_src))
            run(e, DESTS, lambda at: load2(at(0), h_dst, x_dst))

        @block.tensor
        def _(e):
            e.wait_ge(const_made, CONSTS)
            e.wait_ge(idx_float, 1)
            for n, f in enumerate((flt[0], flt[3], flt[5], flt[4])):
                for a in range(2):
                    mm = e.transpose(psum[:, n, a * HT:(a + 1) * HT], f[0:HT, a * P:(a + 1) * P],
                                     ident[0:HT, 0:HT])
            mm.then_inc(idx_turned, 1)
            e.wait_ge(idx_made, 4)

            def node_products(ch, first):
                e.wait_ge(ln_h, ch.g + 1)
                for j in range(ch.pairs):
                    e.matmul(ps_g[:, 0:P + 1], hb[ch.s][:, j, 0:P], hb[ch.s][:, j, :],
                             start=(first and j == 0), stop=False, skip_group_check=True)
                for u, (j0, n) in enumerate(quads(ch)):
                    wait_past(e, ht_copied, ch.c * 2 + (u - 1))
                    for j in range(j0, j0 + n):
                        mm = e.transpose(ps_t[u][:, (j - j0) * P:(j - j0 + 1) * P], hb[ch.s][:, j, 0:P],
                                         ident[:, :])
                    mm.then_inc(ht_turned, 1)

            def node_step(at):
                node_products(at(0), first=at(-1) is None)

            run(e, NODES, node_step)
            e.wait_ge(weights_in, 16 * WEIGHTS)

            def turn_attrs(ch, last):
                e.wait_ge(ea_in[ch.s], (ch.w + 1) * 32 + (16 if last else 0))
                wait_past(e, ea_copied, ch.c * 2)
                if isinstance(ch.c, int) and ch.c == 0:
                    e.wait_ge(ht_copied, 2 * BC)
                for u, (j0, n) in enumerate(quads(ch)):
                    for j in range(j0, j0 + n):
                        mm = e.transpose(ps_t[u][:, (j - j0) * P:(j - j0 + 1) * P],
                                         ea[ch.s][:, j * P:(j + 1) * P], ident[:, :])
                mm.then_inc(ea_turned, 1)

            def attr_products(ch):
                wait_past(e, msg_made, ch.c)
                for u, (j0, n) in enumerate(quads(ch)):
                    e.wait_ge(ea_copied, ch.c * 2 + (u + 1))
                    e.matmul(ps_z[:, u, 0:n * P], we_blk[:, :], ea_t[ch.s][:, j0 * P:(j0 + n) * P],
                             start=True, stop=False, skip_group_check=True)
                e.wait_ge(ln_h, ch.g + 1)
                for u, (j0, n) in enumerate(quads(ch)):
                    for j in range(j0, j0 + n):
                        mm = e.matmul(ps_z[:, u, (j - j0) * P:(j - j0 + 1) * P], hb[ch.s][:, j, 0:P],
                                      ident[:, :], start=False, stop=(j == j0 + n - 1), skip_group_check=True)
                mm.then_inc(h_used[ch.s], 1)

            def attr_step(at):
                if at(0):
                    turn_attrs(at(0), last=at(1) is None)
                if at(-1):
                    attr_products(at(-1))

            run(e, SOURCES, attr_step, lag=1, lead=1)

            def bring(n, col, how, at):
                e.wait_ge(link_col, n)
                e.matmul(ps_o[:, at:at + col.shape[1]], how[:, :], col, start=True, stop=True).then_inc(link_ps, 1)

            bring(2, run_max, swap, 0)
            bring(4, soft_ends, down, 0)

            def turn_agg(at):
                ch = at(0)
                e.wait_ge(agg_made, ch.c + 1)
                wait_past(e, agg_rows, ch.c - 1)
                for j in range(EJ):
                    mm = e.transpose(ps_agg[ch.s][:, j * P:(j + 1) * P], agg_t[ch.s][:, j * P:(j + 1) * P],
                                     ident[:, :])
                mm.then_inc(agg_turned, 1)

            run(e, EDGES, turn_agg)

            def gram_dest(at):
                ch = at(0)
                e.wait_ge(v_made, ch.c + 1)
                for j in range(EJ):
                    mm = e.matmul(ps_g[:, 0:P + 1], hin[ch.s][:, j * P:(j + 1) * P], vb[ch.s][:, j, :],
                                  start=False, stop=False, skip_group_check=True)
                mm.then_inc(v_used[ch.s], 1)

            run(e, EDGES, gram_dest)

            e.wait_ge(stat, 2)
            e.matmul(ps_w[:, 0:H], gram_sb[:, :], w1_dup[:, :], start=True, stop=True).then_inc(stat_ps, 1)
            e.wait_ge(stat, 3)
            e.matmul(ps_o[:, 0:1], gram_w[:, :], ones_col[:, :], start=True, stop=True).then_inc(stat_ps, 1)
            e.matmul(ps_t[0][:, 0:1], w1_dup[:, :], sum_c, start=True, stop=True).then_inc(stat_ps, 1)
            e.wait_ge(bn_ready, 1)

            def turn_h(ch, u):
                j0, n = quads(ch)[u]
                if ch.part is SOURCES:
                    e.wait_ge(h_summed, ch.c + 1)
                else:
                    e.wait_ge(h2_in[ch.s], (ch.k - SOURCES.k0[ch.s] + 1) * 16)
                wait_past(e, t_copied, (ch.g - BC) * 2 + (u - 1))
                for j in range(j0, j0 + n):
                    mm = e.transpose(ps_t[u][:, (j - j0) * P:(j - j0 + 1) * P],
                                     hin[ch.s][:, j * P:(j + 1) * P], ident[:, :])
                mm.then_inc(t_done, 1)

            def hidden_product(ch, u):
                j0, n = quads(ch)[u]
                if ch.part is NODES:
                    e.wait_ge(node_in[ch.q], (ch.v + 1) * 32)
                    h = node_h[ch.q][:, j0 * P:(j0 + n) * P]
                else:
                    e.wait_ge(t_copied, (ch.g - BC) * 2 + (u + 1))
                    h = ht[u][:, 0:n * P]
                wait_past(e, y_done, ch.g * 2 + u)
                for a in range(2):
                    mm = e.matmul(ps_z[:, a, 0:n * P], w1_dup[a * D:(a + 1) * D, :],
                                  h[a * D:(a + 1) * D, :], start=True, stop=True)
                mm.then_inc(z_done, 1)

            def first_product(ch, u):
                j0, n = quads(ch)[u]
                e.wait_ge(y_done, ch.g * 2 + (u + 1))
                wait_past(e, x1_done, ch.g * 2 + (u if ch.part is DESTS else u - 1))
                for j in range(n):
                    for a in range(2):
                        mm = e.matmul(w_bank(ch, u)[:, (2 * j + a) * D:(2 * j + a + 1) * D],
                                      yb[u][:, (a * 4 + j) * P:(a * 4 + j + 1) * P], w2_sb[:, :],
                                      start=True, stop=True)
                mm.then_inc(w_done, 1)

            def turn_h1(ch, u):
                j0, n = quads(ch)[u]
                e.wait_ge(l_h, ch.g + 1)
                wait_past(e, t1_copied, outs(ch) * 2 + (u - 1))
                for j in range(j0, j0 + n):
                    mm = e.transpose(ps_t1[u][:, (j - j0) * P:(j - j0 + 1) * P], hb[ch.s][:, j, 0:P],
                                     ident[:, :])
                mm.then_inc(t1_done, 1)

            def out_product(ch, u):
                j0, n = quads(ch)[u]
                if ch.part is DESTS:
                    e.wait_ge(mean_made, ch.c + 1)
                e.wait_ge(t1_copied, outs(ch) * 2 + (u + 1))
                wait_past(e, fin_done, outs(ch) * 2 + (u - 1 if ch.part is NODES else u))
                e.matmul(o_bank(ch, u)[:, 0:n * P], ones3[:, :], bias3[:, 0:n * P], start=True, stop=False,
                         skip_group_check=True)
                for j in range(n):
                    o = o_bank(ch, u)[:, j * P:(j + 1) * P]
                    if ch.part is DESTS:
                        e.matmul(o, mean_t[ch.s][:, (j0 + j) * P:(j0 + j + 1) * P], wb_blk[:, :],
                                 start=False, stop=False, skip_group_check=True)
                    mm = e.matmul(o, h1t[u][:, j * P:(j + 1) * P], wa_blk[:, :],
                                  start=False, stop=(j == n - 1), skip_group_check=True)
                mm.then_inc(o_done, 1)

            def turn_source(ch):
                e.wait_ge(l_h, ch.g + 1)
                wait_past(e, n_summed, ch.c)
                for j in range(EJ):
                    mm = e.transpose(ps_t1_flat[:, j * P:(j + 1) * P], hb[ch.s][:, j, 0:P], ident[:, :])
                mm.then_inc(hs_turned, 1)

            def second(at):
                now, ago, old, soon = at(0), at(-1), at(-2), at(1)
                ahead = now and soon and now.part is not NODES
                if now:
                    hidden_product(now, 0)
                if ago:
                    first_product(ago, 1)
                if old and old.part is SOURCES:
                    turn_source(old)
                elif old:
                    turn_h1(old, 0)
                    turn_h1(old, 1)
                if ahead:
                    turn_h(soon, 0)
                if now:
                    hidden_product(now, 1)
                if old and old.part is not SOURCES:
                    out_product(old, 0)
                if ahead:
                    turn_h(soon, 1)
                if now:
                    first_product(now, 0)
                if old and old.part is not SOURCES:
                    out_product(old, 1)

            def turn_first(part):
                for u in range(2):
                    turn_h(Chunk(part, 4, 0, 0), u)

            run(e, NODES, second, lag=2, lead=1, unroll=4)
            e.wait_ge(x1_done, 2 * BC)
            e.wait_ge(fin_done, 2 * BC)
            turn_first(SOURCES)
            run(e, SOURCES, second, lag=2, lead=1, unroll=4)
            bring(6, mean_ends, down, 0)
            turn_first(DESTS)
            run(e, DESTS, second, lag=2, lead=1, unroll=4)

        @block.scalar
        def _(e):
            e.wait_ge(const_made, CONSTS)

            def square(ch):
                e.wait_ge(ln_centred[ch.s], ch.k + 1)
                wait_past(e, ln_ssq, ch.g)
                n = ch.tiles * D
                e.activation(sq[:, 0:n], xc[ch.s][:, 0:n], ACT.Square).then_inc(ln_squared, 1)

            def root(ch):
                e.wait_ge(ln_ssq, ch.g + 1)
                e.activation(st[ch.s][:, 2, 0:ch.tiles], st[ch.s][:, 1, 0:ch.tiles], ACT.Sqrt,
                             bias=norm_eps, scale=1.0 / D).then_inc(ln_std, 1)

            def copy_turned(ch):
                wait_past(e, ht_out[ch.s], ch.w * 16)
                for u, (j0, n) in enumerate(quads(ch)):
                    e.wait_ge(ht_turned, ch.c * 2 + (u + 1))
                    e.activation(hin[ch.s][:, j0 * P:(j0 + n) * P], ps_t[u][:, 0:n * P], ACT.Copy)\
                        .then_inc(ht_copied, 1)

            def copy_attrs(ch):
                e.wait_ge(ea_turned, ch.c + 1)
                wait_past(e, h_used[ch.s], ch.w)
                for u, (j0, n) in enumerate(quads(ch)):
                    e.activation(ea_t[ch.s][:, j0 * P:(j0 + n) * P], ps_t[u][:, 0:n * P], ACT.Copy)\
                        .then_inc(ea_copied, 1)

            def first_nodes(at):
                if at(-1):
                    root(at(-1))
                if at(0):
                    square(at(0))
                if at(-2):
                    copy_turned(at(-2))

            run(e, NODES, first_nodes, lag=2)

            def first_sources(at):
                if at(-1):
                    root(at(-1))
                if at(0):
                    square(at(0))
                    copy_attrs(at(0))

            run(e, SOURCES, first_sources, lag=1)

            def exponent(at):
                ch = at(0)
                e.wait_ge(arg_made, ch.c + 1)
                e.activation(reg_m[:, cols(ch)], reg_m[:, cols(ch)], ACT.Exp).then_inc(exp_made, 1)

            run(e, EDGES, exponent)

            def inverse(ch, ready, region, before, bias):
                e.wait_ge(ready, ch.c + 1)
                wait_past(e, newton_b, ch.c + (before or -1))
                g = inv_place(ch, before)
                e.activation(g, region[:, cols(ch)], ACT.Ln, bias=bias).then_inc(inv_guess, 1)
                e.wait_ge(inv_guess, (ch.c + before) * 2 + 1)
                e.activation(g, g, ACT.Exp, scale=-1.0).then_inc(inv_guess, 1)

            run(e, EDGES, lambda at: inverse(at(0), s_linked, reg_m, 0, soft_eps))

            def first_dests(at):
                if at(-1):
                    root(at(-1))
                if at(0):
                    square(at(0))

            run(e, DESTS, first_dests, lag=1)

            e.wait_ge(stat, 6)
            e.activation(std_c, var_c, ACT.Sqrt, bias=norm_eps).then_inc(stat_std, 1)
            e.wait_ge(bn_ready, 1)

            def copy_h(ch, u):
                n = quads(ch)[u][1]
                e.wait_ge(t_done, (ch.g - BC) * 2 + (u + 1))
                wait_past(e, z_done, ch.g * 2 + (u - 1))
                e.activation(ht[u][:, 0:n * P], ps_t[u][:, 0:n * P], ACT.Copy).then_inc(t_copied, 1)

            def hidden(ch, u):
                n = quads(ch)[u][1]
                e.wait_ge(z_done, ch.g * 2 + (u + 1))
                wait_past(e, w_done, ch.g * 2 + (u - 1))
                e.activation(yb[u][:, :].rearrange("p (a q) -> p a q", a=2)[:, :, 0:n * P],
                             ps_z[:, :, 0:n * P], ACT.Relu, bias=shift_c, scale=scale_c).then_inc(y_done, 1)

            def copy_h1(ch, u):
                n = quads(ch)[u][1]
                e.wait_ge(t1_done, outs(ch) * 2 + (u + 1))
                wait_past(e, o_done, outs(ch) * 2 + (u - 1))
                e.activation(h1t[u][:, 0:n * P], ps_t1[u][:, 0:n * P], ACT.Copy).then_inc(t1_copied, 1)

            def square2(ch):
                n = ch.tiles * D
                e.wait_ge(l_centred, ch.g + 1)
                wait_past(e, l_ssq, ch.g)
                e.activation(sq[:, 0:n], xc[ch.s][:, 0:n], ACT.Square).then_inc(l_squared, 1)

            def root2(ch):
                e.wait_ge(l_ssq, ch.g + 1)
                e.activation(st[ch.s][:, 2, 0:ch.tiles], st[ch.s][:, 1, 0:ch.tiles], ACT.Sqrt,
                             bias=norm_eps, scale=1.0 / D).then_inc(l_std, 1)

            def second(at):
                now, ago, old, soon = at(0), at(-1), at(-2), at(1)
                ahead = now and soon and now.part is not NODES
                if now:
                    hidden(now, 0)
                if old and old.part is not SOURCES:
                    copy_h1(old, 0)
                    copy_h1(old, 1)
                if ahead:
                    copy_h(soon, 0)
                if now and now.part is DESTS:
                    inverse(now, c_linked, reg_a, EC, 0.0)
                if now:
                    hidden(now, 1)
                if ago:
                    square2(ago)
                if ahead:
                    copy_h(soon, 1)
                if ago:
                    root2(ago)

            def copy_first(part):
                for u in range(2):
                    copy_h(Chunk(part, 4, 0, 0), u)

            run(e, NODES, second, lag=2, lead=1, unroll=4)
            copy_first(SOURCES)
            run(e, SOURCES, second, lag=2, lead=1, unroll=4)
            copy_first(DESTS)
            run(e, DESTS, second, lag=2, lead=1, unroll=4)

        @block.vector
        def _(e):
            for n, pad in enumerate((0, N, N)):
                e.memset(raw[n], pad).then_inc(raw_filled, 1)
            e.wait_ge(raw_in, 16 * 11)
            for n in range(3):
                e.tensor_copy(flt[n][0:HT, :], raw[n][0:HT, :]).then_inc(idx_step, 1)
            e.tensor_copy(other_dst, other_raw[:, :]).then_inc(idx_step, 1)
            e.wait_ge(idx_step, 4)
            e.tensor_scalar(flt[3][0:HT, :], flt[1][0:HT, :], float(N - 1), None, ALU.min).then_inc(idx_step, 1)
            e.tensor_tensor(flt[4][0:HT, :], flt[1][0:HT, :], flt[2][0:HT, :], ALU.not_equal)\
                .then_inc(idx_step, 1)
            e.wait_ge(idx_step, 6)
            e.scalar_tensor_tensor(out=flt[5][0:HT, :], in0=flt[1][0:HT, :], scalar=-float(N),
                                   in1=flt[4][0:HT, :], op0=ALU.add, op1=ALU.mult).then_inc(idx_step, 1)
            e.wait_ge(idx_step, 7)
            e.tensor_scalar(flt[5][0:HT, :], flt[5][0:HT, :], float(N), None, ALU.add).then_inc(idx_float, 1)
            e.wait_ge(idx_turned, 1)
            for n, to in enumerate((src_idx, dst_idx, put_idx, seg_end)):
                e.tensor_copy(to[:, :].rearrange("p (j a) -> p a j", a=2),
                              psum[:, n, 0:2 * HT].rearrange("p (a j) -> p a j", a=2)).then_inc(idx_made, 1)

            def row_sum(ch):
                e.wait_ge(x_in[ch.s], (ch.k + 1) * 16)
                e.tensor_reduce(st[ch.s][:, 0, 0:ch.tiles], tile_rows(xb[ch.s], ch), AX.X, ALU.add)\
                    .then_inc(ln_sum, 1)

            def centre(ch):
                e.wait_ge(ln_sum, ch.g + 1)
                e.scalar_tensor_tensor(out=tile_rows(xc[ch.s], ch), in0=spread(ch, 0), scalar=-1.0 / D,
                                       in1=tile_rows(xb[ch.s], ch), op0=ALU.mult, op1=ALU.add)\
                    .then_inc(ln_centred[ch.s], 1)

            def square_sum(ch):
                e.wait_ge(ln_squared, ch.g + 1)
                e.tensor_reduce(st[ch.s][:, 1, 0:ch.tiles], tile_rows(sq, ch), AX.X, ALU.add).then_inc(ln_ssq, 1)

            def invert(ch):
                e.wait_ge(ln_std, ch.g + 1)
                e.reciprocal(st[ch.s][:, 3, 0:ch.tiles], st[ch.s][:, 2, 0:ch.tiles]).then_inc(ln_rstd, 1)

            def invert_last_node(ch):
                e.wait_ge(ln_std, ch.g + 1)
                e.reciprocal(st[ch.s][:, 3, :], st[ch.s][:, 2, :]).then_inc(edges_set, 1)
                e.wait_ge(edges_set, 1)
                e.tensor_scalar(st[ch.s][:, 3, :], st[ch.s][:, 3, :], own_rows[:, :], None, ALU.mult)\
                    .then_inc(ln_rstd, 1)

            def norm(ch):
                e.wait_ge(ln_rstd, ch.g + 1)
                if ch.part is NODES:
                    wait_past(e, ht_turned, ch.c * 2 - 2)
                if ch.part is SOURCES:
                    e.wait_ge(ht_turned, 2 * BC)
                    wait_past(e, h_used[ch.s], ch.w)
                    wait_past(e, h_out[ch.s], ch.w * 16)
                if ch.part is DESTS:
                    e.wait_ge(h_out[ch.s], (ch.w + EC // 2) * 16)
                e.scalar_tensor_tensor(out=hb[ch.s][:, 0:ch.pairs, 0:P], in0=pair_rows(xc[ch.s], ch), scalar=0.0,
                                       in1=spread(ch, 3), op0=ALU.max, op1=ALU.mult).then_inc(ln_h, 1)

            def first_nodes(at):
                now, ago = at(0), at(-1)
                if ago:
                    square_sum(ago)
                if now:
                    row_sum(now)
                if ago and now is None:
                    invert_last_node(ago)
                elif ago:
                    invert(ago)
                if now:
                    centre(now)
                if ago:
                    norm(ago)

            run(e, NODES, first_nodes, lag=1)

            e.wait_ge(weights_in, 16 * WEIGHTS)
            e.wait_ge(const_made, CONSTS)
            low = 0
            for n, row in enumerate((0, 32, 64)):
                part = bias_part
                e.tensor_copy(part[:, :], bias_f[n % 2]).then_inc(bias_made, 1)
                low += 1
                e.wait_ge(bias_made, low)
                e.tensor_copy(bias3[row:row + 1, :], part[row:row + 1, :]).then_inc(bias_made, 1)
                e.tensor_tensor(bias_f[1 - n % 2], bias_f[n % 2], part[:, :], ALU.subtract).then_inc(bias_made, 1)
                low += 2
                e.wait_ge(bias_made, low)

            e.wait_ge(zeroed, 16 * BC)
            e.memset(same[:, HALF:HALF + 1], 0).then_inc(edges_set, 1)

            def before_col(region, ch):
                return region[:, ds(ch.c * W - 1, 1)]

            def masks(ch, first, last):
                d = dcol[ch.s]
                e.wait_ge(dcol_in[ch.s], (ch.w + 1) * 32)
                if first:
                    e.memset(d[:, 0:1], -1).then_inc(edges_set, 1)
                    e.wait_ge(edges_set, 3)
                if last:
                    e.memset(d[D:P, W + 1 - PADS:W + 1], N).then_inc(edges_set, 1)
                    e.wait_ge(edges_set, 4)
                e.tensor_tensor(same[:, cols(ch)], d[:, 1:W + 1], d[:, 0:W], ALU.is_equal).then_inc(same_made, 1)
                e.tensor_scalar(linked[:, cols(ch)], d[:, 1:W + 1], other_dst, None, ALU.is_equal)\
                    .then_inc(linked_made, 1)

            def messages(ch, first):
                e.wait_ge(h_used[ch.s], ch.w + 1)
                e.tensor_scalar(reg_a[:, cols(ch)], ps_z_flat[:, 0:W], 0.0, MSG_EPS, ALU.max, ALU.add)\
                    .then_inc(msg_made, 1)
                e.wait_ge(msg_made, ch.c + 1)
                e.wait_ge(same_made, ch.c + 1)
                if not first:
                    e.wait_ge(run_made, ch.c)
                e.tensor_tensor_scan(reg_m[:, cols(ch)], same[:, cols(ch)], reg_a[:, cols(ch)],
                                     0.0 if first else before_col(reg_m, ch), ALU.mult, ALU.max)\
                    .then_inc(run_made, 1)

            def first_sources(at):
                now, ago, old = at(0), at(-1), at(-2)
                if ago:
                    square_sum(ago)
                if old:
                    messages(old, first=at(-3) is None)
                if now:
                    row_sum(now)
                if ago:
                    invert(ago)
                if now:
                    centre(now)
                if ago:
                    norm(ago)
                    masks(ago, first=old is None, last=now is None)

            run(e, SOURCES, first_sources, lag=2)

            e.wait_ge(run_made, EC)
            e.tensor_tensor_scan(reg_m[:, ::-1], same[:, 1:HALF + 1][:, ::-1], reg_m[:, ::-1], 0.0,
                                 ALU.mult, ALU.max).then_inc(max_made, 1)

            e.wait_ge(max_made, 1)
            e.tensor_copy(run_max[0:D, :], reg_m[0:D, HALF - 1:HALF]).then_inc(link_col, 1)
            e.tensor_copy(run_max[D:P, :], reg_m[D:P, 0:1]).then_inc(link_col, 1)
            e.wait_ge(link_ps, 1)
            e.wait_ge(link_col, 2)
            e.tensor_tensor(tot_max, ps_o[:, 0:1], run_max, ALU.max).then_inc(link_made, 1)
            e.wait_ge(link_made, 1)

            def argument(ch):
                m, a = reg_m[:, cols(ch)], reg_a[:, cols(ch)]
                e.scalar_tensor_tensor(out=m, in0=linked[:, cols(ch)], scalar=tot_max, in1=m,
                                       op0=ALU.mult, op1=ALU.max).then_inc(max_linked, 1)
                e.wait_ge(max_linked, ch.c + 1)
                e.tensor_tensor(m, a, m, ALU.subtract).then_inc(arg_made, 1)

            def sums(ch, first):
                m, a, keep = reg_m[:, cols(ch)], reg_a[:, cols(ch)], same[:, cols(ch)]
                e.wait_ge(exp_made, ch.c + 1)
                e.tensor_tensor(a, a, m, ALU.mult).then_inc(weighted, 1)
                if not first:
                    e.wait_ge(e_summed, ch.c)
                e.tensor_tensor_scan(m, keep, m, 0.0 if first else before_col(reg_m, ch), ALU.mult, ALU.add)\
                    .then_inc(e_summed, 1)
                e.wait_ge(weighted, ch.c + 1)
                if not first:
                    e.wait_ge(a_summed, ch.c)
                e.tensor_tensor_scan(a, keep, a, 0.0 if first else before_col(reg_a, ch), ALU.mult, ALU.add)\
                    .then_inc(a_summed, 1)

            def exponentials(at):
                if at(0):
                    argument(at(0))
                if at(-1):
                    sums(at(-1), first=at(-2) is None)

            run(e, EDGES, exponentials, lag=1)

            def border_sums(ends, carry, n, a_ready, b_ready):
                e.wait_ge(a_ready, EC)
                e.wait_ge(b_ready, EC)
                e.tensor_copy(ends[:, 0:1], reg_m[:, HALF - 1:HALF]).then_inc(link_col, 1)
                e.tensor_copy(ends[:, 1:2], reg_a[:, HALF - 1:HALF]).then_inc(link_col, 1)
                e.wait_ge(link_ps, n)
                e.tensor_copy(carry, ps_o[:, 0:2]).then_inc(link_made, 1)
                e.wait_ge(link_made, n)

            border_sums(soft_ends, soft_carry, 2, e_summed, a_summed)

            def link(ch, region, carry, done):
                r = region[:, cols(ch)]
                e.scalar_tensor_tensor(out=r, in0=linked[:, cols(ch)], scalar=carry, in1=r,
                                       op0=ALU.mult, op1=ALU.add).then_inc(done, 1)

            def newton(ch, region, bias, before):
                g, r = inv_place(ch, before), region[:, cols(ch)]
                e.wait_ge(inv_guess, (ch.c + before) * 2 + 2)
                e.scalar_tensor_tensor(out=r, in0=r, scalar=bias, in1=g, op0=ALU.add, op1=ALU.mult)\
                    .then_inc(newton_a, 1)
                e.wait_ge(newton_a, ch.c + (before + 1))
                e.scalar_tensor_tensor(out=r, in0=r, scalar=-2.0, in1=g, op0=ALU.add, op1=ALU.mult)\
                    .then_inc(newton_b, 1)

            def aggregate(at):
                now, ago, old = at(0), at(-1), at(-2)
                if now:
                    link(now, reg_m, soft_carry[:, 0:1], s_linked)
                    link(now, reg_a, soft_carry[:, 1:2], a_linked)
                if ago:
                    newton(ago, reg_m, SOFTMAX_EPS, 0)
                if old:
                    e.wait_ge(agg_turned, old.c + 1)
                    end = seg_end[:, ds(old.c * ET, ET)].unsqueeze(2).to_broadcast([P, ET, D])
                    e.tensor_tensor(reg_m[:, cols(old)].rearrange("p (t d) -> p t d", d=D),
                                    ps_agg[old.s][:, 0:W].rearrange("p (t d) -> p t d", d=D),
                                    end, ALU.mult).then_inc(agg_rows, 1)
                if ago:
                    e.wait_ge(newton_b, ago.c + 1)
                    e.wait_ge(a_linked, ago.c + 1)
                    e.scalar_tensor_tensor(out=agg_t[ago.s][:, 0:W], in0=reg_m[:, cols(ago)], scalar=-1.0,
                                           in1=reg_a[:, cols(ago)], op0=ALU.mult, op1=ALU.mult)\
                        .then_inc(agg_made, 1)

            run(e, EDGES, aggregate, lag=2)

            for s in range(2):
                e.memset(vb[s][:, :, P:P + 1], 1.0).then_inc(edges_set, 1)

            def gram_input(ch):
                e.wait_ge(ln_h, ch.g + 1)
                e.wait_ge(d_in[ch.s], (ch.w + 1) * 16)
                wait_past(e, v_used[ch.s], ch.w)
                e.wait_ge(edges_set, 6)
                e.scalar_tensor_tensor(out=vb[ch.s][:, :, 0:P], in0=hb[ch.s][:, 0:EJ, 0:P], scalar=2.0,
                                       in1=pair_rows(hin[ch.s], ch), op0=ALU.mult, op1=ALU.add).then_inc(v_made, 1)

            def sum_dest(ch):
                e.wait_ge(v_made, ch.c + 1)
                h = hb[ch.s][:, 0:EJ, 0:P]
                e.tensor_tensor(h, h, pair_rows(hin[ch.s], ch), ALU.add).then_inc(dest_summed, 1)

            def first_dests(at):
                now, ago = at(0), at(-1)
                if ago:
                    square_sum(ago)
                if now:
                    row_sum(now)
                if ago:
                    invert(ago)
                if now:
                    centre(now)
                if ago:
                    norm(ago)
                    gram_input(ago)
                    sum_dest(ago)

            run(e, DESTS, first_dests, lag=1)

            for s in range(2):
                e.wait_ge(v_used[s], EC // 2)
            e.tensor_tensor(gram_sb[:, :], ps_g[:, 0:P], blocks[:, :], ALU.mult).then_inc(stat, 1)
            e.tensor_copy(sum_c, ps_g[:, P:P + 1]).then_inc(stat, 1)
            e.wait_ge(stat_ps, 1)
            e.tensor_tensor(gram_w[:, :], ps_w[:, 0:H], w1_dup[:, :], ALU.mult).then_inc(stat, 1)
            e.wait_ge(stat_ps, 3)
            e.tensor_scalar(ex2_c, ps_o[:, 0:1], 1.0 / N, None, ALU.mult).then_inc(stat, 1)
            e.tensor_scalar(mean_c, ps_t[0][:, 0:1], 1.0 / N, None, ALU.mult).then_inc(stat, 1)
            e.wait_ge(stat, 5)
            e.tensor_tensor(m2_c, mean_c, mean_c, ALU.mult).then_inc(stat_mid, 1)
            e.wait_ge(stat_mid, 1)
            e.tensor_tensor(m2_c, ex2_c, m2_c, ALU.subtract).then_inc(stat_mid, 1)
            e.wait_ge(stat_mid, 2)
            e.tensor_scalar(var_c, m2_c, 0.0, None, ALU.max).then_inc(stat, 1)
            e.wait_ge(stat_std, 1)
            e.reciprocal(rs_c, std_c).then_inc(stat_mid, 1)
            e.wait_ge(stat_mid, 3)
            e.tensor_tensor(scale_c, gamma_c, rs_c, ALU.mult).then_inc(stat_mid, 1)
            e.wait_ge(stat_mid, 4)
            e.tensor_tensor(mscale_c, mean_c, scale_c, ALU.mult).then_inc(stat_mid, 1)
            e.wait_ge(stat_mid, 5)
            e.tensor_tensor(shift_c, beta_c, mscale_c, ALU.subtract).then_inc(bn_ready, 1)

            def add_agg(ch):
                e.wait_ge(h2_in[ch.s], (ch.w + 1) * 16)
                e.wait_ge(agg2_in[ch.s], (ch.w + 1) * 16)
                e.tensor_tensor(hin[ch.s][:, 0:W], hin[ch.s][:, 0:W], agg_s[ch.s], ALU.add).then_inc(h_summed, 1)

            def x1_of(ch):
                if ch.part is NODES:
                    return node_x1[ch.q]
                return (source_x1 if ch.part is SOURCES else dest_x1)[ch.q]

            def first_residual(ch, u):
                j0, n = quads(ch)[u]
                part = slice(j0 * P, (j0 + n) * P)
                if ch.part is NODES:
                    e.wait_ge(node_in[ch.q], (ch.v + 1) * 32)
                    if u == 0:
                        wait_past(e, out_stored[ch.q], ch.v * 16)
                    xs = node_x[ch.q]
                else:
                    e.wait_ge(x2_in[ch.s], (ch.k - SOURCES.k0[ch.s] + 1) * 16)
                    xs = xb[ch.s]
                if ch.part is DESTS and u == 0:
                    wait_past(e, patched[ch.q], ch.v * (16 * ET))
                e.wait_ge(w_done, ch.g * 2 + (u + 1))
                e.tensor_tensor(x1_of(ch)[:, part], w_bank(ch, u)[:, 0:n * P], xs[:, part], ALU.add)\
                    .then_inc(x1_done, 1)

            def centre2(ch):
                e.wait_ge(x1_done, ch.g * 2 + 2)
                e.tensor_reduce(st[ch.s][:, 0, 0:ch.tiles], tile_rows(x1_of(ch), ch), AX.X, ALU.add)\
                    .then_inc(l_sum, 1)
                e.wait_ge(l_sum, ch.g + 1)
                e.scalar_tensor_tensor(out=tile_rows(xc[ch.s], ch), in0=spread(ch, 0), scalar=-1.0 / D,
                                       in1=tile_rows(x1_of(ch), ch), op0=ALU.mult, op1=ALU.add)\
                    .then_inc(l_centred, 1)

            def square_sum2(ch):
                e.wait_ge(l_squared, ch.g + 1)
                e.tensor_reduce(st[ch.s][:, 1, 0:ch.tiles], tile_rows(sq, ch), AX.X, ALU.add).then_inc(l_ssq, 1)

            def norm2(ch):
                e.wait_ge(l_std, ch.g + 1)
                e.reciprocal(st[ch.s][:, 3, 0:ch.tiles], st[ch.s][:, 2, 0:ch.tiles]).then_inc(l_rstd, 1)
                e.wait_ge(l_rstd, ch.g + 1)
                if ch.part is SOURCES:
                    wait_past(e, hs_turned, ch.c - 1)
                else:
                    wait_past(e, t1_done, outs(ch) * 2 - 2)
                e.scalar_tensor_tensor(out=hb[ch.s][:, 0:ch.pairs, 0:P], in0=pair_rows(xc[ch.s], ch), scalar=0.0,
                                       in1=spread(ch, 3), op0=ALU.max, op1=ALU.mult).then_inc(l_h, 1)

            def final(ch, u):
                j0, n = quads(ch)[u]
                part = slice(j0 * P, (j0 + n) * P)
                e.wait_ge(o_done, outs(ch) * 2 + (u + 1))
                e.scalar_tensor_tensor(out=x1_of(ch)[:, part], in0=o_bank(ch, u)[:, 0:n * P], scalar=0.0,
                                       in1=x1_of(ch)[:, part], op0=ALU.max, op1=ALU.add).then_inc(fin_done, 1)

            def neighbours(ch, first):
                e.wait_ge(hs_turned, ch.c + 1)
                if first:
                    for q in range(4):
                        e.wait_ge(out_stored[q], 16 * used(BC, 4, q))
                else:
                    e.wait_ge(n_summed, ch.c)
                    e.wait_ge(c_summed, ch.c)
                e.tensor_tensor_scan(reg_m[:, cols(ch)], same[:, cols(ch)], ps_t1_flat[:, 0:W],
                                     0.0 if first else before_col(reg_m, ch), ALU.mult, ALU.add).then_inc(n_summed, 1)
                e.tensor_tensor_scan(reg_a[:, cols(ch)], same[:, cols(ch)], ones_row[:, :],
                                     0.0 if first else before_col(reg_a, ch), ALU.mult, ALU.add).then_inc(c_summed, 1)

            def mean(ch):
                e.wait_ge(newton_b, ch.c + (EC + 1))
                e.wait_ge(n_linked, ch.c + 1)
                e.scalar_tensor_tensor(out=mean_t[ch.s][:, 0:W], in0=reg_a[:, cols(ch)], scalar=-1.0,
                                       in1=reg_m[:, cols(ch)], op0=ALU.mult, op1=ALU.mult).then_inc(mean_made, 1)

            def second(at):
                now, ago, old, soon = at(0), at(-1), at(-2), at(1)
                if now and soon and now.part is SOURCES:
                    add_agg(soon)
                if now and now.part is DESTS:
                    link(now, reg_a, mean_carry[:, 1:2], c_linked)
                if ago and ago.part is DESTS:
                    newton(ago, reg_a, 0.0, EC)
                if ago:
                    first_residual(ago, 1)
                    centre2(ago)
                if old and old.part is SOURCES:
                    neighbours(old, first=at(-3) is None)
                elif old:
                    final(old, 0)
                if ago:
                    square_sum2(ago)
                if now:
                    first_residual(now, 0)
                if ago:
                    norm2(ago)
                if old and old.part is not SOURCES:
                    final(old, 1)
                if ago and ago.part is DESTS:
                    link(ago, reg_m, mean_carry[:, 0:1], n_linked)
                    mean(ago)

            run(e, NODES, second, lag=2, lead=1, unroll=4)

            add_agg(Chunk(SOURCES, 4, 0, 0))
            run(e, SOURCES, second, lag=2, lead=1, unroll=4)

            border_sums(mean_ends, mean_carry, 3, n_summed, c_summed)

            run(e, DESTS, second, lag=2, lead=1, unroll=4)


_INS = ["x", "src", "dst", "edge_attr_64", "L0_gnn_W_edge", "L0_gnn_W1", "L0_gnn_gamma", "L0_gnn_beta",
        "L0_gnn_W2", "L1_gnn_W", "L1_gnn_b"]


def kernel(**inputs):
    import concourse.bacc as _bacc
    from concourse.bass_utils import run_bass_kernel_spmd as _run

    nc = _bacc.Bacc("TRN2", target_bir_lowering=False, num_devices=1)
    arrays, args = {}, []
    for name in _INS:
        a = np.ascontiguousarray(inputs[name])
        arrays[f"in_{name}_dram"] = a
        args.append(nc.dram_tensor(f"in_{name}_dram", a.shape, mybir.dt.from_np(a.dtype), kind="ExternalInput").ap())
    args.append(nc.dram_tensor("out_0_dram", inputs["x"].shape, F32, kind="ExternalOutput").ap())
    build(nc, *args)
    r = _run(nc, [arrays], core_ids=[0])
    return r.results[0]["out_0_dram"]
```

```python
from contextlib import ExitStack

import numpy as np

import concourse.bass as bass
from concourse import mybir

F32 = mybir.dt.float32
BF16 = mybir.dt.bfloat16
I32 = mybir.dt.int32
U8 = mybir.dt.uint8
ALU = mybir.AluOpType
ACT = mybir.ActivationFunctionType
AX = mybir.AxisListType

P = 128
LN_EPS = 1e-5
BN_EPS = 1e-5
MSG_EPS = 1e-7
SOFTMAX_EPS = 1e-16


def ds(start, size):
    return bass.ds(start, size)


class Part:

    def __init__(self, n, g0, k0, tiles):
        self.n, self.g0, self.k0, self.tiles = n, g0, k0, tiles

    def after(self, n, tiles):
        return Part(n, self.g0 + self.n, (self.k0[0] + (self.n + 1) // 2, self.k0[1] + self.n // 2), tiles)


class Chunk:

    def __init__(self, part, unroll, i, u):
        self.part, self.tiles, self.pairs = part, part.tiles, part.tiles // 2
        self.c = i * unroll + u
        self.g = self.c + part.g0
        self.s = u % 2
        self.w = i * (unroll // 2) + u // 2
        self.k = self.w + part.k0[self.s]
        self.q = u % 4
        self.v = i * (unroll // 4) + u // 4


def run(e, part, step, lag=0, lead=0, unroll=2, before=None, after=None):
    first = 4 if unroll == 4 else 2 + (lag + 1) // 2 * 2
    rounds = max(0, (part.n - lead - first) // unroll)

    def alone(c):
        def at(d):
            if before and c + d < 0:
                return Chunk(before, unroll, 0, before.n + c + d)
            if after and c + d >= part.n:
                return Chunk(after, unroll, 0, c + d - part.n)
            if not 0 <= c + d < part.n:
                return None
            return Chunk(part, unroll, 0, c + d)
        step(at)

    for c in range(first):
        alone(c)
    with e.Fori(0, rounds) as i:
        for u in range(unroll):
            step(lambda d, u=u: Chunk(part, unroll, i, first + u + d))
    for c in range(first + rounds * unroll, part.n + lag):
        alone(c)


def build(nc, x, src, dst, edge_attr, w_edge, w1, gamma, beta, w2, w_out, b_out, out):
    N, D = x.shape
    E = src.shape[0]
    H = w1.shape[1]
    assert D == 64 and H == P

    BT = 16
    BROWS = BT * P
    BC = -(-N // BROWS)
    LAST0 = N - BROWS
    OVER = BC * BROWS - N
    assert OVER % BT == 0 and BC % 2 == 1
    OVERP = OVER // BT

    EJ = 7
    HT = -(-E // (2 * P * EJ)) * EJ
    HALF = HT * P
    ET = 2 * EJ
    EC = HT // EJ
    assert EC % 2 == 0
    W = EJ * P
    PADS = 2 * HALF - E
    assert 0 < PADS < P - 1
    TAIL = P - PADS

    NODES = Part(BC, 0, (0, 0), BT)
    SOURCES = NODES.after(EC, ET)
    DESTS = SOURCES.after(EC, ET)
    EDGES = Part(EC, 0, (0, 0), ET)

    NO_AGG = EC * P * ET
    pos_tab = nc.dram_tensor("pos_tab", [N, 1], I32, kind="Internal").ap()
    ht_node = nc.dram_tensor("ht_node", [BC * P, BT * D], F32, kind="Internal").ap()
    x_src, x_dst, h_src, h_dst, agg_src = (
        nc.dram_tensor(n, [EC * P, ET * D], F32, kind="Internal").ap()
        for n in ("x_src", "x_dst", "h_src", "h_dst", "agg_src"))
    agg_all = nc.dram_tensor("agg_all", [NO_AGG + 1, D], F32, kind="Internal").ap()
    agg_dst = agg_all[0:NO_AGG, :].rearrange("(r t) d -> r (t d)", t=ET)

    with ExitStack() as ctx:
        def sb(name, shape, dt=F32):
            return ctx.enter_context(nc.sbuf_tensor(name, shape, dt))

        def sem(name):
            return ctx.enter_context(nc.semaphore(name))

        def sem2(name):
            return [sem(f"{name}_{s}") for s in range(2)]

        def sem4(name):
            return [sem(f"{name}_{q}") for q in range(4)]

        ident = sb("ident", [P, P])
        swap = sb("swap", [P, P])
        down = sb("down", [P, P])
        blocks = sb("blocks", [P, P])
        ones_col = sb("ones_col", [P, 1])
        own_rows = sb("own_rows", [P, 1])
        ones_row = sb("ones_row", [P, W], BF16)
        ones3 = sb("ones3", [96, P], BF16)
        bias3 = sb("bias3", [96, 8 * D], BF16)
        we_blk = sb("we_blk", [P, P])
        wa_blk = sb("wa_blk", [P, P])
        wb_blk = sb("wb_blk", [P, P])
        w1_dup = sb("w1_dup", [P, H])
        w2_sb = sb("w2_sb", [H, D])
        vecs = sb("vecs", [P, 16])
        (gamma_c, beta_c, mean_c, ex2_c, m2_c, var_c, std_c, rs_c, scale_c, mscale_c, shift_c, sum_c,
         norm_eps, soft_eps) = (vecs[:, n:n + 1] for n in range(14))
        gram_sb = sb("gram_sb", [P, P])
        gram_w = sb("gram_w", [P, H])
        links = sb("links", [P, 16])
        run_max, tot_max, other_dst = (links[:, n:n + 1] for n in range(3))
        soft_ends, soft_carry, mean_ends, mean_carry = (links[:, n:n + 2] for n in (4, 6, 8, 10))

        src_idx = sb("src_idx", [P, HT * 2], I32)
        dst_idx = sb("dst_idx", [P, HT * 2], I32)
        put_idx = sb("put_idx", [P, HT * 2], I32)
        seg_end = sb("seg_end", [P, HT * 2])
        other_raw = sb("other_raw", [P, 1], I32)
        stage_idx = [sb(f"stage_idx{s}", [P, ET], I32) for s in range(2)]

        edge_row = sb("edge_row", [P, HT * 2], I32)
        row_stage, pos_stage = ([sb(f"{n}{s}", [P, ET], I32) for s in range(2)]
                                for n in ("row_stage", "pos_stage"))

        reg_m = sb("reg_m", [P, HALF])
        reg_a = sb("reg_a", [P, HALF])
        same = sb("same", [P, HALF + 4], U8)
        linked = sb("linked", [P, HALF], U8)

        xb = [sb(f"xb{s}", [P, BT * D]) for s in range(2)]
        xc = [sb(f"xc{s}", [P, BT * D]) for s in range(2)]
        sq = sb("sq", [P, BT * D])
        hb = [sb(f"hb{s}", [P, BT // 2, P + 1]) for s in range(2)]
        hin = [sb(f"hin{s}", [P, BT * D]) for s in range(2)]
        x1b = [sb(f"x1b{s}", [P, BT * D]) for s in range(2)]
        ht = [sb(f"ht{u}", [P, 4 * P]) for u in range(2)]
        yb = [sb(f"yb{u}", [P, 2 * 4 * P]) for u in range(2)]
        h1t = [sb(f"h1t{u}", [P, 4 * P]) for u in range(2)]
        gb = [sb(f"gb{s}", [P, ET * D]) for s in range(2)]
        st = [sb(f"st{s}", [P, 4, BT]) for s in range(2)]

        bias_part = sb("bias_part", [96, 8 * D], BF16)

        ea = hin
        ea_t = yb
        dcol = [x1b[s][:, 0:W + 1].bitcast(I32) for s in range(2)]
        vb = [x1b[s][:, 0:EJ * (P + 1)].rearrange("p (j q) -> p j q", q=P + 1) for s in range(2)]
        agg_t = yb
        mean_t = gb
        raw = [reg_m[:, n * 2 * P:(n + 1) * 2 * P].bitcast(I32) for n in range(3)]
        flt = [reg_m[:, (n + 3) * 2 * P:(n + 4) * 2 * P] for n in range(6)]
        bias_f = [reg_m[0:96, (n + 9) * 2 * P:(n + 9) * 2 * P + 8 * D] for n in (0, 2, 4)]
        NP = N // P
        no_agg = reg_a[:, 0:NP + 1].bitcast(I32)
        zero_row = reg_a[0:1, BT * D:BT * D + D]
        first_x = [reg_a[:, (n + 2) * BT * D:(n + 3) * BT * D] for n in range(4)]
        first_t = [reg_m[:, (n + 3) * BT * D:(n + 4) * BT * D] for n in range(2)]
        node_h, node_x, node_x1 = ([reg_a[:, n * BT * D:(n + 1) * BT * D] for n in range(m, m + 4)]
                                   for m in (0, 4, 8))
        agg_s = [gb[s][:, :] for s in range(2)]
        spare = [same[:, n * 4 * W:(n + 1) * 4 * W].bitcast(F32) for n in range(3)]
        source_x1 = [x1b[s][:, 0:W] for s in (0, 1, 0, 1)]
        dest_x1 = [x1b[0][:, 0:W], x1b[1][:, 0:W], spare[0], spare[1]]
        count_guess = spare[2]

        psum = ctx.enter_context(nc.psum_tensor("psum", [P, 8, 512], F32))
        ps_t = [psum[:, 0, :], psum[:, 1, :]]
        ps_t_flat = psum[:, 0:2, :].rearrange("p a b -> p (a b)")
        ps_z = psum[:, 2:4, :]
        ps_z_flat = psum[:, 2:4, :].rearrange("p a b -> p (a b)")
        ps_w = psum[:, 4, :]
        ps_o = psum[:, 5, :]
        ps_t1 = [psum[:, 6, :], psum[:, 7, :]]
        ps_t1_flat = psum[:, 6:8, :].rearrange("p a b -> p (a b)")
        ps_agg = [ps_z_flat, ps_t_flat]
        ps_g = psum[:, 7, :]

        const_made, raw_filled, raw_in, idx_float, idx_step, idx_turned, idx_made = \
            (sem(n) for n in ("const_made", "raw_filled", "raw_in", "idx_float", "idx_step", "idx_turned",
                              "idx_made"))
        weights_in, bias_made, pos_set, staged = \
            (sem(n) for n in ("weights_in", "bias_made", "pos_set", "staged"))
        gathered, kept = sem2("gathered"), sem2("kept")
        pool_steps, sync_steps = sem("pool_steps"), sem("sync_steps")
        x_in, ln_centred, h_used, h_out, ht_out = \
            (sem2(n) for n in ("x_in", "ln_centred", "h_used", "h_out", "ht_out"))
        ln_sum, ln_squared, ln_ssq, ln_std, ln_rstd, ln_h, ht_turned, ht_copied = \
            (sem(n) for n in ("ln_sum", "ln_squared", "ln_ssq", "ln_std", "ln_rstd", "ln_h", "ht_turned",
                              "ht_copied"))
        ea_in, dcol_in, d_in, v_used = (sem2(n) for n in ("ea_in", "dcol_in", "d_in", "v_used"))
        ea_turned, ea_copied, same_made, linked_made, msg_made, run_made, edges_set, v_made = \
            (sem(n) for n in ("ea_turned", "ea_copied", "same_made", "linked_made", "msg_made", "run_made",
                              "edges_set", "v_made"))
        max_made, link_col, link_ps, link_made, max_linked, arg_made, exp_made, weighted, e_summed, a_summed = \
            (sem(n) for n in ("max_made", "link_col", "link_ps", "link_made", "max_linked", "arg_made",
                              "exp_made", "weighted", "e_summed", "a_summed"))
        s_linked, a_linked, inv_guess, newton_a, newton_b, agg_made, agg_turned, agg_rows = \
            (sem(n) for n in ("s_linked", "a_linked", "inv_guess", "newton_a", "newton_b", "agg_made",
                              "agg_turned", "agg_rows"))
        agg_stored = sem2("agg_stored")
        row_staged, pos_moved = sem("row_staged"), sem("pos_moved")
        pos_put, pos_got = sem2("pos_put"), sem2("pos_got")
        stat, stat_mid, stat_ps, stat_std, bn_ready = \
            (sem(n) for n in ("stat", "stat_mid", "stat_ps", "stat_std", "bn_ready"))
        dest_summed, agg2_in = sem("dest_summed"), sem2("agg2_in")
        first_in, bias_in = sem4("first_in"), sem("bias_in")
        node_in, out_stored, patched = sem4("node_in"), sem4("out_stored"), sem4("patched")
        h2_in, x2_in = sem2("h2_in"), sem2("x2_in")
        h_summed, t_done, t_copied, z_done, y_done, w_done, x1_done = \
            (sem(n) for n in ("h_summed", "t_done", "t_copied", "z_done", "y_done", "w_done", "x1_done"))
        l_sum, l_centred, l_squared, l_ssq, l_std, l_rstd, l_h = \
            (sem(n) for n in ("l_sum", "l_centred", "l_squared", "l_ssq", "l_std", "l_rstd", "l_h"))
        t1_done, t1_copied, o_done, fin_done, hs_turned = \
            (sem(n) for n in ("t1_done", "t1_copied", "o_done", "fin_done", "hs_turned"))
        n_summed, c_summed, n_linked, c_linked, mean_made = \
            (sem(n) for n in ("n_summed", "c_summed", "n_linked", "c_linked", "mean_made"))

        block = ctx.enter_context(nc.Block())

        CONSTS = 26
        WEIGHTS = 11
        STAGED = (0, EC, 4 * EC)

        def used(chunks, slots, s):
            return (chunks - s + slots - 1) // slots

        def wait_past(e, which, value):
            if not (isinstance(value, int) and value <= 0):
                e.wait_ge(which, value)

        def inv_place(ch, before):
            return count_guess if before else xc[ch.s][:, 0:W]

        def cols(ch):
            return ds(ch.c * W, W)

        def node_view(t, rows):
            return t[rows, :].rearrange("(p t) d -> p (t d)", p=P)

        def node_rows(ch):
            return ds(ch.c * BROWS, BROWS)

        def edge_rows(t, ch):
            return t[ds(ch.c * P, P), :]

        def tile_rows(buf, ch):
            return buf[:, 0:ch.tiles * D].rearrange("p (t d) -> p t d", d=D)

        def pair_rows(buf, ch):
            return buf[:, 0:ch.tiles * D].rearrange("p (j q) -> p j q", q=2 * D)

        def spread(ch, row):
            return st[ch.s][:, row, 0:ch.tiles].unsqueeze(2).to_broadcast([P, ch.tiles, D])

        def quads(ch):
            return ((0, 4), (4, ch.pairs - 4))

        def outs(ch):
            return ch.c if ch.part is NODES else ch.c + BC

        def act_tiles(ch):
            return 8 if ch.part is NODES else 0

        def linked_late(ch):
            return ch.part is DESTS and isinstance(ch.c, int) and ch.c == 2

        def counts_in_turn(ch):
            return ch.part is DESTS and not (isinstance(ch.c, int) and ch.c < 2)

        def w_bank(ch, u):
            if u == 1 and ch.part is not DESTS:
                return ps_t[0] if ch.part is NODES else ps_o
            return ps_w

        def o_bank(ch, u):
            return ps_t[1] if ch.part is NODES and u == 1 else ps_o

        @block.gpsimd
        def _(e):
            made = 0

            def note(ins):
                nonlocal made
                ins.then_inc(const_made, 1)
                made += 1

            def diagonal(ap, base):
                e.wait_ge(const_made, made)
                note(e.affine_select(out=ap, in_=ap, compare_op=ALU.not_equal, fill=1.0, base=base,
                                     pattern=[[-1, P]], channel_multiplier=1))

            for m in (ident, swap, down, blocks, bias3, we_blk, wa_blk, wb_blk):
                note(e.memset(m[:, :], 0.0))
            for m in (ones_col, own_rows, ones_row, ones3):
                note(e.memset(m[:, :], 1.0))
            for m in hb:
                note(e.memset(m[:, :, P:P + 1], 1.0))
            note(e.memset(norm_eps, LN_EPS))
            note(e.memset(soft_eps, SOFTMAX_EPS))
            note(e.memset(no_agg, NO_AGG))
            note(e.memset(zero_row, 0.0))
            note(e.iota(edge_row[:, :], pattern=[[P * ET, EC], [1, ET]], base=0, channel_multiplier=ET))
            diagonal(ident[:, :], 0)
            diagonal(swap[:, :], D)
            diagonal(swap[:, :], -D)
            diagonal(down[:, :], D)
            for half in (slice(0, D), slice(D, P)):
                e.wait_ge(const_made, made)
                note(e.memset(blocks[half, half], 1.0))
            e.wait_ge(const_made, made)
            note(e.affine_select(out=own_rows[:, :], in_=own_rows[:, :], compare_op=ALU.is_ge, fill=0.0,
                                 base=-OVERP, pattern=[[0, 1]], channel_multiplier=1))
            assert made == CONSTS

            def stage(idx, ch, before):
                e.tensor_copy(stage_idx[ch.s][:, :], idx[:, ds(ch.c * ET, ET)]).then_inc(staged, 1)
                e.wait_ge(staged, ch.c + (before + 1))
                e.sem_inc(pool_steps, 1)

            def gather(table, idx, rows, turn):
                part = Part(EC, 0, (turn * EC // 2, turn * EC // 2), ET)

                def get(ch, tiles):
                    for t in tiles:
                        e.indirect_dma_start(
                            gb[ch.s][:, t * D:(t + 1) * D], None, table,
                            bass.IndirectOffsetOnAxis(ap=stage_idx[ch.s][:, t:t + 1], axis=0),
                        ).then_inc(gathered[ch.s], 16)

                def keep(ch):
                    e.wait_ge(gathered[ch.s], (ch.k + 1) * (16 * ET))
                    e.dma_start(edge_rows(rows, ch), gb[ch.s][:, :]).then_inc(kept[ch.s], 16)

                def get_and_keep(at):
                    ch = at(0)
                    if ch:
                        wait_past(e, kept[ch.s], ch.k * 16)
                        stage(idx, ch, STAGED[turn])
                        get(ch, range(0, ET // 2))
                    if at(-1):
                        keep(at(-1))
                    if ch:
                        get(ch, range(ET // 2, ET))

                run(e, part, get_and_keep, lag=1)

            e.wait_ge(idx_made, 4)
            gather(x, src_idx, x_src, 0)
            gather(x, dst_idx, x_dst, 1)

            e.wait_ge(pos_set, 16 * 3)

            def put_row(at):
                ch = at(0)
                wait_past(e, pos_put[ch.s], ch.w * (16 * ET))
                e.sem_inc(pool_steps, 1)
                e.tensor_copy(row_stage[ch.s][:, :], edge_row[:, ds(ch.c * ET, ET)]).then_inc(row_staged, 1)
                stage(put_idx, ch, 2 * EC)
                e.wait_ge(row_staged, ch.c + 1)
                e.sem_inc(pool_steps, 1)
                for t in range(ET):
                    e.indirect_dma_start(
                        pos_tab, bass.IndirectOffsetOnAxis(ap=stage_idx[ch.s][:, t:t + 1], axis=0),
                        row_stage[ch.s][:, t:t + 1], None, bounds_check=N - 1, oob_is_err=False,
                    ).then_inc(pos_put[ch.s], 16)

            run(e, EDGES, put_row)
            for s in range(2):
                e.wait_ge(pos_put[s], 16 * ET * (EC // 2))

            def get_rows(at):
                if at(0):
                    ch = at(0)
                    stage(src_idx, ch, 3 * EC)
                    for t in range(ET):
                        e.indirect_dma_start(
                            pos_stage[ch.s][:, t:t + 1], None, pos_tab,
                            bass.IndirectOffsetOnAxis(ap=stage_idx[ch.s][:, t:t + 1], axis=0),
                        ).then_inc(pos_got[ch.s], 16)
                if at(-1):
                    ch = at(-1)
                    e.wait_ge(pos_got[ch.s], (ch.w + 1) * (16 * ET))
                    e.sem_inc(pool_steps, 1)
                    e.tensor_copy(src_idx[:, ds(ch.c * ET, ET)], pos_stage[ch.s][:, :]).then_inc(pos_moved, 1)

            run(e, EDGES, get_rows, lag=1)

            e.wait_ge(pos_moved, EC)
            for s in range(2):
                e.wait_ge(agg_stored[s], 16 * (EC // 2))
            gather(agg_all, src_idx, agg_src, 2)

            for q in range(4):
                e.wait_ge(out_stored[q], 16 * used(BC, 4, q))

            def put_out(at):
                ch = at(0)
                e.wait_ge(fin_done, ch.c * 2 + 2 * BC + 1)
                if at(-2):
                    e.wait_ge(patched[at(-2).q], (at(-2).v + 1) * (16 * ET))
                stage(put_idx, ch, 5 * EC)
                for t in range(ET):
                    if t == 8:
                        e.wait_ge(fin_done, ch.c * 2 + 2 * (BC + 1))
                        e.sem_inc(pool_steps, 1)
                    e.indirect_dma_start(
                        out, bass.IndirectOffsetOnAxis(ap=stage_idx[ch.s][:, t:t + 1], axis=0),
                        dest_x1[ch.q][:, t * D:(t + 1) * D], None, bounds_check=N - 1, oob_is_err=False,
                    ).then_inc(patched[ch.q], 16)

            run(e, EDGES, put_out, unroll=4)
            for q in range(4):
                e.wait_ge(patched[q], 16 * ET * used(EC, 4, q))

        @block.sync
        def _(e):
            rest = slice(LAST0 + OVER, N)

            def rest_view(t):
                return t[rest, :].rearrange("(p t) d -> p (t d)", t=BT)

            def rows_of(at):
                return slice(LAST0, N) if at(1) is None else node_rows(at(0))

            e.wait_ge(raw_filled, 3)
            for buf, ap, ahead in ((raw[0], src, 0), (raw[1], dst, 0), (raw[2], dst, 1)):
                e.dma_start(buf[0:HT, 0:P], ap[ahead:ahead + HALF].rearrange("(t p) -> t p", p=P))\
                    .then_inc(raw_in, 16)
                full = HALF + (HT - 1) * P
                e.dma_start(buf[0:HT - 1, P:2 * P],
                            ap[HALF + ahead:full + ahead].rearrange("(t p) -> t p", p=P)).then_inc(raw_in, 16)
                e.dma_start(buf[HT - 1:HT, P:P + TAIL - ahead],
                            ap[full + ahead:E].rearrange("(t p) -> t p", t=1)).then_inc(raw_in, 16)

            def border(at):
                return dst[at:at + 1].rearrange("(o p) -> o p", o=1).to_broadcast([D, 1])

            e.dma_start(other_raw[0:D, :], border(HALF)).then_inc(raw_in, 16)
            e.dma_start(other_raw[D:P, :], border(HALF - 1)).then_inc(raw_in, 16)

            def load_node(at):
                ch = at(0)
                wait_past(e, ln_centred[ch.s], ch.k - 1)
                e.dma_start(first_x[ch.q], node_view(x, rows_of(at))).then_inc(first_in[ch.q], 16)

            def store_node(ch):
                e.wait_ge(ht_copied, ch.c * 2 + 2)
                e.dma_start(edge_rows(ht_node, ch), first_t[ch.s]).then_inc(ht_out[ch.s], 16)

            def weights():
                e.wait_ge(const_made, CONSTS)
                e.dma_start(pos_tab[0:NP * P, :].rearrange("(p t) o -> p (t o)", p=P), no_agg[:, 0:NP])\
                    .then_inc(pos_set, 16)
                e.dma_start(pos_tab[NP * P:N, :], no_agg[0:N - NP * P, 0:1]).then_inc(pos_set, 16)
                e.dma_start(agg_all[NO_AGG:NO_AGG + 1, :], zero_row).then_inc(pos_set, 16)
                for m, w in ((we_blk, w_edge), (wa_blk, w_out[0:D, :]), (wb_blk, w_out[D:2 * D, :])):
                    e.dma_start(m[0:D, 0:D], w).then_inc(weights_in, 16)
                    e.dma_start(m[D:P, D:P], w).then_inc(weights_in, 16)
                e.dma_start(w1_dup[0:D, :], w1).then_inc(weights_in, 16)
                e.dma_start(w1_dup[D:P, :], w1).then_inc(weights_in, 16)
                e.dma_start(w2_sb[:, :], w2).then_inc(weights_in, 16)
                e.dma_start(gamma_c, gamma.rearrange("(p o) -> p o", o=1)).then_inc(weights_in, 16)
                e.dma_start(beta_c, beta.rearrange("(p o) -> p o", o=1)).then_inc(weights_in, 16)

            def edge_cols(ap, at, n):
                return ap[ds(at, n)].rearrange("(o n) -> o n", o=1).to_broadcast([D, n])

            def attr(at, n):
                return edge_attr[ds(at, n), :].rearrange("(j p) d -> p j d", p=P)

            def early(ch):
                return isinstance(ch.c, int) and ch.c < 2

            def load_source_x(ch):
                e.wait_ge(kept[ch.s], (ch.w + 1) * 16)
                if not early(ch):
                    e.sem_inc(sync_steps, 1)
                    e.wait_ge(ln_centred[ch.s], ch.k)
                e.dma_start(xb[ch.s][:, 0:ET * D], edge_rows(x_src, ch)).then_inc(x_in[ch.s], 16)

            def load_attrs(ch, last):
                if not early(ch):
                    e.wait_ge(ea_turned, ch.c - 1)
                v = ea[ch.s][:, 0:ET * D].rearrange("p (j a d) -> p j a d", a=2, d=D)
                e.dma_start(v[:, :, 0, :], attr(ch.c * W, W)).then_inc(ea_in[ch.s], 16)
                if last:
                    full, start = (EJ - 1) * P, HALF + (EC - 1) * W
                    e.dma_start(v[:, 0:EJ - 1, 1, :], attr(start, full)).then_inc(ea_in[ch.s], 16)
                    e.dma_start(v[0:TAIL, EJ - 1, 1, :], edge_attr[start + full:E, :]).then_inc(ea_in[ch.s], 16)
                else:
                    e.dma_start(v[:, :, 1, :], attr(ch.c * W + HALF, W)).then_inc(ea_in[ch.s], 16)

            def load_dst(ch, first, last):
                if not early(ch):
                    e.wait_ge(linked_made, ch.c - 1)
                lo = 1 if first else 0
                hi = W + 1 - PADS if last else W + 1
                start = 0 if first else ch.c * W - 1
                e.dma_start(dcol[ch.s][0:D, lo:W + 1], edge_cols(dst, start, W + 1 - lo)).then_inc(dcol_in[ch.s], 16)
                e.dma_start(dcol[ch.s][D:P, lo:hi], edge_cols(dst, start + HALF, hi - lo)).then_inc(dcol_in[ch.s], 16)

            def node_io(at):
                if at(0):
                    load_node(at)
                if at(-1) and at(-2) is None:
                    weights()
                if at(-4):
                    store_node(at(-4))
                if at(-1) and at(0) is None:
                    for c in range(2):
                        load_source_x(Chunk(SOURCES, 2, 0, c))
                        load_attrs(Chunk(SOURCES, 2, 0, c), last=False)
                        load_dst(Chunk(SOURCES, 2, 0, c), first=c == 0, last=False)

            run(e, NODES, node_io, lag=4, lead=1, unroll=4)

            def store_h(ch, rows):
                e.wait_ge(ln_h, ch.g + 1)
                e.dma_start(edge_rows(rows, ch).rearrange("p (j q) -> p j q", q=P),
                            hb[ch.s][:, 0:EJ, 0:P]).then_inc(h_out[ch.s], 16)

            def source_io(at):
                ch = at(0)
                if ch and not early(ch):
                    load_source_x(ch)
                if at(1) and not early(at(1)):
                    load_attrs(at(1), last=at(2) is None)
                if at(-2):
                    store_h(at(-2), h_src)
                if ch and not early(ch):
                    load_dst(ch, first=False, last=at(1) is None)

            run(e, SOURCES, source_io, lag=2, lead=2)

            def store_agg(at):
                ch = at(0)
                e.wait_ge(agg_rows, ch.c + 1)
                e.dma_start(edge_rows(agg_dst, ch), reg_m[:, cols(ch)]).then_inc(agg_stored[ch.s], 16)

            def load_dest(ch):
                e.wait_ge(kept[ch.s], (ch.w + (EC // 2 + 1)) * 16)
                e.sem_inc(sync_steps, 1)
                e.wait_ge(ln_centred[ch.s], ch.k)
                e.dma_start(xb[ch.s][:, 0:ET * D], edge_rows(x_dst, ch)).then_inc(x_in[ch.s], 16)

            for c in range(2):
                load_dest(Chunk(DESTS, 2, 0, c))
            run(e, EDGES, store_agg)

            def load2_node(ch, rows):
                wait_past(e, x1_done, ch.g * 2 - 6)
                e.dma_start(node_h[ch.q], edge_rows(ht_node, ch)).then_inc(node_in[ch.q], 16)
                e.dma_start(node_x[ch.q], node_view(x, rows)).then_inc(node_in[ch.q], 16)

            def load2_early(c):
                for s in range(2):
                    e.wait_ge(ht_out[s], 16 * SOURCES.k0[s])
                load2_node(Chunk(NODES, 4, 0, c), node_rows(Chunk(NODES, 4, 0, c)))

            def load_dest_agg(ch):
                if isinstance(ch.c, int) and ch.c < 2:
                    e.wait_ge(agg_stored[0], 16 * (EC // 2))
                    e.wait_ge(agg_stored[1], 16 * (EC // 2))
                wait_past(e, v_used[ch.s], ch.w)
                wait_past(e, dest_summed, ch.c - 1)
                e.dma_start(hin[ch.s][:, 0:ET * D], edge_rows(agg_dst, ch)).then_inc(d_in[ch.s], 16)

            def store_dest(ch):
                e.wait_ge(dest_summed, ch.c + 1)
                e.dma_start(edge_rows(h_dst, ch).rearrange("p (j q) -> p j q", q=P),
                            hb[ch.s][:, 0:EJ, 0:P]).then_inc(h_out[ch.s], 16)

            def dest_io(at):
                if at(0) and not early(at(0)):
                    load_dest(at(0))
                if at(-2):
                    store_dest(at(-2))
                if at(0):
                    load_dest_agg(at(0))
                for c in range(4):
                    if at(1 - c) and at(2 - c) is None:
                        load2_early(c)

            run(e, DESTS, dest_io, lag=2, lead=2)

            e.dma_start(bias_f[0].rearrange("p (t d) -> p t d", d=D),
                        b_out.rearrange("(a t d) -> a t d", a=1, t=1).to_broadcast([96, 8, D]))\
                .then_inc(bias_in, 16)

            def store2_node(ch, last):
                e.wait_ge(fin_done, ch.c * 2 + 2)
                if last:
                    e.dma_start(rest_view(out), node_x1[ch.q][OVERP:P, :]).then_inc(out_stored[ch.q], 16)
                else:
                    e.dma_start(node_view(out, node_rows(ch)), node_x1[ch.q]).then_inc(out_stored[ch.q], 16)

            def load2(ch, h, xs):
                first = ch.part is SOURCES and early(ch)
                if first:
                    e.wait_ge(ln_centred[ch.s], DESTS.k0[ch.s] + EC // 2)
                else:
                    e.wait_ge(t_done, (ch.g - BC) * 2 - 2)
                e.dma_start(hin[ch.s][:, 0:W], edge_rows(h, ch)).then_inc(h2_in[ch.s], 16)
                if ch.part is SOURCES:
                    wait_past(e, h_summed, ch.c - 1)
                    e.dma_start(agg_s[ch.s], edge_rows(agg_src, ch)).then_inc(agg2_in[ch.s], 16)
                if not first:
                    e.wait_ge(x1_done, ch.g * 2 - 2)
                e.dma_start(xb[ch.s][:, 0:W], edge_rows(xs, ch)).then_inc(x2_in[ch.s], 16)

            def node2_io(at):
                if at(0) and at(-4):
                    load2_node(at(0), rows_of(at))
                if at(-1) and at(0) is None:
                    for s in range(2):
                        e.wait_ge(h_out[s], 16 * EC)
                        e.wait_ge(v_used[s], EC // 2)
                        e.wait_ge(kept[s], 16 * 3 * (EC // 2))
                    for c in range(2):
                        load2(Chunk(SOURCES, 2, 0, c), h_src, x_src)
                if at(-4):
                    store2_node(at(-4), last=at(-3) is None)

            run(e, NODES, node2_io, lag=4, lead=1, unroll=4)

            def edge2_io(at):
                ch = at(0)
                if ch.part is DESTS:
                    load2(ch, h_dst, x_dst)
                elif not early(ch):
                    load2(ch, h_src, x_src)

            run(e, SOURCES, edge2_io)
            run(e, DESTS, edge2_io)

        @block.tensor
        def _(e):
            e.wait_ge(const_made, CONSTS)
            e.wait_ge(idx_float, 1)
            for n, f in enumerate((flt[0], flt[3], flt[5], flt[4])):
                for a in range(2):
                    mm = e.transpose(psum[:, n, a * HT:(a + 1) * HT], f[0:HT, a * P:(a + 1) * P],
                                     ident[0:HT, 0:HT])
            mm.then_inc(idx_turned, 1)
            e.wait_ge(idx_made, 4)

            def node_products(ch, first):
                e.wait_ge(ln_h, ch.g + 1)
                for j in range(ch.pairs):
                    e.matmul(ps_g[:, 0:P + 1], hb[ch.s][:, j, 0:P], hb[ch.s][:, j, :],
                             start=(first and j == 0), stop=False, skip_group_check=True)
                for u, (j0, n) in enumerate(quads(ch)):
                    wait_past(e, ht_copied, ch.c * 2 + (u - 1))
                    for j in range(j0, j0 + n):
                        mm = e.transpose(ps_t[u][:, (j - j0) * P:(j - j0 + 1) * P], hb[ch.s][:, j, 0:P],
                                         ident[:, :])
                    mm.then_inc(ht_turned, 1)

            def node_step(at):
                node_products(at(0), first=at(-1) is None)

            run(e, NODES, node_step)
            e.wait_ge(weights_in, 16 * WEIGHTS)

            def turn_attrs(ch, last):
                e.wait_ge(ea_in[ch.s], (ch.w + 1) * 32 + (16 if last else 0))
                wait_past(e, ea_copied, ch.c * 2)
                if isinstance(ch.c, int) and ch.c == 0:
                    e.wait_ge(ht_copied, 2 * BC)
                for u, (j0, n) in enumerate(quads(ch)):
                    for j in range(j0, j0 + n):
                        mm = e.transpose(ps_t[u][:, (j - j0) * P:(j - j0 + 1) * P],
                                         ea[ch.s][:, j * P:(j + 1) * P], ident[:, :])
                mm.then_inc(ea_turned, 1)

            def attr_products(ch):
                wait_past(e, msg_made, ch.c)
                for u, (j0, n) in enumerate(quads(ch)):
                    e.wait_ge(ea_copied, ch.c * 2 + (u + 1))
                    e.matmul(ps_z[:, u, 0:n * P], we_blk[:, :], ea_t[ch.s][:, j0 * P:(j0 + n) * P],
                             start=True, stop=False, skip_group_check=True)
                e.wait_ge(ln_h, ch.g + 1)
                for u, (j0, n) in enumerate(quads(ch)):
                    for j in range(j0, j0 + n):
                        mm = e.matmul(ps_z[:, u, (j - j0) * P:(j - j0 + 1) * P], hb[ch.s][:, j, 0:P],
                                      ident[:, :], start=False, stop=(j == j0 + n - 1), skip_group_check=True)
                mm.then_inc(h_used[ch.s], 1)

            def attr_step(at):
                if at(0):
                    turn_attrs(at(0), last=at(1) is None)
                if at(-1):
                    attr_products(at(-1))

            run(e, SOURCES, attr_step, lag=1, lead=1)

            def bring(n, col, how, at):
                e.wait_ge(link_col, n)
                e.matmul(ps_o[:, at:at + col.shape[1]], how[:, :], col, start=True, stop=True).then_inc(link_ps, 1)

            bring(2, run_max, swap, 0)
            bring(4, soft_ends, down, 0)

            def turn_agg(at):
                ch = at(0)
                e.wait_ge(agg_made, ch.c + 1)
                wait_past(e, agg_rows, ch.c - 1)
                for j in range(EJ):
                    mm = e.transpose(ps_agg[ch.s][:, j * P:(j + 1) * P], agg_t[ch.s][:, j * P:(j + 1) * P],
                                     ident[:, :])
                mm.then_inc(agg_turned, 1)

            run(e, EDGES, turn_agg)


            def turn_h(ch, u):
                j0, n = quads(ch)[u]
                if ch.part is SOURCES:
                    e.wait_ge(h_summed, ch.c + 1)
                else:
                    e.wait_ge(h2_in[ch.s], (ch.k - SOURCES.k0[ch.s] + 1) * 16)
                wait_past(e, t_copied, (ch.g - BC) * 2 + (u - 1))
                for j in range(j0, j0 + n):
                    mm = e.transpose(ps_t[u][:, (j - j0) * P:(j - j0 + 1) * P],
                                     hin[ch.s][:, j * P:(j + 1) * P], ident[:, :])
                mm.then_inc(t_done, 1)

            def hidden_product(ch, u):
                j0, n = quads(ch)[u]
                if ch.part is NODES:
                    e.wait_ge(node_in[ch.q], (ch.v + 1) * 32)
                    h = node_h[ch.q][:, j0 * P:(j0 + n) * P]
                else:
                    e.wait_ge(t_copied, (ch.g - BC) * 2 + (u + 1))
                    h = ht[u][:, 0:n * P]
                wait_past(e, y_done, ch.g * 2 + u)
                for a in range(2):
                    mm = e.matmul(ps_z[:, a, 0:n * P], w1_dup[a * D:(a + 1) * D, :],
                                  h[a * D:(a + 1) * D, :], start=True, stop=True)
                mm.then_inc(z_done, 1)

            def gram_dest(at):
                ch = at(0)
                if at(1) is None:
                    hidden_product(Chunk(NODES, 4, 0, 0), 0)
                e.wait_ge(v_made, ch.c + 1)
                for j in range(EJ):
                    mm = e.matmul(ps_g[:, 0:P + 1], hin[ch.s][:, j * P:(j + 1) * P], vb[ch.s][:, j, :],
                                  start=False, stop=False, skip_group_check=True)
                mm.then_inc(v_used[ch.s], 1)

            run(e, EDGES, gram_dest, lead=1)

            e.wait_ge(stat, 2)
            e.matmul(ps_w[:, 0:H], gram_sb[:, :], w1_dup[:, :], start=True, stop=True).then_inc(stat_ps, 1)
            e.wait_ge(stat, 3)
            e.matmul(ps_o[:, 0:1], gram_w[:, :], ones_col[:, :], start=True, stop=True).then_inc(stat_ps, 1)
            e.matmul(ps_t[0][:, 0:1], w1_dup[:, :], sum_c, start=True, stop=True).then_inc(stat_ps, 1)
            e.wait_ge(bn_ready, 1)

            def first_product(ch, u):
                j0, n = quads(ch)[u]
                e.wait_ge(y_done, ch.g * 2 + (u + 1))
                wait_past(e, x1_done, ch.g * 2 + (u if ch.part is DESTS else u - 1))
                for j in range(n):
                    for a in range(2):
                        mm = e.matmul(w_bank(ch, u)[:, (2 * j + a) * D:(2 * j + a + 1) * D],
                                      yb[u][:, (a * 4 + j) * P:(a * 4 + j + 1) * P], w2_sb[:, :],
                                      start=True, stop=True)
                mm.then_inc(w_done, 1)

            def turn_h1(ch, u):
                j0, n = quads(ch)[u]
                e.wait_ge(l_h, ch.g + 1)
                wait_past(e, t1_copied, outs(ch) * 2 + (u - 1))
                if ch.part is DESTS and u == 0:
                    e.wait_ge(n_summed, EC)
                for j in range(j0, j0 + n):
                    mm = e.transpose(ps_t1[u][:, (j - j0) * P:(j - j0 + 1) * P], hb[ch.s][:, j, 0:P],
                                     ident[:, :])
                mm.then_inc(t1_done, 1)

            def out_product(ch, u):
                j0, n = quads(ch)[u]
                if ch.part is NODES and isinstance(ch.c, int) and ch.c == 0:
                    e.wait_ge(bias_made, 3 * 3)
                if ch.part is DESTS:
                    e.wait_ge(mean_made, ch.c + 1)
                e.wait_ge(t1_copied, outs(ch) * 2 + (u + 1))
                wait_past(e, fin_done, outs(ch) * 2 + (u - 1 if ch.part is NODES else u))
                e.matmul(o_bank(ch, u)[:, 0:n * P], ones3[:, :], bias3[:, 0:n * P], start=True, stop=False,
                         skip_group_check=True)
                for j in range(n):
                    o = o_bank(ch, u)[:, j * P:(j + 1) * P]
                    if ch.part is DESTS:
                        e.matmul(o, mean_t[ch.s][:, (j0 + j) * P:(j0 + j + 1) * P], wb_blk[:, :],
                                 start=False, stop=False, skip_group_check=True)
                    mm = e.matmul(o, h1t[u][:, j * P:(j + 1) * P], wa_blk[:, :],
                                  start=False, stop=(j == n - 1), skip_group_check=True)
                mm.then_inc(o_done, 1)

            def turn_source(ch):
                e.wait_ge(l_h, ch.g + 1)
                wait_past(e, n_summed, ch.c)
                for j in range(EJ):
                    mm = e.transpose(ps_t1_flat[:, j * P:(j + 1) * P], hb[ch.s][:, j, 0:P], ident[:, :])
                mm.then_inc(hs_turned, 1)

            def second(at):
                now, ago, old, soon = at(0), at(-1), at(-2), at(1)
                ahead = now and soon and now.part is not NODES
                if now and not (now.part is NODES and ago is None):
                    hidden_product(now, 0)
                if now and linked_late(now):
                    bring(6, mean_ends, down, 0)
                if ago:
                    first_product(ago, 1)
                if old and old.part is SOURCES:
                    turn_source(old)
                elif old:
                    turn_h1(old, 0)
                    turn_h1(old, 1)
                if ahead:
                    turn_h(soon, 0)
                if now:
                    hidden_product(now, 1)
                if old and old.part is not SOURCES:
                    out_product(old, 0)
                if ahead:
                    turn_h(soon, 1)
                if now:
                    first_product(now, 0)
                if old and old.part is not SOURCES:
                    out_product(old, 1)

            run(e, NODES, second, lag=2, lead=1, unroll=4)
            e.wait_ge(x1_done, 2 * BC)
            e.wait_ge(fin_done, 2 * BC)
            for u in range(2):
                turn_h(Chunk(SOURCES, 4, 0, 0), u)
            run(e, SOURCES, second, lead=1, unroll=4, after=DESTS)
            run(e, DESTS, second, lag=2, lead=1, unroll=4, before=SOURCES)

        @block.scalar
        def _(e):
            e.wait_ge(const_made, CONSTS)

            def square(ch):
                e.wait_ge(ln_centred[ch.s], ch.k + 1)
                wait_past(e, ln_ssq, ch.g)
                n, done = ch.tiles * D, act_tiles(ch)
                for t in range(done):
                    e.activation(sq[:, t * D:(t + 1) * D], xc[ch.s][:, t * D:(t + 1) * D], ACT.Square,
                                 accum_out=st[ch.s][:, 1, t:t + 1])
                e.activation(sq[:, done * D:n], xc[ch.s][:, done * D:n], ACT.Square).then_inc(ln_squared, 1)

            def root(ch):
                e.wait_ge(ln_ssq, ch.g + 1)
                e.activation(st[ch.s][:, 2, 0:ch.tiles], st[ch.s][:, 1, 0:ch.tiles], ACT.Sqrt,
                             bias=norm_eps, scale=1.0 / D).then_inc(ln_std, 1)

            def copy_turned(ch):
                wait_past(e, ht_out[ch.s], ch.w * 16)
                for u, (j0, n) in enumerate(quads(ch)):
                    e.wait_ge(ht_turned, ch.c * 2 + (u + 1))
                    e.activation(first_t[ch.s][:, j0 * P:(j0 + n) * P], ps_t[u][:, 0:n * P], ACT.Copy)\
                        .then_inc(ht_copied, 1)

            def copy_attrs(ch):
                e.wait_ge(ea_turned, ch.c + 1)
                wait_past(e, h_used[ch.s], ch.w)
                for u, (j0, n) in enumerate(quads(ch)):
                    e.activation(ea_t[ch.s][:, j0 * P:(j0 + n) * P], ps_t[u][:, 0:n * P], ACT.Copy)\
                        .then_inc(ea_copied, 1)

            def first_nodes(at):
                if at(-1):
                    root(at(-1))
                if at(0):
                    square(at(0))
                if at(-2):
                    copy_turned(at(-2))

            run(e, NODES, first_nodes, lag=2)

            def first_sources(at):
                if at(-1):
                    root(at(-1))
                if at(0):
                    square(at(0))
                    copy_attrs(at(0))

            run(e, SOURCES, first_sources, lag=1)

            def exponent(at):
                ch = at(0)
                e.wait_ge(arg_made, ch.c + 1)
                e.activation(reg_m[:, cols(ch)], reg_m[:, cols(ch)], ACT.Exp).then_inc(exp_made, 1)

            run(e, EDGES, exponent)

            def inverse(ch, ready, region, before, bias):
                e.wait_ge(ready, ch.c + 1)
                wait_past(e, newton_b, ch.c + (before or -1))
                g = inv_place(ch, before)
                e.activation(g, region[:, cols(ch)], ACT.Ln, bias=bias).then_inc(inv_guess, 1)
                e.wait_ge(inv_guess, (ch.c + before) * 2 + 1)
                e.activation(g, g, ACT.Exp, scale=-1.0).then_inc(inv_guess, 1)

            run(e, EDGES, lambda at: inverse(at(0), s_linked, reg_m, 0, soft_eps))

            def first_dests(at):
                if at(-1):
                    root(at(-1))
                if at(0):
                    square(at(0))

            run(e, DESTS, first_dests, lag=1)

            e.wait_ge(stat, 6)
            e.activation(std_c, var_c, ACT.Sqrt, bias=norm_eps).then_inc(stat_std, 1)
            e.wait_ge(bn_ready, 1)

            def copy_h(ch, u):
                n = quads(ch)[u][1]
                e.wait_ge(t_done, (ch.g - BC) * 2 + (u + 1))
                wait_past(e, z_done, ch.g * 2 + (u - 1))
                e.activation(ht[u][:, 0:n * P], ps_t[u][:, 0:n * P], ACT.Copy).then_inc(t_copied, 1)

            def hidden(ch, u):
                n = quads(ch)[u][1]
                e.wait_ge(z_done, ch.g * 2 + (u + 1))
                wait_past(e, w_done, ch.g * 2 + (u - 1))
                e.activation(yb[u][:, :].rearrange("p (a q) -> p a q", a=2)[:, :, 0:n * P],
                             ps_z[:, :, 0:n * P], ACT.Relu, bias=shift_c, scale=scale_c).then_inc(y_done, 1)

            def copy_h1(ch, u):
                n = quads(ch)[u][1]
                e.wait_ge(t1_done, outs(ch) * 2 + (u + 1))
                wait_past(e, o_done, outs(ch) * 2 + (u - 1))
                e.activation(h1t[u][:, 0:n * P], ps_t1[u][:, 0:n * P], ACT.Copy).then_inc(t1_copied, 1)

            def square2(ch):
                n = ch.tiles * D
                e.wait_ge(l_centred, ch.g + 1)
                wait_past(e, l_ssq, ch.g)
                e.activation(sq[:, 0:n], xc[ch.s][:, 0:n], ACT.Square).then_inc(l_squared, 1)

            def root2(ch):
                e.wait_ge(l_ssq, ch.g + 1)
                e.activation(st[ch.s][:, 2, 0:ch.tiles], st[ch.s][:, 1, 0:ch.tiles], ACT.Sqrt,
                             bias=norm_eps, scale=1.0 / D).then_inc(l_std, 1)

            def second(at):
                now, ago, old, soon = at(0), at(-1), at(-2), at(1)
                ahead = now and soon and now.part is not NODES
                if now:
                    hidden(now, 0)
                if now and linked_late(now):
                    inverse(old, c_linked, reg_a, EC, 0.0)
                    inverse(ago, c_linked, reg_a, EC, 0.0)
                if old and old.part is not SOURCES:
                    copy_h1(old, 0)
                    copy_h1(old, 1)
                if ahead:
                    copy_h(soon, 0)
                if now and counts_in_turn(now):
                    inverse(now, c_linked, reg_a, EC, 0.0)
                if now:
                    hidden(now, 1)
                if ago:
                    square2(ago)
                if ahead:
                    copy_h(soon, 1)
                if ago:
                    root2(ago)

            run(e, NODES, second, lag=2, lead=1, unroll=4)
            for u in range(2):
                copy_h(Chunk(SOURCES, 4, 0, 0), u)
            run(e, SOURCES, second, lead=1, unroll=4, after=DESTS)
            run(e, DESTS, second, lag=2, lead=1, unroll=4, before=SOURCES)

        @block.vector
        def _(e):
            for n, pad in enumerate((0, N, N)):
                e.memset(raw[n], pad).then_inc(raw_filled, 1)
            e.wait_ge(raw_in, 16 * 11)
            for n in range(3):
                e.tensor_copy(flt[n][0:HT, :], raw[n][0:HT, :]).then_inc(idx_step, 1)
            e.tensor_copy(other_dst, other_raw[:, :]).then_inc(idx_step, 1)
            e.wait_ge(idx_step, 4)
            e.tensor_scalar(flt[3][0:HT, :], flt[1][0:HT, :], float(N - 1), None, ALU.min).then_inc(idx_step, 1)
            e.tensor_tensor(flt[4][0:HT, :], flt[1][0:HT, :], flt[2][0:HT, :], ALU.not_equal)\
                .then_inc(idx_step, 1)
            e.wait_ge(idx_step, 6)
            e.scalar_tensor_tensor(out=flt[5][0:HT, :], in0=flt[1][0:HT, :], scalar=-float(N),
                                   in1=flt[4][0:HT, :], op0=ALU.add, op1=ALU.mult).then_inc(idx_step, 1)
            e.wait_ge(idx_step, 7)
            e.tensor_scalar(flt[5][0:HT, :], flt[5][0:HT, :], float(N), None, ALU.add).then_inc(idx_float, 1)
            e.wait_ge(idx_turned, 1)
            for n, to in enumerate((src_idx, dst_idx, put_idx, seg_end)):
                e.tensor_copy(to[:, :].rearrange("p (j a) -> p a j", a=2),
                              psum[:, n, 0:2 * HT].rearrange("p (a j) -> p a j", a=2)).then_inc(idx_made, 1)

            def x_of(ch):
                return first_x[ch.q] if ch.part is NODES else xb[ch.s]

            def row_sum(ch):
                if ch.part is NODES:
                    e.wait_ge(first_in[ch.q], (ch.v + 1) * 16)
                else:
                    e.wait_ge(x_in[ch.s], (ch.k - SOURCES.k0[ch.s] + 1) * 16)
                e.tensor_reduce(st[ch.s][:, 0, 0:ch.tiles], tile_rows(x_of(ch), ch), AX.X, ALU.add)\
                    .then_inc(ln_sum, 1)

            def centre(ch):
                e.wait_ge(ln_sum, ch.g + 1)
                e.scalar_tensor_tensor(out=tile_rows(xc[ch.s], ch), in0=spread(ch, 0), scalar=-1.0 / D,
                                       in1=tile_rows(x_of(ch), ch), op0=ALU.mult, op1=ALU.add)\
                    .then_inc(ln_centred[ch.s], 1)

            def square_sum(ch):
                done = act_tiles(ch)
                e.wait_ge(ln_squared, ch.g + 1)
                e.tensor_reduce(st[ch.s][:, 1, done:ch.tiles], tile_rows(sq, ch)[:, done:ch.tiles, :], AX.X,
                                ALU.add).then_inc(ln_ssq, 1)

            def invert(ch):
                e.wait_ge(ln_std, ch.g + 1)
                e.reciprocal(st[ch.s][:, 3, 0:ch.tiles], st[ch.s][:, 2, 0:ch.tiles]).then_inc(ln_rstd, 1)

            def invert_last_node(ch):
                e.wait_ge(ln_std, ch.g + 1)
                e.reciprocal(st[ch.s][:, 3, :], st[ch.s][:, 2, :]).then_inc(edges_set, 1)
                e.wait_ge(edges_set, 1)
                e.tensor_scalar(st[ch.s][:, 3, :], st[ch.s][:, 3, :], own_rows[:, :], None, ALU.mult)\
                    .then_inc(ln_rstd, 1)

            def norm(ch):
                e.wait_ge(ln_rstd, ch.g + 1)
                if ch.part is NODES:
                    wait_past(e, ht_turned, ch.c * 2 - 2)
                if ch.part is SOURCES:
                    e.wait_ge(ht_turned, 2 * BC)
                    wait_past(e, h_used[ch.s], ch.w)
                    wait_past(e, h_out[ch.s], ch.w * 16)
                if ch.part is DESTS:
                    e.wait_ge(h_out[ch.s], (ch.w + EC // 2) * 16)
                e.scalar_tensor_tensor(out=hb[ch.s][:, 0:ch.pairs, 0:P], in0=pair_rows(xc[ch.s], ch), scalar=0.0,
                                       in1=spread(ch, 3), op0=ALU.max, op1=ALU.mult).then_inc(ln_h, 1)

            def first_nodes(at):
                now, ago = at(0), at(-1)
                if now:
                    row_sum(now)
                if ago:
                    square_sum(ago)
                if now:
                    centre(now)
                if ago and now is None:
                    invert_last_node(ago)
                elif ago:
                    invert(ago)
                if ago:
                    norm(ago)

            run(e, NODES, first_nodes, lag=1, unroll=4)

            e.wait_ge(pos_set, 16 * 3)
            e.memset(same[:, HALF:HALF + 1], 0).then_inc(edges_set, 1)

            def before_col(region, ch):
                return region[:, ds(ch.c * W - 1, 1)]

            def masks(ch, first, last):
                d = dcol[ch.s]
                e.wait_ge(dcol_in[ch.s], (ch.w + 1) * 32)
                if first:
                    e.memset(d[:, 0:1], -1).then_inc(edges_set, 1)
                    e.wait_ge(edges_set, 3)
                if last:
                    e.memset(d[D:P, W + 1 - PADS:W + 1], N).then_inc(edges_set, 1)
                    e.wait_ge(edges_set, 4)
                e.tensor_tensor(same[:, cols(ch)], d[:, 1:W + 1], d[:, 0:W], ALU.is_equal).then_inc(same_made, 1)
                e.tensor_scalar(linked[:, cols(ch)], d[:, 1:W + 1], other_dst, None, ALU.is_equal)\
                    .then_inc(linked_made, 1)

            def messages(ch, first):
                e.wait_ge(h_used[ch.s], ch.w + 1)
                e.tensor_scalar(reg_a[:, cols(ch)], ps_z_flat[:, 0:W], 0.0, MSG_EPS, ALU.max, ALU.add)\
                    .then_inc(msg_made, 1)
                e.wait_ge(msg_made, ch.c + 1)
                e.wait_ge(same_made, ch.c + 1)
                if first:
                    for s in range(2):
                        e.wait_ge(ht_out[s], 16 * SOURCES.k0[s])
                else:
                    e.wait_ge(run_made, ch.c)
                e.tensor_tensor_scan(reg_m[:, cols(ch)], same[:, cols(ch)], reg_a[:, cols(ch)],
                                     0.0 if first else before_col(reg_m, ch), ALU.mult, ALU.max)\
                    .then_inc(run_made, 1)

            def first_sources(at):
                now, ago, old = at(0), at(-1), at(-2)
                if now:
                    row_sum(now)
                if ago:
                    square_sum(ago)
                if old:
                    messages(old, first=at(-3) is None)
                if ago:
                    invert(ago)
                if now:
                    centre(now)
                if ago:
                    norm(ago)
                    masks(ago, first=old is None, last=now is None)

            run(e, SOURCES, first_sources, lag=2)

            e.wait_ge(run_made, EC)
            e.tensor_tensor_scan(reg_m[:, ::-1], same[:, 1:HALF + 1][:, ::-1], reg_m[:, ::-1], 0.0,
                                 ALU.mult, ALU.max).then_inc(max_made, 1)

            e.wait_ge(max_made, 1)
            e.tensor_copy(run_max[0:D, :], reg_m[0:D, HALF - 1:HALF]).then_inc(link_col, 1)
            e.tensor_copy(run_max[D:P, :], reg_m[D:P, 0:1]).then_inc(link_col, 1)
            e.wait_ge(link_ps, 1)
            e.wait_ge(link_col, 2)
            e.tensor_tensor(tot_max, ps_o[:, 0:1], run_max, ALU.max).then_inc(link_made, 1)
            e.wait_ge(link_made, 1)

            def argument(ch):
                m, a = reg_m[:, cols(ch)], reg_a[:, cols(ch)]
                e.scalar_tensor_tensor(out=m, in0=linked[:, cols(ch)], scalar=tot_max, in1=m,
                                       op0=ALU.mult, op1=ALU.max).then_inc(max_linked, 1)
                e.wait_ge(max_linked, ch.c + 1)
                e.tensor_tensor(m, a, m, ALU.subtract).then_inc(arg_made, 1)

            def sums(ch, first):
                m, a, keep = reg_m[:, cols(ch)], reg_a[:, cols(ch)], same[:, cols(ch)]
                e.wait_ge(exp_made, ch.c + 1)
                e.tensor_tensor(a, a, m, ALU.mult).then_inc(weighted, 1)
                if not first:
                    e.wait_ge(e_summed, ch.c)
                e.tensor_tensor_scan(m, keep, m, 0.0 if first else before_col(reg_m, ch), ALU.mult, ALU.add)\
                    .then_inc(e_summed, 1)
                e.wait_ge(weighted, ch.c + 1)
                if not first:
                    e.wait_ge(a_summed, ch.c)
                e.tensor_tensor_scan(a, keep, a, 0.0 if first else before_col(reg_a, ch), ALU.mult, ALU.add)\
                    .then_inc(a_summed, 1)

            def exponentials(at):
                if at(0):
                    argument(at(0))
                if at(-1):
                    sums(at(-1), first=at(-2) is None)

            run(e, EDGES, exponentials, lag=1)

            def border_sums(ends, carry, n, a_ready, b_ready):
                e.wait_ge(a_ready, EC)
                e.wait_ge(b_ready, EC)
                e.tensor_copy(ends[:, 0:1], reg_m[:, HALF - 1:HALF]).then_inc(link_col, 1)
                e.tensor_copy(ends[:, 1:2], reg_a[:, HALF - 1:HALF]).then_inc(link_col, 1)
                e.wait_ge(link_ps, n)
                e.tensor_copy(carry, ps_o[:, 0:2]).then_inc(link_made, 1)
                e.wait_ge(link_made, n)

            border_sums(soft_ends, soft_carry, 2, e_summed, a_summed)

            def link(ch, region, carry, done):
                r = region[:, cols(ch)]
                e.scalar_tensor_tensor(out=r, in0=linked[:, cols(ch)], scalar=carry, in1=r,
                                       op0=ALU.mult, op1=ALU.add).then_inc(done, 1)

            def newton(ch, region, bias, before):
                g, r = inv_place(ch, before), region[:, cols(ch)]
                e.wait_ge(inv_guess, (ch.c + before) * 2 + 2)
                e.scalar_tensor_tensor(out=r, in0=r, scalar=bias, in1=g, op0=ALU.add, op1=ALU.mult)\
                    .then_inc(newton_a, 1)
                e.wait_ge(newton_a, ch.c + (before + 1))
                e.scalar_tensor_tensor(out=r, in0=r, scalar=-2.0, in1=g, op0=ALU.add, op1=ALU.mult)\
                    .then_inc(newton_b, 1)

            def aggregate(at):
                now, ago, old = at(0), at(-1), at(-2)
                if now:
                    link(now, reg_m, soft_carry[:, 0:1], s_linked)
                    link(now, reg_a, soft_carry[:, 1:2], a_linked)
                if ago:
                    newton(ago, reg_m, SOFTMAX_EPS, 0)
                if old:
                    e.wait_ge(agg_turned, old.c + 1)
                    end = seg_end[:, ds(old.c * ET, ET)].unsqueeze(2).to_broadcast([P, ET, D])
                    e.tensor_tensor(reg_m[:, cols(old)].rearrange("p (t d) -> p t d", d=D),
                                    ps_agg[old.s][:, 0:W].rearrange("p (t d) -> p t d", d=D),
                                    end, ALU.mult).then_inc(agg_rows, 1)
                if ago:
                    e.wait_ge(newton_b, ago.c + 1)
                    e.wait_ge(a_linked, ago.c + 1)
                    e.scalar_tensor_tensor(out=agg_t[ago.s][:, 0:W], in0=reg_m[:, cols(ago)], scalar=-1.0,
                                           in1=reg_a[:, cols(ago)], op0=ALU.mult, op1=ALU.mult)\
                        .then_inc(agg_made, 1)

            run(e, EDGES, aggregate, lag=2)

            for s in range(2):
                e.memset(vb[s][:, :, P:P + 1], 1.0).then_inc(edges_set, 1)

            def gram_input(ch):
                e.wait_ge(ln_h, ch.g + 1)
                e.wait_ge(d_in[ch.s], (ch.w + 1) * 16)
                wait_past(e, v_used[ch.s], ch.w)
                e.wait_ge(edges_set, 6)
                e.scalar_tensor_tensor(out=vb[ch.s][:, :, 0:P], in0=hb[ch.s][:, 0:EJ, 0:P], scalar=2.0,
                                       in1=pair_rows(hin[ch.s], ch), op0=ALU.mult, op1=ALU.add).then_inc(v_made, 1)

            def sum_dest(ch):
                e.wait_ge(v_made, ch.c + 1)
                h = hb[ch.s][:, 0:EJ, 0:P]
                e.tensor_tensor(h, h, pair_rows(hin[ch.s], ch), ALU.add).then_inc(dest_summed, 1)

            def first_dests(at):
                now, ago = at(0), at(-1)
                if now:
                    row_sum(now)
                if ago:
                    square_sum(ago)
                if now:
                    centre(now)
                if ago:
                    invert(ago)
                    norm(ago)
                    gram_input(ago)
                    sum_dest(ago)

            run(e, DESTS, first_dests, lag=1)

            for s in range(2):
                e.wait_ge(v_used[s], EC // 2)
            e.tensor_tensor(gram_sb[:, :], ps_g[:, 0:P], blocks[:, :], ALU.mult).then_inc(stat, 1)
            e.tensor_copy(sum_c, ps_g[:, P:P + 1]).then_inc(stat, 1)
            e.wait_ge(stat_ps, 1)
            e.tensor_tensor(gram_w[:, :], ps_w[:, 0:H], w1_dup[:, :], ALU.mult).then_inc(stat, 1)
            e.wait_ge(stat_ps, 3)
            e.tensor_scalar(ex2_c, ps_o[:, 0:1], 1.0 / N, None, ALU.mult).then_inc(stat, 1)
            e.tensor_scalar(mean_c, ps_t[0][:, 0:1], 1.0 / N, None, ALU.mult).then_inc(stat, 1)
            e.wait_ge(stat, 5)
            e.tensor_tensor(m2_c, mean_c, mean_c, ALU.mult).then_inc(stat_mid, 1)
            e.wait_ge(stat_mid, 1)
            e.tensor_tensor(m2_c, ex2_c, m2_c, ALU.subtract).then_inc(stat_mid, 1)
            e.wait_ge(stat_mid, 2)
            e.tensor_scalar(var_c, m2_c, 0.0, None, ALU.max).then_inc(stat, 1)
            e.wait_ge(stat_std, 1)
            e.reciprocal(rs_c, std_c).then_inc(stat_mid, 1)
            e.wait_ge(stat_mid, 3)
            e.tensor_tensor(scale_c, gamma_c, rs_c, ALU.mult).then_inc(stat_mid, 1)
            e.wait_ge(stat_mid, 4)
            e.tensor_tensor(mscale_c, mean_c, scale_c, ALU.mult).then_inc(stat_mid, 1)
            e.wait_ge(stat_mid, 5)
            e.tensor_tensor(shift_c, beta_c, mscale_c, ALU.subtract).then_inc(bn_ready, 1)

            e.wait_ge(bias_in, 16)
            low = 0
            for n, row in enumerate((0, 32, 64)):
                part = bias_part
                e.tensor_copy(part[:, :], bias_f[n % 2]).then_inc(bias_made, 1)
                low += 1
                e.wait_ge(bias_made, low)
                e.tensor_copy(bias3[row:row + 1, :], part[row:row + 1, :]).then_inc(bias_made, 1)
                e.tensor_tensor(bias_f[1 - n % 2], bias_f[n % 2], part[:, :], ALU.subtract).then_inc(bias_made, 1)
                low += 2
                e.wait_ge(bias_made, low)

            def add_agg(ch):
                e.wait_ge(h2_in[ch.s], (ch.w + 1) * 16)
                e.wait_ge(agg2_in[ch.s], (ch.w + 1) * 16)
                e.tensor_tensor(hin[ch.s][:, 0:W], hin[ch.s][:, 0:W], agg_s[ch.s], ALU.add).then_inc(h_summed, 1)

            def x1_of(ch):
                if ch.part is NODES:
                    return node_x1[ch.q]
                return (source_x1 if ch.part is SOURCES else dest_x1)[ch.q]

            def first_residual(ch, u):
                j0, n = quads(ch)[u]
                part = slice(j0 * P, (j0 + n) * P)
                if ch.part is NODES:
                    e.wait_ge(node_in[ch.q], (ch.v + 1) * 32)
                    if u == 0:
                        wait_past(e, out_stored[ch.q], ch.v * 16)
                    xs = node_x[ch.q]
                else:
                    e.wait_ge(x2_in[ch.s], (ch.k - SOURCES.k0[ch.s] + 1) * 16)
                    xs = xb[ch.s]
                if ch.part is DESTS and u == 0:
                    wait_past(e, patched[ch.q], ch.v * (16 * ET))
                e.wait_ge(w_done, ch.g * 2 + (u + 1))
                e.tensor_tensor(x1_of(ch)[:, part], w_bank(ch, u)[:, 0:n * P], xs[:, part], ALU.add)\
                    .then_inc(x1_done, 1)

            def centre2(ch):
                e.wait_ge(x1_done, ch.g * 2 + 2)
                e.tensor_reduce(st[ch.s][:, 0, 0:ch.tiles], tile_rows(x1_of(ch), ch), AX.X, ALU.add)\
                    .then_inc(l_sum, 1)
                e.wait_ge(l_sum, ch.g + 1)
                e.scalar_tensor_tensor(out=tile_rows(xc[ch.s], ch), in0=spread(ch, 0), scalar=-1.0 / D,
                                       in1=tile_rows(x1_of(ch), ch), op0=ALU.mult, op1=ALU.add)\
                    .then_inc(l_centred, 1)

            def square_sum2(ch):
                e.wait_ge(l_squared, ch.g + 1)
                e.tensor_reduce(st[ch.s][:, 1, 0:ch.tiles], tile_rows(sq, ch), AX.X, ALU.add).then_inc(l_ssq, 1)

            def norm2(ch):
                e.wait_ge(l_std, ch.g + 1)
                e.reciprocal(st[ch.s][:, 3, 0:ch.tiles], st[ch.s][:, 2, 0:ch.tiles]).then_inc(l_rstd, 1)
                e.wait_ge(l_rstd, ch.g + 1)
                if ch.part is SOURCES:
                    wait_past(e, hs_turned, ch.c - 1)
                else:
                    wait_past(e, t1_done, outs(ch) * 2 - 2)
                e.scalar_tensor_tensor(out=hb[ch.s][:, 0:ch.pairs, 0:P], in0=pair_rows(xc[ch.s], ch), scalar=0.0,
                                       in1=spread(ch, 3), op0=ALU.max, op1=ALU.mult).then_inc(l_h, 1)

            def final(ch, u):
                j0, n = quads(ch)[u]
                part = slice(j0 * P, (j0 + n) * P)
                e.wait_ge(o_done, outs(ch) * 2 + (u + 1))
                e.scalar_tensor_tensor(out=x1_of(ch)[:, part], in0=o_bank(ch, u)[:, 0:n * P], scalar=0.0,
                                       in1=x1_of(ch)[:, part], op0=ALU.max, op1=ALU.add).then_inc(fin_done, 1)

            def neighbours(ch, first):
                e.wait_ge(hs_turned, ch.c + 1)
                if first:
                    for q in range(4):
                        e.wait_ge(out_stored[q], 16 * used(BC, 4, q))
                else:
                    e.wait_ge(n_summed, ch.c)
                    e.wait_ge(c_summed, ch.c)
                e.tensor_tensor_scan(reg_m[:, cols(ch)], same[:, cols(ch)], ps_t1_flat[:, 0:W],
                                     0.0 if first else before_col(reg_m, ch), ALU.mult, ALU.add).then_inc(n_summed, 1)
                e.tensor_tensor_scan(reg_a[:, cols(ch)], same[:, cols(ch)], ones_row[:, :],
                                     0.0 if first else before_col(reg_a, ch), ALU.mult, ALU.add).then_inc(c_summed, 1)

            def first_dest(ch):
                return isinstance(ch.c, int) and ch.c == 0

            def mean(ch):
                link(ch, reg_m, mean_carry[:, 0:1], n_linked)
                e.wait_ge(newton_b, ch.c + (EC + 1))
                e.wait_ge(n_linked, ch.c + 1)
                e.scalar_tensor_tensor(out=mean_t[ch.s][:, 0:W], in0=reg_a[:, cols(ch)], scalar=-1.0,
                                       in1=reg_m[:, cols(ch)], op0=ALU.mult, op1=ALU.mult).then_inc(mean_made, 1)

            def second(at):
                now, ago, old, soon = at(0), at(-1), at(-2), at(1)
                if now and soon and soon.part is SOURCES:
                    add_agg(soon)
                if now and linked_late(now):
                    border_sums(mean_ends, mean_carry, 3, n_summed, c_summed)
                    link(old, reg_a, mean_carry[:, 1:2], c_linked)
                    link(ago, reg_a, mean_carry[:, 1:2], c_linked)
                    newton(old, reg_a, 0.0, EC)
                    mean(old)
                if now and counts_in_turn(now):
                    link(now, reg_a, mean_carry[:, 1:2], c_linked)
                if ago and ago.part is DESTS and not first_dest(ago):
                    newton(ago, reg_a, 0.0, EC)
                if ago:
                    first_residual(ago, 1)
                    centre2(ago)
                if old and old.part is SOURCES:
                    neighbours(old, first=at(-3) is None)
                elif old:
                    final(old, 0)
                if ago:
                    square_sum2(ago)
                if now:
                    first_residual(now, 0)
                if ago:
                    norm2(ago)
                if old and old.part is not SOURCES:
                    final(old, 1)
                if ago and ago.part is DESTS and not first_dest(ago):
                    mean(ago)

            run(e, NODES, second, lag=2, lead=1, unroll=4)

            add_agg(Chunk(SOURCES, 4, 0, 0))
            run(e, SOURCES, second, lead=1, unroll=4, after=DESTS)
            run(e, DESTS, second, lag=2, lead=1, unroll=4, before=SOURCES)


_INS = ["x", "src", "dst", "edge_attr_64", "L0_gnn_W_edge", "L0_gnn_W1", "L0_gnn_gamma", "L0_gnn_beta",
        "L0_gnn_W2", "L1_gnn_W", "L1_gnn_b"]


def kernel(**inputs):
    import concourse.bacc as _bacc
    from concourse.bass_utils import run_bass_kernel_spmd as _run

    nc = _bacc.Bacc("TRN2", target_bir_lowering=False, num_devices=1)
    arrays, args = {}, []
    for name in _INS:
        a = np.ascontiguousarray(inputs[name])
        arrays[f"in_{name}_dram"] = a
        args.append(nc.dram_tensor(f"in_{name}_dram", a.shape, mybir.dt.from_np(a.dtype), kind="ExternalInput").ap())
    args.append(nc.dram_tensor("out_0_dram", inputs["x"].shape, F32, kind="ExternalOutput").ap())
    build(nc, *args)
    r = _run(nc, [arrays], core_ids=[0])
    return r.results[0]["out_0_dram"]
```
